# Optimizing a Trainium2 kernel written in Bass

```python
import numpy as np
import jax
import jax.numpy as jnp

def _softmax(x, axis=-1):
    return jax.nn.softmax(x, axis=axis)

def _gelu(x):
    return jax.nn.gelu(x, approximate=True)

def _silu(x):
    return jax.nn.silu(x)

def _sigmoid(x):
    return jax.nn.sigmoid(x)

def _layernorm(x, axis=-1, eps=1e-05):
    m = jnp.mean(x, axis=axis, keepdims=True)
    v = jnp.var(x, axis=axis, keepdims=True)
    return (x - m) / jnp.sqrt(v + eps)

def _scatter_add(tgt, idx, src, axis=0):
    return tgt.at[idx].add(src)

def _segment_sum(src, seg, n):
    return jax.ops.segment_sum(src, seg, n)
kernel_name = 'mk_flamingo_gated_d2_seqx_r8_5d1c3a'

def setup_inputs(seed: int=0):
    np.random.seed(seed)
    _w = jnp.asarray

    def _rec_inputs():
        import jax
        import jax.numpy as jnp
        _rk = jax.random.key(seed)
        x = -0.000125 + 0.9999 * jax.random.normal(jax.random.fold_in(_rk, 1), (64, 64, 256), jnp.float32)
        _lenS = 64 - jax.random.randint(jax.random.fold_in(_rk, 7), (64,), 0, max(1, 64 // 4) + 1, jnp.int32)
        _lenS2 = 64 - jax.random.randint(jax.random.fold_in(_rk, 8), (64,), 0, max(1, 64 // 4) + 1, jnp.int32)
        _ctx_2048P = jax.random.normal(jax.random.fold_in(_rk, 11), (64, 16, 256), jnp.float32)
        _ctx_2048c = jax.random.dirichlet(jax.random.fold_in(_rk, 511), 0.3 * jnp.ones((16,), jnp.float32), (64, 64))
        _ctx_2048t = jnp.einsum('bsk,bkd->bsd', _ctx_2048c, _ctx_2048P)
        _ctx_2048t = _ctx_2048t * jax.lax.rsqrt(jnp.mean(jnp.square(_ctx_2048t)) + 1e-12) * 0.953939
        ctx_2048 = -1.52775e-05 + 0.999936 * (_ctx_2048t + 0.3 * jax.random.normal(jax.random.fold_in(_rk, 611), (64, 64, 256), jnp.float32))
        _g = jax.random.normal(jax.random.fold_in(_rk, 9001), (2, 2), jnp.float32)
        _g = jnp.sign(_g) * jnp.maximum(jnp.abs(_g), 1.0) + (_g == 0) * 1.0
        g_xattn = _g[0]
        g_ffn = _g[1]
        return (x, ctx_2048, g_xattn, g_ffn)
    x, ctx_2048, g_xattn, g_ffn = _rec_inputs()

    def _L0_xattn_setup():
        import jax, jax.numpy as jnp
        import numpy as np
        B, S, D, H = (4, 512, 256, 16)
        HD = D // H
        key = jax.random.key(seed)
        ks = jax.random.split(key, 12)
        sc = 1.0 / np.sqrt(D)
        inp = {'q': jax.random.normal(ks[0], (B, S, D), jnp.float32), 'k': jax.random.normal(ks[1], (B, S, D), jnp.float32), 'v': jax.random.normal(ks[2], (B, S, D), jnp.float32), 'Wq': jax.random.normal(ks[3], (D, D), jnp.float32) * sc, 'bq': jnp.zeros((D,), jnp.float32), 'Wk': jax.random.normal(ks[4], (D, D), jnp.float32) * sc, 'bk': jnp.zeros((D,), jnp.float32), 'Wv': jax.random.normal(ks[5], (D, D), jnp.float32) * sc, 'bv': jnp.zeros((D,), jnp.float32), 'Wo': jax.random.normal(ks[6], (D, D), jnp.float32) * sc, 'bo': jnp.zeros((D,), jnp.float32)}
        return inp
    _L0_xattn_all = _L0_xattn_setup()
    _L0_xattn_in = {k: v for k, v in _L0_xattn_all.items() if k in ('Wq', 'bq', 'Wk', 'bk', 'Wv', 'bv', 'Wo', 'bo')}
    del _L0_xattn_all

    def _L0_ffn_setup():
        import jax, jax.numpy as jnp
        import numpy as np
        E = 16
        D = 256
        H = 176
        HS = 2 * 176
        TOP_K = 6
        ROUTE_SCALE = 1.0
        key = jax.random.key(seed)
        ks = jax.random.split(key, 16)
        s = 0.02
        return {'x': jax.random.normal(ks[0], (4, 128, D), dtype=jnp.float32), 'gate_w': jax.random.normal(ks[1], (E, D), dtype=jnp.float32) * s, 'gate_b': jax.random.normal(ks[2], (E,), dtype=jnp.float32) * s, 'w1': jax.random.normal(ks[3], (E, H, D), dtype=jnp.float32) * s, 'b1': jax.random.normal(ks[4], (E, H), dtype=jnp.float32) * s, 'w2': jax.random.normal(ks[5], (E, D, H), dtype=jnp.float32) * s, 'b2': jax.random.normal(ks[6], (E, D), dtype=jnp.float32) * s, 'w3': jax.random.normal(ks[7], (E, H, D), dtype=jnp.float32) * s, 'b3': jax.random.normal(ks[8], (E, H), dtype=jnp.float32) * s, 'ws1': jax.random.normal(ks[9], (HS, D), dtype=jnp.float32) * s, 'bs1': jax.random.normal(ks[10], (HS,), dtype=jnp.float32) * s, 'ws2': jax.random.normal(ks[11], (D, HS), dtype=jnp.float32) * s, 'bs2': jax.random.normal(ks[12], (D,), dtype=jnp.float32) * s, 'ws3': jax.random.normal(ks[13], (HS, D), dtype=jnp.float32) * s, 'bs3': jax.random.normal(ks[14], (HS,), dtype=jnp.float32) * s}
    _L0_ffn_all = _L0_ffn_setup()
    _L0_ffn_in = {k: v for k, v in _L0_ffn_all.items() if k in ('gate_w', 'gate_b', 'w1', 'b1', 'w2', 'b2', 'w3', 'b3', 'ws1', 'bs1', 'ws2', 'bs2', 'ws3', 'bs3')}
    del _L0_ffn_all

    def _L1_xattn_setup():
        import jax, jax.numpy as jnp
        import numpy as np
        B_DIM, T_DIM, C_DIM = (16, 128, 256)

        def _wkv(w, u, k, v):
            Bn, Tn, Cn = k.shape
            NEG_INF = jnp.float32(-1e+38)

            def step(carry, kv_t):
                p, q, o = carry
                kt, vt = kv_t
                no = jnp.maximum(o, u + kt)
                A = jnp.exp(o - no)
                E = jnp.exp(u + kt - no)
                y = (A * p + E * vt) / (A * q + E)
                no2 = jnp.maximum(w + o, kt)
                A2 = jnp.exp(w + o - no2)
                E2 = jnp.exp(kt - no2)
                return ((A2 * p + E2 * vt, A2 * q + E2, no2), y)
            init = (jnp.zeros((Bn, Cn), k.dtype), jnp.zeros((Bn, Cn), k.dtype), jnp.full((Bn, Cn), NEG_INF, k.dtype))
            kT = jnp.moveaxis(k, 1, 0)
            vT = jnp.moveaxis(v, 1, 0)
            _, yT = jax.lax.scan(step, init, (kT, vT))
            return jnp.moveaxis(yT, 0, 1)
        key = jax.random.key(seed)
        k1, k2, k3, k4 = jax.random.split(key, 4)
        w = -jnp.exp(jax.random.normal(k1, (C_DIM,), jnp.float32))
        u = jax.random.normal(k2, (C_DIM,), jnp.float32)
        k = jax.random.normal(k3, (B_DIM, T_DIM, C_DIM), jnp.float32)
        v = jax.random.normal(k4, (B_DIM, T_DIM, C_DIM), jnp.float32)
        return {'B': B_DIM, 'T': T_DIM, 'C': C_DIM, 'w': w, 'u': u, 'k': k, 'v': v}
    _L1_xattn_all = _L1_xattn_setup()
    _L1_xattn_in = {k: v for k, v in _L1_xattn_all.items() if k in ('w', 'u')}
    del _L1_xattn_all

    def _L1_ffn_setup():
        import jax, jax.numpy as jnp
        import numpy as np
        from jax import lax
        B, S, H = (2, 64, 256)
        I = 96
        E = 64
        K = 8
        key = jax.random.key(seed)
        k1, k2, k3, k4 = jax.random.split(key, 4)
        hidden_states = jax.random.normal(k1, (B, S, H), jnp.float32)
        gate_weight = jax.random.normal(k2, (E, H), jnp.float32) * 0.02
        gate_up_weights = jax.random.normal(k3, (E, H, 2 * I), jnp.float32) * 0.02
        down_weights = jax.random.normal(k4, (E, I, H), jnp.float32) * 0.02
        return {'hidden_states': hidden_states, 'gate_weight': gate_weight, 'gate_up_weights': gate_up_weights, 'down_weights': down_weights}
    _L1_ffn_all = _L1_ffn_setup()
    _L1_ffn_in = {k: v for k, v in _L1_ffn_all.items() if k in ('gate_weight', 'gate_up_weights', 'down_weights')}
    del _L1_ffn_all
    return {'x': x, 'ctx_2048': ctx_2048, 'g_xattn': g_xattn, 'g_ffn': g_ffn, 'L0_xattn_Wq': _L0_xattn_in['Wq'], 'L0_xattn_bq': _L0_xattn_in['bq'], 'L0_xattn_Wk': _L0_xattn_in['Wk'], 'L0_xattn_bk': _L0_xattn_in['bk'], 'L0_xattn_Wv': _L0_xattn_in['Wv'], 'L0_xattn_bv': _L0_xattn_in['bv'], 'L0_xattn_Wo': _L0_xattn_in['Wo'], 'L0_xattn_bo': _L0_xattn_in['bo'], 'L0_ffn_gate_w': _L0_ffn_in['gate_w'], 'L0_ffn_gate_b': _L0_ffn_in['gate_b'], 'L0_ffn_w1': _L0_ffn_in['w1'], 'L0_ffn_b1': _L0_ffn_in['b1'], 'L0_ffn_w2': _L0_ffn_in['w2'], 'L0_ffn_b2': _L0_ffn_in['b2'], 'L0_ffn_w3': _L0_ffn_in['w3'], 'L0_ffn_b3': _L0_ffn_in['b3'], 'L0_ffn_ws1': _L0_ffn_in['ws1'], 'L0_ffn_bs1': _L0_ffn_in['bs1'], 'L0_ffn_ws2': _L0_ffn_in['ws2'], 'L0_ffn_bs2': _L0_ffn_in['bs2'], 'L0_ffn_ws3': _L0_ffn_in['ws3'], 'L0_ffn_bs3': _L0_ffn_in['bs3'], 'L1_xattn_w': _L1_xattn_in['w'], 'L1_xattn_u': _L1_xattn_in['u'], 'L1_ffn_gate_weight': _L1_ffn_in['gate_weight'], 'L1_ffn_gate_up_weights': _L1_ffn_in['gate_up_weights'], 'L1_ffn_down_weights': _L1_ffn_in['down_weights']}

def reference(x, ctx_2048, g_xattn, g_ffn, L0_xattn_Wq, L0_xattn_bq, L0_xattn_Wk, L0_xattn_bk, L0_xattn_Wv, L0_xattn_bv, L0_xattn_Wo, L0_xattn_bo, L0_ffn_gate_w, L0_ffn_gate_b, L0_ffn_w1, L0_ffn_b1, L0_ffn_w2, L0_ffn_b2, L0_ffn_w3, L0_ffn_b3, L0_ffn_ws1, L0_ffn_bs1, L0_ffn_ws2, L0_ffn_bs2, L0_ffn_ws3, L0_ffn_bs3, L1_xattn_w, L1_xattn_u, L1_ffn_gate_weight, L1_ffn_gate_up_weights, L1_ffn_down_weights):
    import jax
    import jax.numpy as jnp

    def _L0_xattn_ref(q, k, v, Wq, bq, Wk, bk, Wv, bv, Wo, bo):
        import jax, jax.numpy as jnp
        import numpy as np
        B, S, D, H = (4, 512, 256, 16)
        HD = D // H
        bs, sl, nf = q.shape
        Q = (q @ Wq.T + bq).reshape(bs, sl, H, HD)
        K = (k @ Wk.T + bk).reshape(bs, sl, H, HD)
        V = (v @ Wv.T + bv).reshape(bs, sl, H, HD)
        score = jnp.einsum('bshd,bsgd->bshg', Q, K)
        weight = jax.nn.softmax(score, axis=-1)
        attn = jnp.einsum('bshg,bsgd->bshd', weight, V).reshape(bs, sl, nf)
        return attn @ Wo.T + bo

    def _L0_ffn_ref(x, gate_w, gate_b, w1, b1, w2, b2, w3, b3, ws1, bs1, ws2, bs2, ws3, bs3):
        import jax, jax.numpy as jnp
        import numpy as np
        E = 16
        D = 256
        H = 176
        HS = 2 * 176
        TOP_K = 6
        ROUTE_SCALE = 1.0
        shape = x.shape
        xf = x.reshape(-1, shape[-1])
        scores = xf @ gate_w.T
        probs = jax.nn.softmax(scores.astype(jnp.float32), axis=-1)
        biased = probs + gate_b
        _, idx = jax.lax.top_k(biased, TOP_K)
        weights = jnp.take_along_axis(probs, idx, axis=1) * ROUTE_SCALE
        weights = weights.astype(x.dtype)
        onehot = jax.nn.one_hot(idx, E, dtype=weights.dtype)
        cw = jnp.einsum('tk,tke->te', weights, onehot)

        def expert_step(y, params):
            W1, B1, W2, B2, W3, B3, c = params
            h = jax.nn.silu(xf @ W1.T + B1) * (xf @ W3.T + B3)
            out = h @ W2.T + B2
            return (y + c[:, None] * out, None)
        y0 = jnp.zeros_like(xf)
        y, _ = jax.lax.scan(expert_step, y0, (w1, b1, w2, b2, w3, b3, cw.T))
        z = jax.nn.silu(xf @ ws1.T + bs1) * (xf @ ws3.T + bs3) @ ws2.T + bs2
        return (y + z).reshape(shape)

    def _L1_xattn_ref(B, T, C, w, u, k, v):
        import jax, jax.numpy as jnp
        import numpy as np
        B_DIM, T_DIM, C_DIM = (16, 128, 256)

        def _wkv(w, u, k, v):
            Bn, Tn, Cn = k.shape
            NEG_INF = jnp.float32(-1e+38)

            def step(carry, kv_t):
                p, q, o = carry
                kt, vt = kv_t
                no = jnp.maximum(o, u + kt)
                A = jnp.exp(o - no)
                E = jnp.exp(u + kt - no)
                y = (A * p + E * vt) / (A * q + E)
                no2 = jnp.maximum(w + o, kt)
                A2 = jnp.exp(w + o - no2)
                E2 = jnp.exp(kt - no2)
                return ((A2 * p + E2 * vt, A2 * q + E2, no2), y)
            init = (jnp.zeros((Bn, Cn), k.dtype), jnp.zeros((Bn, Cn), k.dtype), jnp.full((Bn, Cn), NEG_INF, k.dtype))
            kT = jnp.moveaxis(k, 1, 0)
            vT = jnp.moveaxis(v, 1, 0)
            _, yT = jax.lax.scan(step, init, (kT, vT))
            return jnp.moveaxis(yT, 0, 1)
        return _wkv(w, u, k, v)

    def _L1_ffn_ref(hidden_states, gate_weight, gate_up_weights, down_weights):
        import jax, jax.numpy as jnp
        import numpy as np
        from jax import lax
        B, S, H = (2, 64, 256)
        I = 96
        E = 64
        K = 8
        orig_shape = hidden_states.shape
        x = hidden_states.reshape(-1, H)
        T = x.shape[0]
        logits = x @ gate_weight.T
        probs = jax.nn.softmax(logits.astype(jnp.float32), axis=-1)
        routing_weights, selected_experts = lax.top_k(probs, K)
        wsum = routing_weights.sum(axis=-1, keepdims=True)
        wsum = jnp.where(wsum == 0, 1.0, wsum)
        routing_weights = (routing_weights / wsum).astype(x.dtype)
        combine = jnp.zeros((T, E), x.dtype).at[jnp.arange(T)[:, None], selected_experts].add(routing_weights)

        def body(acc, ws):
            wgu, wd, we = ws
            gu = x @ wgu
            gate, up = jnp.split(gu, 2, axis=-1)
            act = jax.nn.silu(gate) * up
            out = act @ wd
            return (acc + we[:, None] * out, None)
        init = jnp.zeros_like(x)
        final, _ = lax.scan(body, init, (gate_up_weights, down_weights, combine.T))
        return final.reshape(orig_shape)
    x = x + jnp.tanh(g_xattn[0]) * _L0_xattn_ref(_layernorm(x, axis=-1), ctx_2048, ctx_2048, L0_xattn_Wq, L0_xattn_bq, L0_xattn_Wk, L0_xattn_bk, L0_xattn_Wv, L0_xattn_bv, L0_xattn_Wo, L0_xattn_bo)
    x = x + jnp.tanh(g_ffn[0]) * _L0_ffn_ref(_layernorm(x, axis=-1), L0_ffn_gate_w, L0_ffn_gate_b, L0_ffn_w1, L0_ffn_b1, L0_ffn_w2, L0_ffn_b2, L0_ffn_w3, L0_ffn_b3, L0_ffn_ws1, L0_ffn_bs1, L0_ffn_ws2, L0_ffn_bs2, L0_ffn_ws3, L0_ffn_bs3)
    x = x + jnp.tanh(g_xattn[1]) * _L1_xattn_ref(64, 64, 256, L1_xattn_w, L1_xattn_u, _layernorm(x, axis=-1), ctx_2048)
    x = x + jnp.tanh(g_ffn[1]) * _L1_ffn_ref(_layernorm(x, axis=-1), L1_ffn_gate_weight, L1_ffn_gate_up_weights, L1_ffn_down_weights)
    return x

_drawn_inputs = setup_inputs


def setup_inputs(seed=0):
    import zlib

    import numpy as np

    out = dict(_drawn_inputs(seed))
    spreads = {'g_ffn': (-1.0, 0.6),
     'L0_xattn_bq': (0.0, 0.1),
     'L0_xattn_bk': (0.0, 0.1),
     'L0_xattn_bv': (0.0, 0.1),
     'L0_xattn_bo': (0.0, 0.1)}
    factors = {'L0_ffn_gate_w': 8.0,
     'L0_ffn_gate_b': 8.0,
     'L0_ffn_w1': 8.0,
     'L0_ffn_b1': 8.0,
     'L0_ffn_w2': 8.0,
     'L0_ffn_b2': 8.0,
     'L0_ffn_w3': 8.0,
     'L0_ffn_b3': 8.0,
     'L0_ffn_ws1': 5.011,
     'L0_ffn_bs1': 8.0,
     'L0_ffn_ws2': 4.942,
     'L0_ffn_bs2': 5.384,
     'L0_ffn_ws3': 4.97,
     'L0_ffn_bs3': 8.0,
     'L1_ffn_gate_weight': 8.0,
     'L1_ffn_gate_up_weights': 8.0,
     'L1_ffn_down_weights': 8.0}
    for name, (base, spread) in spreads.items():
        noise = np.random.default_rng([zlib.crc32(name.encode()), seed]).standard_normal(out[name].shape)
        drawn = base * np.exp(spread * noise) if base else spread * noise
        out[name] = jnp.asarray(drawn.astype(out[name].dtype))
    for name, factor in factors.items():
        out[name] = (out[name] * factor).astype(out[name].dtype)
    return out
```

```python
from contextlib import ExitStack

import concourse.bass as bass
from concourse import mybir

F32 = mybir.dt.float32
BF16 = mybir.dt.bfloat16
I32 = mybir.dt.int32
U32 = mybir.dt.uint32
ALU = mybir.AluOpType
ACT = mybir.ActivationFunctionType
AX = mybir.AxisListType.X

P = 128
D = 256
KC = D // P
NTOK = 64 * 64
NT = NTOK // P
GT = 4
GS = GT * P
NG = NTOK // GS
HEADS = 16
HD = D // HEADS
TB = P // HD
NN = GS // TB
SEQ = 64
GB = GS // SEQ
EPS = 1e-5
LOW = -1e38
HS = 352
HSP = [128, 128, 96]
CHOICES = 8


class Layer:

    def __init__(self, name, experts, top, hidden, chunks, bias):
        self.name, self.E, self.K, self.H, self.NC, self.bias = name, experts, top, hidden, chunks, bias
        self.MH = hidden // chunks
        self.tiles = -(-(NTOK * top // P + experts - 1) // 4) * 4
        self.up0 = 2 * KC * hidden
        self.b0 = self.up0 + chunks * D
        self.W = self.b0 + (2 * chunks if bias else 0)


L0 = Layer("a", 16, 6, 176, 2, True)
L1 = Layer("b", 64, 8, 96, 1, False)
ROWS = max(L0.tiles, L1.tiles) * P
TD = 8


def flamingo(nc, x, ctxT, gates, wqkvT, bqkv, woT, bo, gate0T, gate0b, exp0, sh1T, sh3T, sh2T, shb, bs2,
             wkv_w, wkv_u, gate1T, exp1, out):
    qkv_d = nc.dram_tensor("qkv_d", (NG, 3, D, GS), F32).ap()
    p_d = nc.dram_tensor("p_d", (NG, P, HEADS * NN), F32).ap()
    o_d = nc.dram_tensor("o_d", (NG, D, GS), F32).ap()
    xs_d = nc.dram_tensor("xs_d", (ROWS, D), F32).ap()
    ys_d = nc.dram_tensor("ys_d", (ROWS, D), F32).ap()

    ctx = ExitStack()
    with ctx:
        names = {}

        def sb_in(stack):
            def sb(name, shape, dt=F32):
                names[name] = names.get(name, 0) + 1
                return stack.enter_context(nc.sbuf_tensor(f"{name}_{names[name]}", shape, dt))
            return sb

        def sem(name):
            return ctx.enter_context(nc.semaphore(name))

        sb = sb_in(ctx)
        x_res = sb("x_res", [P, NT, D])
        z = sb("z", [P, NT, D])
        n_x = sb("n_x", [P, 2, GT, D])
        zero_rows = sb("zero_rows", [P, 8 * D])
        ident = sb("ident", [P, P])
        ones = sb("ones", [P, P])
        ones_h = sb("ones_h", [P, P], BF16)
        before = sb("before", [P, P], BF16)
        tgate = sb("tgate", [P, 4])
        stats = sb("stats", [P, NT, 6])
        mean = sb("mean", [P, NT])
        rstd = sb("rstd", [P, NT])
        mean_v = sb("mean_v", [P, NT])
        tmp_t = sb("tmp_t", [P, NT])
        slot_i = sb("slot_i", [P, NT, CHOICES], I32)
        weight = sb("weight", [P, NT, CHOICES])
        tile_e = sb("tile_e", [1, max(L0.tiles, L1.tiles)], I32)
        idx_s = sb("idx_s", [P, 2, CHOICES], I32)
        ps = ctx.enter_context(nc.psum_tensor("ps", [P, 8, 512], F32))

        with ExitStack() as st:
            s_ = sb_in(st)
            a_w = s_("a_w", [P, 3 * KC, D])
            a_b = s_("a_b", [P, 3 * KC])
            a_ctx = s_("a_ctx", [P, 2, KC, GS])
            a_xT = s_("a_xT", [P, 2, KC, GS])
            a_out = s_("a_out", [P, 2, 3 * KC, GS])
        with ExitStack() as st:
            s_ = sb_in(st)
            diag = [s_(f"diag{s}", [P, TB, HEADS, NN]) for s in range(2)]
            kv = s_("kv", [P, 2, HEADS, NN])
            s_sub = s_("s_sub", [P, 2, NN, HEADS])
            p_un = s_("p_un", [P, 2, HEADS, NN])
            o_nm = s_("o_nm", [P, 2, HEADS, NN])
            smax = s_("smax", [P, NN])
            rsum = s_("rsum", [P, NG, NN])
        with ExitStack() as st:
            s_ = sb_in(st)
            d_w = s_("d_w", [P, KC, D])
            d_bo = s_("d_bo", [P, D])
            d_o = s_("d_o", [P, 2, KC, GS])
        with ExitStack() as st:
            s_ = sb_in(st)
            e_xT = s_("e_xT", [P, 2, KC, GS])
            e_g0 = s_("e_g0", [P, KC, L0.E])
            e_g1 = s_("e_g1", [P, KC, L1.E])
            e_w1 = s_("e_w1", [P, KC, HS])
            e_w3 = s_("e_w3", [P, KC, HS])
            e_w2 = s_("e_w2", [P, 3, D])
            e_b = s_("e_b", [P, 6])
            e_bs2 = s_("e_bs2", [P, D])
            e_sg = s_("e_sg", [P, 2, GS])
            e_h = s_("e_h", [P, 2, 3, GS])
        with ExitStack() as st:
            s_ = sb_in(st)
            F = L1.E * NT
            r_p = s_("r_p", [P, F])
            r_b = s_("r_b", [P, F])
            r_w = s_("r_w", [P, F])
            r_c = s_("r_c", [P, F])
            r_i = s_("r_i", [P, F])
            r_s = s_("r_s", [P, F])
            r_keep = s_("r_keep", [P, F])
            r_m = s_("r_m", [P, F], BF16)
            r_val = s_("r_val", [P, NT, CHOICES])
            r_idx = s_("r_idx", [P, NT, CHOICES], U32)
            r_idf = s_("r_idf", [P, NT, CHOICES])
            r_sl = s_("r_sl", [P, NT, CHOICES])
            r_gb = s_("r_gb", [P, L0.E])
            r_ie = s_("r_ie", [P, L1.E])
            r_ij = s_("r_ij", [P, NT])
            r_it = s_("r_it", [P, max(L0.tiles, L1.tiles)])
            r_te = s_("r_te", [P, L1.E])
            r_cum = s_("r_cum", [P, L1.E])
            r_st = s_("r_st", [P, L1.E])
            r_dg = s_("r_dg", [P, L1.E])
            r_end = s_("r_end", [P, 1])
            r_cmp = s_("r_cmp", [P, max(L0.tiles, L1.tiles)], BF16)
            r_t1 = s_("r_t1", [P, NT])
        with ExitStack() as st:
            s_ = sb_in(st)
            g_rows = [s_(f"g_rows{s}", [P, D]) for s in range(2)]
        with ExitStack() as st:
            s_ = sb_in(st)
            h_w = [s_(f"h_w{s}", [P, L0.W]) for s in range(TD)]
            h_x = [s_(f"h_x{s}", [P, D]) for s in range(TD)]
            h_y = [s_(f"h_y{s}", [P, D]) for s in range(TD)]
            h_xT = s_("h_xT", [P, 2, KC, P])
            h_sg = s_("h_sg", [P, 2, 2, P])
            h_h = s_("h_h", [P, 2, 2, P])
        with ExitStack() as st:
            s_ = sb_in(st)
            c_g = [s_(f"c_g{s}", [P, CHOICES, D]) for s in range(2)]
            c_acc = s_("c_acc", [P, 2, D])
        with ExitStack() as st:
            s_ = sb_in(st)
            w_wu = s_("w_wu", [P, 2 * KC])
            w_dec = s_("w_dec", [P, KC, GB, SEQ + 1])
            w_k = s_("w_k", [P, 2, KC, GB, SEQ + 1])
            w_v = s_("w_v", [P, 2, KC, GS])
            w_o = s_("w_o", [P, GB, SEQ + 1])
            w_t = s_("w_t", [P, 2, 4, GB, SEQ])
            w_a2 = s_("w_a2", [P, 2, GB, SEQ + 1])
            w_e2 = s_("w_e2", [P, 2, GB, SEQ + 1])
            w_ex = s_("w_ex", [P, 2, 2, GB, SEQ])
            w_ev = s_("w_ev", [P, GB, SEQ + 1])
            w_p = s_("w_p", [P, GB, SEQ + 1])
            w_q = s_("w_q", [P, GB, SEQ + 1])
            w_n = s_("w_n", [P, GB, SEQ])
            w_m = s_("w_m", [P, GB, SEQ])
            w_d = s_("w_d", [P, GB, SEQ])
            w_y = s_("w_y", [P, 2, KC, GB, SEQ])

        stage_done = sem("stage_done")
        spacer = sem("spacer")
        in_sem = sem("in_sem")
        in_count = [0]
        zeroed = sem("zeroed")
        const_ready = sem("const_ready")
        tanh_done = sem("tanh_done")
        var_ready = sem("var_ready")
        std_ready = sem("std_ready")
        xn_ready = sem("xn_ready")
        tr_done = sem("tr_done")
        xT_ready = sem("xT_ready")
        ctx_in = [sem(f"ctx_in{s}") for s in range(2)]
        proj_done = sem("proj_done")
        proj_out = sem("proj_out")
        qkv_st = [sem(f"qkv_st{s}") for s in range(2)]
        diag_in = [sem(f"diag_in{s}") for s in range(2)]
        diag_zero = sem("diag_zero")
        sc_done = sem("sc_done")
        sub_done = sem("sub_done")
        exp_done = sem("exp_done")
        sum_done = sem("sum_done")
        p_st = [sem(f"p_st{s}") for s in range(2)]
        pv_done = sem("pv_done")
        o_done = sem("o_done")
        o_st = [sem(f"o_st{s}") for s in range(2)]
        o_in = [sem(f"o_in{s}") for s in range(2)]
        op_done = sem("op_done")
        op_used = sem("op_used")
        sh_done = sem("sh_done")
        sh_silu = sem("sh_silu")
        sh_h = sem("sh_h")
        sh_z = sem("sh_z")
        sh_zu = sem("sh_zu")
        rt_done = sem("rt_done")
        sc_ready = sem("sc_ready")
        pr_ready = sem("pr_ready")
        hot_ready = sem("hot_ready")
        rank_ready = sem("rank_ready")
        cmp_ready = sem("cmp_ready")
        map_ready = sem("map_ready")
        row_ready = sem("row_ready")
        lay = {}
        for L in (L0, L1):
            n = L.name
            lay[n] = dict(
                row_st=[sem(f"row_st{n}{s}") for s in range(2)],
                x_in=[sem(f"x_in{n}{s}") for s in range(TD)],
                w_in=[sem(f"w_in{n}{s}") for s in range(TD)],
                y_st=[sem(f"y_st{n}{s}") for s in range(TD)],
                t_done=sem(f"t_done{n}"),
                t_ready=sem(f"t_ready{n}"),
                u_done=sem(f"u_done{n}"),
                s_done=sem(f"s_done{n}"),
                h_done=sem(f"h_done{n}"),
                d_done=sem(f"d_done{n}"),
                y_done=sem(f"y_done{n}"),
                g_in=[sem(f"g_in{n}{s}") for s in range(2)],
                g_idx=sem(f"g_idx{n}"),
                g_used=sem(f"g_used{n}"),
                g_st=sem(f"g_st{n}"),
            )
        wk_y = sem("wk_y")
        wk_t = sem("wk_t")
        wk_e = sem("wk_e")
        wk_yt = sem("wk_yt")
        wk_yu = sem("wk_yu")
        wk_k = sem("wk_k")
        wk_v = [sem(f"wk_v{s}") for s in range(2)]
        wk_pad = sem("wk_pad")

        block = ctx.enter_context(nc.Block())

        stages = ["A", "B", "C", "D", "E0", "F0", "G0", "H0", "I0", "W", "E1", "F1", "G1", "H1", "I1"]

        def end_stage(eng, name):
            n = stages.index(name) + 1
            eng.drain().then_inc(stage_done, 1)
            eng.wait_ge(stage_done, 5 * n)

        @block.sync
        def _(sp):
            def load(dst, src):
                sp.dma_start(dst, src).then_inc(in_sem, 16)
                in_count[0] += 1

            def loaded():
                sp.wait_ge(in_sem, 16 * in_count[0])

            x_v = x.rearrange("(t p) d -> p t d", p=P)
            for q in range(4):
                load(x_res[:, q * NT // 4:(q + 1) * NT // 4, :], x_v[:, q * NT // 4:(q + 1) * NT // 4, :])
            load(a_w[:], wqkvT.rearrange("(a p) n -> p a n", p=P))
            load(a_b[:], bqkv)
            load(tgate[:], gates.partition_broadcast(P))
            ctx_v = ctxT.rearrange("(c p) (g n) -> g p c n", p=P, n=GS)

            def a_group(b, s):
                sp.wait_ge(proj_done, 12 * b + 6 * s + 6)
                sp.dma_start(a_ctx[:, s], ctx_v[bass.ds(2 * b + s, 1)].rearrange("a p c n -> (a p) c n"))\
                  .then_inc(ctx_in[s], 16)

            with sp.Fori(0, NG // 2) as b:
                for s in range(2):
                    a_group(b, s)
            sp.wait_ge(const_ready, 4)
            z_v = xs_d.rearrange("(n p r) d -> n p (r d)", p=P, r=8)
            with sp.Fori(0, ROWS // (8 * P)) as i:
                sp.dma_start(z_v[bass.ds(i, 1)].rearrange("a p n -> (a p) n"), zero_rows[:]).then_inc(zeroed, 16)
            end_stage(sp, "A")

            q_v = qkv_d.rearrange("u j (h d) (t n) -> u j t d h n", h=HEADS, t=TB)
            v_v = qkv_d.rearrange("u j (g d) (t n) -> u j t g d n", g=HEADS, t=TB)
            p_v = p_d.rearrange("u (t h) (g n) -> u t g h n", h=HEADS, g=HEADS)
            sp.wait_ge(diag_zero, 1)

            def diag_load(u, s, src_d, src_r):
                for t in range(TB):
                    rows = slice(HD * t, HD * t + HD)
                    sp.dma_start(diag[s][rows, t], src_d(u, t)).then_inc(diag_in[s], 16)
                    sp.dma_start(kv[rows, s], src_r(u, t)).then_inc(diag_in[s], 16)

            with sp.Fori(0, NG // 2) as b:
                for s in range(2):
                    sp.wait_ge(sc_done, 2 * b + s + 1)
                    diag_load(2 * b + s, s,
                              lambda u, t: q_v[bass.ds(u, 1), 2, t].rearrange("a d h n -> (a d) h n"),
                              lambda u, t: q_v[bass.ds(u, 1), 0, t].rearrange("a d h n -> (a d) h n"))
            end_stage(sp, "B")
            with sp.Fori(0, NG // 2) as b:
                for s in range(2):
                    sp.wait_ge(pv_done, 2 * b + s + 1)
                    diag_load(2 * b + s, s,
                              lambda u, t: p_v[bass.ds(u, 1), t].rearrange("a g h n -> (a g) h n"),
                              lambda u, t: v_v[bass.ds(u, 1), 1, t].rearrange("a g d n -> (a g) d n"))
            end_stage(sp, "C")

            load(d_w[:], woT.rearrange("(c p) n -> p c n", p=P))
            load(d_bo[:], bo.partition_broadcast(P))
            od_v = o_d.rearrange("u (c p) n -> u p c n", p=P)
            with sp.Fori(0, NG // 2) as b:
                for s in range(2):
                    sp.wait_ge(op_done, 2 * b + s + 1)
                    sp.dma_start(d_o[:, s], od_v[bass.ds(2 * b + s, 1)].rearrange("a p c n -> (a p) c n"))\
                      .then_inc(o_in[s], 16)
            end_stage(sp, "D")

            def experts(L):
                q = lay[L.name]
                wsrc = exp0 if L is L0 else exp1
                x_t = xs_d.rearrange("(n p) d -> n p d", p=P)
                y_t = ys_d.rearrange("(n p) d -> n p d", p=P)

                def put(i, s):
                    sp.wait_ge(q["y_done"], i + 3)
                    sp.dma_start(y_t[bass.ds(i, 1)].rearrange("a p d -> (a p) d"), h_y[s][:])\
                      .then_inc(q["y_st"][s], 16)

                def body(b, first):
                    for s in range(TD):
                        i = TD * b + s
                        sp.wait_ge(q["t_done"], i + 1)
                        sp.dma_start(h_x[s][:], x_t[bass.ds(i, 1)].rearrange("a p d -> (a p) d"))\
                          .then_inc(q["x_in"][s], 16)
                        e = sp.value_load(tile_e[0:1, bass.ds(i, 1)], min_val=0, max_val=L.E - 1)
                        sp.wait_ge(q["d_done"], i + 1)
                        sp.dma_start(h_w[s][:, 0:L.W], wsrc[bass.ds(e, 1)].rearrange("a p n -> (a p) n"))\
                          .then_inc(q["w_in"][s], 16)
                        if not first or s >= TD - 1:
                            put(i - (TD - 1), (s + 1) % TD)

                body(0, True)
                with sp.Fori(1, L.tiles // TD) as b:
                    body(b, False)
                for i in range(L.tiles - (TD - 1), L.tiles):
                    put(i, i % TD)
                for s in range(TD):
                    sp.wait_ge(q["y_st"][s], 16 * (L.tiles // TD + 1))

            load(e_g0[:], gate0T.rearrange("(c p) n -> p c n", p=P))
            load(e_w1[:], sh1T.rearrange("(c p) n -> p c n", p=P))
            load(e_w3[:], sh3T.rearrange("(c p) n -> p c n", p=P))
            load(e_w2[:], sh2T.rearrange("(c p) n -> p c n", p=P))
            load(e_b[:], shb)
            load(e_bs2[:], bs2.partition_broadcast(P))
            end_stage(sp, "E0")
            load(r_gb[:], gate0b.partition_broadcast(P))
            sp.wait_ge(zeroed, 16 * (ROWS // (8 * P)))
            end_stage(sp, "F0")
            end_stage(sp, "G0")
            experts(L0)
            end_stage(sp, "H0")
            end_stage(sp, "I0")
            load(w_wu[:, 0:KC], wkv_w)
            load(w_wu[:, KC:2 * KC], wkv_u)
            with sp.Fori(0, NG // 2) as b:
                for s in range(2):
                    sp.wait_ge(wk_y, 2 * b + s + 1)
                    sp.dma_start(w_v[:, s], ctx_v[bass.ds(2 * b + s, 1)].rearrange("a p c n -> (a p) c n"))\
                      .then_inc(wk_v[s], 16)
            end_stage(sp, "W")
            load(e_g1[:], gate1T.rearrange("(c p) n -> p c n", p=P))
            end_stage(sp, "E1")
            end_stage(sp, "F1")
            end_stage(sp, "G1")
            experts(L1)
            end_stage(sp, "H1")
            o_v = out.rearrange("(t p) d -> t p d", p=P)
            with sp.Fori(0, NT) as t:
                sp.wait_ge(lay["b"]["g_used"], t + 3)
                sp.dma_start(o_v[bass.ds(t, 1)].rearrange("a p d -> (a p) d"),
                             x_res[:, bass.ds(t, 1), :].rearrange("p a d -> p (a d)")).then_inc(lay["b"]["g_st"], 16)
            sp.wait_ge(lay["b"]["g_st"], 16 * NT)
            end_stage(sp, "I1")

        n_load = {"A": 7, "D": 9, "E0": 15, "F0": 16, "W": 18, "E1": 19}

        @block.gpsimd
        def _(pool):
            pool.memset(zero_rows[:], 0.0)
            pool.memset(ones[:], 1.0)
            pool.memset(ones_h[:], 1.0)
            pool.drain()
            pool.affine_select(out=ident[:], in_=ones[:], pattern=[[-1, P]], compare_op=ALU.is_equal, fill=0.0,
                               base=0, channel_multiplier=1)
            pool.affine_select(out=before[:], in_=ones_h[:], pattern=[[1, P]], compare_op=ALU.is_gt, fill=0.0,
                               base=0, channel_multiplier=-1)
            pool.drain().then_inc(const_ready, 4)
            end_stage(pool, "A")
            for s in range(2):
                pool.memset(diag[s][:], 0.0)
            pool.drain().then_inc(diag_zero, 1)
            end_stage(pool, "B")
            end_stage(pool, "C")
            end_stage(pool, "D")

            def iotas(L):
                pool.iota(r_ie[:, 0:L.E], pattern=[[1, L.E]], base=0, channel_multiplier=0,
                          allow_small_or_imprecise_dtypes=True)
                pool.iota(r_ij[:], pattern=[[P, NT]], base=0, channel_multiplier=0,
                          allow_small_or_imprecise_dtypes=True)
                pool.iota(r_it[:, 0:L.tiles], pattern=[[1, L.tiles]], base=0, channel_multiplier=0,
                          allow_small_or_imprecise_dtypes=True)
                pool.memset(r_keep[:, 0:L.E * NT], 1.0)
                pool.drain()
                pool.memset(r_keep[:, 0:L.E * NT].rearrange("p (e t) -> p e t", t=NT)[:, :, 0:1], 0.0)
                pool.drain().then_inc(const_ready, 1)

            def scatter(L):
                q = lay[L.name]
                with pool.Fori(0, NT // 2) as b:
                    for s in range(2):
                        pool.wait_ge(row_ready, (0 if L is L0 else NT) + 2 * b + s + 1)
                        pool.sem_inc(spacer, 1)
                        for k in range(L.K):
                            pool.indirect_dma_start(
                                xs_d, bass.IndirectOffsetOnAxis(ap=idx_s[:, s, k:k + 1], axis=0),
                                g_rows[s][:], None).then_inc(q["row_st"][s], 16)
                for s in range(2):
                    pool.wait_ge(q["row_st"][s], 16 * L.K * NT // 2)

            def gather(L):
                q = lay[L.name]
                with pool.Fori(0, NT // 2) as b:
                    for s in range(2):
                        pool.wait_ge(q["g_used"], 2 * b + s + 1)
                        pool.sem_inc(spacer, 1)
                        pool.tensor_copy(idx_s[:, s, 0:L.K], slot_i[:, bass.ds(2 * b + s, 1), 0:L.K]
                                         .rearrange("p a k -> p (a k)")).then_inc(q["g_idx"], 1)
                        pool.wait_ge(q["g_idx"], 2 * b + s + 1)
                        pool.sem_inc(spacer, 1)
                        for k in range(L.K):
                            pool.indirect_dma_start(
                                c_g[s][:, k, :], None, ys_d[0:L.tiles * P, :],
                                bass.IndirectOffsetOnAxis(ap=idx_s[:, s, k:k + 1], axis=0))\
                                .then_inc(q["g_in"][s], 16)
                for s in range(2):
                    pool.wait_ge(q["g_in"][s], 16 * L.K * NT // 2)

            end_stage(pool, "E0")
            iotas(L0)
            end_stage(pool, "F0")
            scatter(L0)
            end_stage(pool, "G0")
            end_stage(pool, "H0")
            gather(L0)
            end_stage(pool, "I0")
            for c in range(KC):
                pool.memset(w_dec[:, c, :, 0:1], LOW)
            for s in range(2):
                for c in range(KC):
                    pool.memset(w_k[:, s, c, :, 0:1], LOW)
                pool.memset(w_a2[:, s, :, 0:1], 0.0)
                pool.memset(w_e2[:, s, :, 0:1], 0.0)
            pool.memset(w_ev[:, :, 0:1], 0.0)
            pool.drain().then_inc(wk_pad, 1)
            end_stage(pool, "W")
            end_stage(pool, "E1")
            iotas(L1)
            end_stage(pool, "F1")
            scatter(L1)
            end_stage(pool, "G1")
            end_stage(pool, "H1")
            gather(L1)
            end_stage(pool, "I1")

        @block.tensor
        def _(pe):
            pe.sem_inc(tr_done, 2)
            pe.sem_inc(proj_done, 12)
            pe.sem_inc(sc_done, 2)
            pe.sem_inc(pv_done, 2)
            pe.sem_inc(op_done, 2)
            pe.sem_inc(rt_done, 2)
            pe.sem_inc(wk_yt, 2)
            for L in (L0, L1):
                pe.sem_inc(lay[L.name]["t_done"], TD)
                pe.sem_inc(lay[L.name]["u_done"], 2)
                pe.sem_inc(lay[L.name]["d_done"], TD)

            def transposes(n, s):
                pe.wait_ge(xn_ready, n + 1)
                pe.wait_ge(xT_ready, n + 1)
                for j in range(GT):
                    for c in range(KC):
                        m = pe.transpose(ps[:, c, j * P:(j + 1) * P], n_x[:, s, j, c * P:(c + 1) * P], ident[:])
                m.then_inc(tr_done, 1)

            pe.wait_ge(const_ready, 4)
            pe.wait_ge(in_sem, 16 * n_load["A"])
            with pe.Fori(0, NG // 2) as b:
                for s in range(2):
                    g = 2 * b + s
                    transposes(g, s)
                    pe.wait_ge(ctx_in[s], 16 * b + 16)
                    for j in range(3 * KC):
                        if j == 2 * KC:
                            pe.wait_ge(xT_ready, g + 2)
                        pe.wait_ge(proj_out, 6 * g + j + 1)
                        src = a_ctx if j < 2 * KC else a_xT
                        for c in range(KC):
                            m = pe.matmul(ps[:, 2 + j, :],
                                          a_w[:, (j // KC) * KC + c, (j % KC) * P:(j % KC) * P + P],
                                          src[:, s, c, :], start=(c == 0), stop=(c == KC - 1))
                        m.then_inc(proj_done, 1)
            end_stage(pe, "A")

            def blocks(done, freed, before_):
                with pe.Fori(0, NG // 2) as b:
                    for s in range(2):
                        pe.wait_ge(diag_in[s], before_ + 16 * 2 * TB * b + 16 * 2 * TB)
                        pe.wait_ge(freed, 2 * b + s + 1)
                        for n in range(NN):
                            m = pe.matmul(ps[:, 2 * s + n // 32, (n % 32) * HD:(n % 32) * HD + HD],
                                          diag[s][:, :, :, n].rearrange("p t h -> p (t h)"), kv[:, s, :, n],
                                          start=True, stop=True)
                        m.then_inc(done, 1)

            blocks(sc_done, sub_done, 0)
            end_stage(pe, "B")
            blocks(pv_done, o_done, 16 * 2 * TB * NG // 2)
            end_stage(pe, "C")

            pe.wait_ge(in_sem, 16 * n_load["D"])
            with pe.Fori(0, NG // 2) as b:
                for s in range(2):
                    pe.wait_ge(o_in[s], 16 * b + 16)
                    pe.wait_ge(op_used, 2 * b + s + 1)
                    for j in range(GT):
                        for c in range(KC):
                            m = pe.matmul(ps[:, 2 * s + j // 2, (j % 2) * D:(j % 2) * D + D],
                                          d_o[:, s, c, j * P:(j + 1) * P], d_w[:, c, :],
                                          start=(c == 0), stop=(c == KC - 1))
                    m.then_inc(op_done, 1)
            end_stage(pe, "D")

            def scores(L, g, s, gw):
                bank = ps[:, 2:2 + L.E * NT // 512, :].rearrange("p b n -> p (b n)")
                for j in range(GT):
                    for c in range(KC):
                        m = pe.matmul(bank[:, bass.ds((g * GT + j) * L.E, L.E)],
                                      e_xT[:, s, c, j * P:(j + 1) * P], gw[:, c, :],
                                      start=(c == 0), stop=(c == KC - 1))
                m.then_inc(rt_done, 1)

            pe.wait_ge(in_sem, 16 * n_load["E0"])
            transposes(NG, 0)

            def shared(b, last):
                for s in range(2):
                    g = 2 * b + s
                    pe.wait_ge(xT_ready, NG + g + 2)
                    scores(L0, g, s, e_g0)
                    for q, w in enumerate(HSP):
                        r = (3 * s + q) % 2
                        pe.wait_ge(sh_h, 3 * g + q + 1)
                        for k, wt in enumerate((e_w1, e_w3)):
                            for c in range(KC):
                                m = pe.matmul(ps[0:w, 3 + 2 * r + k, :], wt[:, c, P * q:P * q + w],
                                              e_xT[:, s, c, :], start=(c == 0), stop=(c == KC - 1))
                        m.then_inc(sh_done, 1)
                    if not (last and s == 1):
                        transposes(NG + g + 1, 1 - s)
                    pe.wait_ge(sh_h, 3 * g + 5)
                    for h in range(2):
                        pe.wait_ge(sh_zu, 2 * g + h + 1)
                        for j in (2 * h, 2 * h + 1):
                            for q, w in enumerate(HSP):
                                m = pe.matmul(ps[:, 7, (j % 2) * D:(j % 2) * D + D],
                                              e_h[0:w, s, q, j * P:(j + 1) * P], e_w2[0:w, q, :],
                                              start=(q == 0), stop=(q == 2))
                        m.then_inc(sh_z, 1)

            with pe.Fori(0, NG // 2 - 1) as b:
                shared(b, False)
            shared(NG // 2 - 1, True)
            end_stage(pe, "E0")

            def route(L, nth):
                F = L.E * NT
                nb = F // 512
                pe.wait_ge(hot_ready, nth)
                for q in range(nb):
                    pe.matmul(ps[:, q, :], before[:], r_m[:, q * 512:(q + 1) * 512], start=True, stop=True)
                    m = pe.matmul(ps[:, 4 + q, :], ones_h[:], r_m[:, q * 512:(q + 1) * 512], start=True, stop=True)
                m.then_inc(rank_ready, 1)
                pe.wait_ge(cmp_ready, nth)
                pe.matmul(ps[0:1, 4, 0:L.tiles], ones_h[0:L.E, 0:1], r_cmp[0:L.E, 0:L.tiles],
                          start=True, stop=True).then_inc(map_ready, 1)

            def experts(L):
                q = lay[L.name]
                h1 = L.H // L.NC

                def tr(i, s, bb):
                    pe.wait_ge(q["x_in"][s], 16 * bb + 16)
                    pe.wait_ge(q["t_ready"], i + 1)
                    for c in range(KC):
                        m = pe.transpose(ps[:, s % 2, c * P:(c + 1) * P], h_x[s][:, c * P:(c + 1) * P], ident[:])
                    m.then_inc(q["t_done"], 1)

                def up(i, s, bb):
                    pe.wait_ge(q["w_in"][s], 16 * bb + 16)
                    pe.wait_ge(q["t_ready"], i + 3)
                    pe.wait_ge(q["h_done"], i + 1)
                    for k in range(2):
                        for j in range(L.NC):
                            for c in range(KC):
                                o = ((k * KC + c) if L is L0 else (c * 2 + k)) * L.H + j * h1
                                m = pe.matmul(ps[0:h1, 2 + s % 2, (k * L.NC + j) * P:(k * L.NC + j) * P + P],
                                              h_w[s][:, o:o + h1], h_xT[:, s % 2, c, :],
                                              start=(c == 0), stop=(c == KC - 1))
                    m.then_inc(q["u_done"], 1)

                def down(i, s):
                    pe.wait_ge(q["h_done"], i + 3)
                    pe.wait_ge(q["y_done"], i + 1)
                    for j in range(L.NC):
                        w = h1 + (1 if L.bias and j == 0 else 0)
                        m = pe.matmul(ps[:, 4 + s % 2, 0:D], h_h[0:w, s % 2, j, :],
                                      h_w[s][0:w, L.up0 + j * D:L.up0 + (j + 1) * D],
                                      start=(j == 0), stop=(j == L.NC - 1))
                    m.then_inc(q["d_done"], 1)

                def body(b, first, last):
                    for s in range(TD):
                        i = TD * b + s
                        if not (last and s == TD - 1):
                            tr(i + 1, (s + 1) % TD, b + (s + 1) // TD)
                        up(i, s, b)
                        if not (first and s == 0):
                            down(i - 1, (s - 1) % TD)

                tr(0, 0, 0)
                body(0, True, False)
                with pe.Fori(1, L.tiles // TD - 1) as b:
                    body(b, False, False)
                body(L.tiles // TD - 1, False, True)
                down(L.tiles - 1, TD - 1)

            route(L0, 1)
            end_stage(pe, "F0")
            end_stage(pe, "G0")
            experts(L0)
            end_stage(pe, "H0")
            end_stage(pe, "I0")

            transposes(2 * NG, 0)

            def wkv(b, last):
                for s in range(2):
                    g = 2 * b + s
                    if not (last and s == 1):
                        transposes(2 * NG + g + 1, 1 - s)
                    pe.wait_ge(wk_y, g + 3)
                    pe.wait_ge(wk_yu, g + 1)
                    for j in range(GT):
                        for c in range(KC):
                            m = pe.transpose(ps[:, 2 + 2 * s + j // 2,
                                                (j % 2) * D + c * P:(j % 2) * D + c * P + P],
                                             w_y[:, s, c].rearrange("p b t -> p (b t)")[:, j * P:(j + 1) * P],
                                             ident[:])
                    m.then_inc(wk_yt, 1)

            with pe.Fori(0, NG // 2 - 1) as b:
                wkv(b, False)
            wkv(NG // 2 - 1, True)
            end_stage(pe, "W")

            pe.wait_ge(in_sem, 16 * n_load["E1"])
            with pe.Fori(0, NG // 2) as b:
                for s in range(2):
                    g = 2 * b + s
                    transposes(3 * NG + g, s)
                    pe.wait_ge(xT_ready, 3 * NG + g + 2)
                    scores(L1, g, s, e_g1)
            end_stage(pe, "E1")
            route(L1, 2)
            end_stage(pe, "F1")
            end_stage(pe, "G1")
            experts(L1)
            end_stage(pe, "H1")
            end_stage(pe, "I1")

        @block.scalar
        def _(act):
            act.sem_inc(xT_ready, 1)
            act.sem_inc(proj_out, 6)
            act.sem_inc(exp_done, 2)
            act.sem_inc(wk_e, 2)
            for s in range(2):
                act.sem_inc(qkv_st[s], 16)
                act.sem_inc(p_st[s], 16)
                act.sem_inc(o_st[s], 16 * TB)
            for L in (L0, L1):
                act.sem_inc(lay[L.name]["t_ready"], 2)

            def std(nth):
                act.wait_ge(var_ready, nth)
                act.activation(rstd[:], mean_v[:], ACT.Sqrt).then_inc(std_ready, 1)

            act.wait_ge(in_sem, 16 * n_load["A"])
            act.activation(tgate[:], tgate[:], ACT.Tanh).then_inc(tanh_done, 1)
            std(1)
            qkv_v = qkv_d.rearrange("u j (c p) n -> u p (j c) n", p=P)
            with act.Fori(0, NG // 2) as b:
                for s in range(2):
                    g = 2 * b + s
                    act.wait_ge(proj_done, 6 * g + 6)
                    act.wait_ge(tr_done, g + 3)
                    act.copy(a_xT[:, s, 0, :], ps[:, 0, :])
                    act.copy(a_xT[:, s, 1, :], ps[:, 1, :]).then_inc(xT_ready, 1)
                    act.wait_ge(qkv_st[s], 16 * b + 16)
                    for j in range(3 * KC):
                        act.wait_ge(proj_done, 6 * g + j + 13)
                        act.activation(a_out[:, s, j, :], ps[:, 2 + j, :], ACT.Identity,
                                       bias=a_b[:, j:j + 1]).then_inc(proj_out, 1)
                    act.wait_ge(proj_out, 6 * g + 12)
                    act.dma_start(qkv_v[bass.ds(g, 1)].rearrange("a p j n -> (a p) j n"), a_out[:, s])\
                       .then_inc(qkv_st[s], 16)
            for s in range(2):
                act.wait_ge(qkv_st[s], 16 * (NG // 2 + 1))
            end_stage(act, "A")

            with act.Fori(0, NG // 2) as b:
                for s in range(2):
                    g = 2 * b + s
                    act.wait_ge(sub_done, g + 3)
                    act.wait_ge(sum_done, g + 1)
                    act.wait_ge(p_st[s], 16 * b + 16)
                    act.activation(p_un[:, s].rearrange("p g n -> p n g"), s_sub[:, s], ACT.Exp)\
                       .then_inc(exp_done, 1)
                    act.wait_ge(exp_done, g + 3)
                    act.dma_start(p_d[bass.ds(g, 1)].rearrange("a p n -> (a p) n"),
                                  p_un[:, s].rearrange("p g n -> p (g n)")).then_inc(p_st[s], 16)
            for s in range(2):
                act.wait_ge(p_st[s], 16 * (NG // 2 + 1))
            end_stage(act, "B")

            ost_v = o_d.rearrange("u (h d) (t n) -> u t h d n", h=HEADS, t=TB)
            with act.Fori(0, NG // 2) as b:
                for s in range(2):
                    g = 2 * b + s
                    act.wait_ge(o_done, g + 3)
                    for t in range(TB):
                        act.dma_start(ost_v[bass.ds(g, 1), t].rearrange("a h d n -> (a h) d n"),
                                      o_nm[HEADS * t:HEADS * t + HEADS, s]).then_inc(o_st[s], 16)
            for s in range(2):
                act.wait_ge(o_st[s], 16 * TB * (NG // 2 + 1))
            end_stage(act, "C")
            end_stage(act, "D")

            def transposed(n, s, dst):
                act.wait_ge(tr_done, n + 3)
                for c in range(KC):
                    m = act.copy(dst(s, c), ps[:, c, :])
                m.then_inc(xT_ready, 1)

            def e_dst(s, c):
                return e_xT[:, s, c, :]

            std(2)
            act.wait_ge(in_sem, 16 * n_load["E0"])
            transposed(NG, 0, e_dst)

            def shared(b, last):
                for s in range(2):
                    g = 2 * b + s
                    for q, w in enumerate(HSP):
                        r = (3 * s + q) % 2
                        act.wait_ge(sh_done, 3 * g + q + 1)
                        act.wait_ge(sh_h, 3 * g + q + 1)
                        act.activation(e_sg[0:w, r, :], ps[0:w, 3 + 2 * r, :], ACT.Silu, bias=e_b[0:w, q:q + 1])\
                           .then_inc(sh_silu, 1)
                    if not (last and s == 1):
                        transposed(NG + g + 1, 1 - s, e_dst)

            with act.Fori(0, NG // 2 - 1) as b:
                shared(b, False)
            shared(NG // 2 - 1, True)
            end_stage(act, "E0")

            def route(L, nth):
                act.wait_ge(sc_ready, nth)
                act.activation(r_p[:, 0:L.E * NT], r_p[:, 0:L.E * NT], ACT.Exp).then_inc(pr_ready, 1)

            def experts(L):
                q = lay[L.name]
                h1 = L.H // L.NC

                def tr(i, s):
                    act.wait_ge(q["t_done"], i + TD + 1)
                    act.wait_ge(q["u_done"], i + 1)
                    act.copy(h_xT[:, s % 2].rearrange("p c n -> p (c n)"), ps[:, s % 2, 0:D])\
                       .then_inc(q["t_ready"], 1)

                def gate(i, s):
                    act.wait_ge(q["u_done"], i + 3)
                    act.wait_ge(q["h_done"], i + 1)
                    for j in range(L.NC):
                        bias = h_w[s][0:h1, L.b0 + j:L.b0 + j + 1] if L.bias else 0.0
                        m = act.activation(h_sg[0:h1, s % 2, j, :], ps[0:h1, 2 + s % 2, j * P:(j + 1) * P],
                                           ACT.Silu, bias=bias)
                    m.then_inc(q["s_done"], 1)

                def body(b, last):
                    for s in range(TD):
                        if not (last and s == TD - 1):
                            tr(TD * b + s + 1, (s + 1) % TD)
                        gate(TD * b + s, s)

                act.preload_act_table(ACT.Silu)
                tr(0, 0)
                with act.Fori(0, L.tiles // TD - 1) as b:
                    body(b, False)
                body(L.tiles // TD - 1, True)

            route(L0, 1)
            end_stage(act, "F0")
            end_stage(act, "G0")
            experts(L0)
            end_stage(act, "H0")
            end_stage(act, "I0")

            std(3)
            act.wait_ge(in_sem, 16 * n_load["W"])
            act.wait_ge(wk_pad, 1)
            with act.Fori(0, NG // 2) as b:
                for s in range(2):
                    g = 2 * b + s
                    act.wait_ge(wk_y, g + 1)
                    act.wait_ge(tr_done, 2 * NG + g + 3)
                    for c in range(KC):
                        m = act.copy(w_k[:, s, c, :, 1:SEQ + 1],
                                     ps[:, c, :].rearrange("p (b t) -> p b t", t=SEQ))
                    m.then_inc(xT_ready, 1)
                    for c in range(KC):
                        act.wait_ge(wk_t, 2 * g + c + 1)
                        act.activation(w_a2[:, c, :, 1:SEQ + 1], w_t[:, c, 0], ACT.Exp, bias=w_wu[:, c:c + 1])
                        act.activation(w_e2[:, c, :, 1:SEQ + 1], w_t[:, c, 1], ACT.Exp)
                        act.activation(w_ex[:, c].rearrange("p j b t -> p (j b t)"),
                                       w_t[:, c, 2:4].rearrange("p j b t -> p (j b t)"), ACT.Exp)\
                           .then_inc(wk_e, 1)
            end_stage(act, "W")

            std(4)
            with act.Fori(0, NG // 2) as b:
                for s in range(2):
                    act.wait_ge(rt_done, NG + 2 * b + s + 1)
                    transposed(3 * NG + 2 * b + s, s, e_dst)
            end_stage(act, "E1")
            route(L1, 2)
            end_stage(act, "F1")
            end_stage(act, "G1")
            experts(L1)
            end_stage(act, "H1")
            end_stage(act, "I1")

        @block.vector
        def _(dve):
            dve.sem_inc(sub_done, 2)
            dve.sem_inc(sum_done, 2)
            dve.sem_inc(o_done, 2)
            dve.sem_inc(op_used, 2)
            dve.sem_inc(sh_h, 2)
            dve.sem_inc(sh_zu, 1)
            dve.sem_inc(wk_y, 2)
            dve.sem_inc(wk_yu, 2)
            for L in (L0, L1):
                dve.sem_inc(lay[L.name]["h_done"], 2)
                dve.sem_inc(lay[L.name]["y_done"], 2)
                dve.sem_inc(lay[L.name]["g_used"], 2)
                for s in range(TD):
                    dve.sem_inc(lay[L.name]["y_st"][s], 16)

            def moments(nth):
                with dve.Fori(0, NT) as t:
                    dve.bn_stats(stats[:, bass.ds(t, 1), :].rearrange("p a k -> p (a k)"),
                                 x_res[:, bass.ds(t, 1), :].rearrange("p a d -> p (a d)"))
                dve.drain()
                dve.tensor_tensor(mean[:], stats[:, :, 1], stats[:, :, 4], ALU.add)
                dve.tensor_tensor(tmp_t[:], stats[:, :, 1], stats[:, :, 4], ALU.subtract)
                dve.tensor_tensor(mean_v[:], stats[:, :, 2], stats[:, :, 5], ALU.add)
                dve.drain()
                dve.tensor_scalar(mean[:], mean[:], 0.5, None, ALU.mult)
                dve.tensor_scalar(mean_v[:], mean_v[:], 1.0 / D, EPS, ALU.mult, ALU.add)
                dve.tensor_tensor(tmp_t[:], tmp_t[:], tmp_t[:], ALU.mult)
                dve.drain()
                dve.scalar_tensor_tensor(mean_v[:], tmp_t[:], 0.25, mean_v[:], ALU.mult, ALU.add)\
                   .then_inc(var_ready, 1)
                dve.wait_ge(std_ready, nth)
                dve.reciprocal(rstd[:], rstd[:])
                dve.drain()

            def normed(dst, t):
                return dve.tensor_scalar(dst, x_res[:, bass.ds(t, 1), :].rearrange("p a d -> p (a d)"),
                                         mean[:, bass.ds(t, 1)], rstd[:, bass.ds(t, 1)],
                                         ALU.subtract, ALU.mult)

            def norm_group(n, g, s):
                dve.wait_ge(tr_done, n + 1)
                dve.sem_inc(spacer, 1)
                for j in range(GT):
                    m = normed(n_x[:, s, j, :], g * GT + j)
                m.then_inc(xn_ready, 1)

            dve.wait_ge(in_sem, 16 * n_load["A"])
            moments(1)
            with dve.Fori(0, NG // 2) as b:
                for s in range(2):
                    norm_group(2 * b + s, 2 * b + s, s)
            end_stage(dve, "A")

            with dve.Fori(0, NG // 2) as b:
                for s in range(2):
                    g = 2 * b + s
                    sc = ps[:, 2 * s:2 * s + 2, :].rearrange("p a (n g) -> p (a n) g", g=HEADS)
                    dve.wait_ge(sc_done, g + 3)
                    dve.reduce_max(smax[:], sc, AX)
                    dve.drain()
                    dve.wait_ge(exp_done, g + 1)
                    dve.tensor_tensor(s_sub[:, s], sc, smax[:].unsqueeze(2).to_broadcast([P, NN, HEADS]),
                                      ALU.subtract).then_inc(sub_done, 1)
                    dve.wait_ge(exp_done, g + 3)
                    dve.sem_inc(spacer, 1)
                    dve.reduce_sum(rsum[:, bass.ds(g, 1), :].rearrange("p a n -> p (a n)"),
                                   p_un[:, s].rearrange("p g n -> p n g"), AX).then_inc(sum_done, 1)
            dve.drain()
            dve.reciprocal(rsum[:], rsum[:])
            end_stage(dve, "B")

            with dve.Fori(0, NG // 2) as b:
                for s in range(2):
                    g = 2 * b + s
                    dve.wait_ge(o_st[s], 16 * TB * b + 16 * TB)
                    dve.wait_ge(pv_done, g + 3)
                    dve.sem_inc(spacer, 1)
                    dve.tensor_tensor(o_nm[:, s].rearrange("p d n -> p n d"),
                                      ps[:, 2 * s:2 * s + 2, :].rearrange("p a (n d) -> p (a n) d", d=HD),
                                      rsum[:, bass.ds(g, 1), :].rearrange("p a n -> p (a n)").unsqueeze(2)
                                      .to_broadcast([P, NN, HD]), ALU.mult).then_inc(o_done, 1)
            end_stage(dve, "C")

            def group_of(g, ap):
                return ap[:, bass.ds(g * GT, GT), :].rearrange("p t d -> p (t d)")

            dve.wait_ge(in_sem, 16 * n_load["D"])
            dve.wait_ge(tanh_done, 1)
            dve.tensor_scalar(d_bo[:], d_bo[:], tgate[:, 0:1], None, ALU.mult)
            dve.drain()
            with dve.Fori(0, NG // 2) as b:
                for s in range(2):
                    g = 2 * b + s
                    dve.wait_ge(op_done, g + 3)
                    dve.sem_inc(spacer, 1)
                    dve.scalar_tensor_tensor(group_of(g, x_res), ps[:, 2 * s:2 * s + 2, :]
                                             .rearrange("p a n -> p (a n)"), tgate[:, 0:1],
                                             group_of(g, x_res), ALU.mult, ALU.add).then_inc(op_used, 1)
                    dve.drain()
                    dve.tensor_tensor(x_res[:, bass.ds(g * GT, GT), :], x_res[:, bass.ds(g * GT, GT), :],
                                      d_bo[:].unsqueeze(1).to_broadcast([P, GT, D]), ALU.add)
            end_stage(dve, "D")

            moments(2)
            dve.wait_ge(in_sem, 16 * n_load["E0"])
            norm_group(NG, 0, 0)

            def shared(b, last):
                for s in range(2):
                    g = 2 * b + s
                    if not (last and s == 1):
                        norm_group(NG + g + 1, g + 1, 1 - s)
                    for q, w in enumerate(HSP):
                        r = (3 * s + q) % 2
                        dve.wait_ge(sh_silu, 3 * g + q + 1)
                        dve.scalar_tensor_tensor(e_h[0:w, s, q, :], ps[0:w, 4 + 2 * r, :], e_b[0:w, 3 + q:4 + q],
                                                 e_sg[0:w, r, :], ALU.add, ALU.mult).then_inc(sh_h, 1)
                    for h in range(2):
                        dve.wait_ge(sh_z, 2 * g + h + 1)
                        dve.sem_inc(spacer, 1)
                        dve.tensor_tensor(z[:, bass.ds(g * GT + 2 * h, 2), :],
                                          ps[:, 7, :].rearrange("p (t d) -> p t d", t=2),
                                          e_bs2[:].unsqueeze(1).to_broadcast([P, 2, D]), ALU.add)\
                           .then_inc(sh_zu, 1)

            with dve.Fori(0, NG // 2 - 1) as b:
                shared(b, False)
            shared(NG // 2 - 1, True)
            end_stage(dve, "E0")

            def route(L, nth):
                E, K, F = L.E, L.K, L.E * NT

                def te(ap):
                    return ap[:, 0:F].rearrange("p (t e) -> p t e", e=E)

                def et(ap):
                    return ap[:, 0:F].rearrange("p (e t) -> p e t", t=NT)

                def over(ap, shape):
                    return ap.unsqueeze(2).to_broadcast(shape)

                TE, ET = [P, NT, E], [P, E, NT]
                raw = ps[:, 2:2 + F // 512, :].rearrange("p b (t e) -> p (b t) e", e=E)
                dve.reduce_max(r_t1[:], raw, AX)
                dve.drain()
                dve.tensor_tensor(te(r_p), raw, over(r_t1[:], TE), ALU.subtract).then_inc(sc_ready, 1)
                dve.wait_ge(pr_ready, nth)
                dve.reduce_sum(r_t1[:], te(r_p), AX)
                dve.drain()
                dve.reciprocal(r_t1[:], r_t1[:])
                dve.drain()
                dve.tensor_tensor(te(r_p), te(r_p), over(r_t1[:], TE), ALU.mult)
                dve.drain()
                chosen_by = te(r_p)
                if L is L0:
                    dve.wait_ge(in_sem, 16 * n_load["F0"])
                    dve.tensor_tensor(te(r_b), te(r_p), r_gb[:].unsqueeze(1).to_broadcast(TE), ALU.add)
                    dve.drain()
                    chosen_by = te(r_b)
                for t in range(NT):
                    dve.max(r_val[:, t, :], chosen_by[:, t, :])
                dve.drain()
                for t in range(NT):
                    dve.max_index(r_idx[:, t, :], r_val[:, t, :], chosen_by[:, t, :])
                dve.drain()
                dve.tensor_copy(r_idf[:], r_idx[:])
                dve.wait_ge(const_ready, 4 + nth)
                dve.drain()

                def hot(k):
                    dve.tensor_tensor(te(r_w), r_ie[:, 0:E].unsqueeze(1).to_broadcast(TE),
                                      over(r_idf[:, :, k], TE), ALU.is_equal)
                    dve.drain()

                if L is L0:
                    dve.memset(r_s[:, 0:F], 0.0)
                    for k in range(K):
                        hot(k)
                        dve.tensor_tensor(te(r_s), te(r_s), te(r_w), ALU.add)
                        dve.tensor_tensor(te(r_c), te(r_p), te(r_w), ALU.mult)
                        dve.drain()
                        dve.reduce_sum(weight[:, :, k], te(r_c), AX)
                    dve.tensor_copy(r_m[:, 0:F], r_s[:, 0:F]).then_inc(hot_ready, 1)
                else:
                    for t in range(NT):
                        dve.match_replace(te(r_w)[:, t, :], r_val[:, t, :], te(r_p)[:, t, :], -1.0)
                    dve.drain()
                    dve.tensor_scalar(r_m[:, 0:F], r_w[:, 0:F], 0.0, None, ALU.is_lt).then_inc(hot_ready, 1)
                    dve.reduce_sum(r_t1[:], r_val[:], AX)
                    dve.drain()
                    dve.tensor_scalar(tmp_t[:], r_t1[:], 0.0, None, ALU.is_equal)
                    dve.drain()
                    dve.tensor_tensor(r_t1[:], r_t1[:], tmp_t[:], ALU.add)
                    dve.drain()
                    dve.reciprocal(r_t1[:], r_t1[:])
                    dve.drain()
                    dve.tensor_tensor(weight[:], r_val[:], over(r_t1[:], [P, NT, CHOICES]), ALU.mult)
                dve.wait_ge(rank_ready, nth)
                nb = F // 512
                dve.tensor_copy(et(r_c).rearrange("p e t -> p t e"),
                                ps[:, 4:4 + nb, :].rearrange("p b (t e) -> p (b t) e", e=E))
                dve.drain()
                dve.tensor_tensor_scan(r_i[:, 0:F], r_keep[:, 0:F], r_c[:, 0:F], 0.0, ALU.mult, ALU.add)
                dve.drain()
                dve.tensor_tensor(et(r_w), over(et(r_i)[:, :, NT - 1], ET), r_ij[:].unsqueeze(1).to_broadcast(ET),
                                  ALU.is_gt)
                dve.drain()
                dve.reduce_sum(r_te[:, 0:E], et(r_w), AX)
                dve.memset(r_dg[:, 0:E], 1.0)
                dve.drain()
                dve.tensor_tensor_scan(r_cum[:, 0:E], r_dg[:, 0:E], r_te[:, 0:E], 0.0, ALU.mult, ALU.add)
                dve.drain()
                dve.tensor_tensor(r_dg[:, 0:E], r_cum[:, 0:E], ident[:, 0:E], ALU.mult)
                dve.tensor_tensor(r_st[:, 0:E], r_cum[:, 0:E], r_te[:, 0:E], ALU.subtract)
                dve.drain()
                dve.reduce_sum(r_end[:], r_dg[:, 0:E], AX)
                dve.tensor_scalar(r_st[:, 0:E], r_st[:, 0:E], float(P), None, ALU.mult)
                dve.tensor_tensor(r_i[:, 0:F], r_i[:, 0:F], r_c[:, 0:F], ALU.subtract)
                dve.drain()
                dve.tensor_scalar(r_cmp[:, 0:L.tiles], r_it[:, 0:L.tiles], r_end[:, 0:1], None, ALU.is_ge)\
                   .then_inc(cmp_ready, 1)
                dve.tensor_tensor(et(r_i), et(r_i), over(r_st[:, 0:E], ET), ALU.add)
                dve.drain()
                dve.tensor_tensor(te(r_s), ps[:, 0:nb, :].rearrange("p b (t e) -> p (b t) e", e=E),
                                  et(r_i).rearrange("p e t -> p t e"), ALU.add)
                dve.drain()
                for k in range(K):
                    hot(k)
                    dve.tensor_tensor(te(r_c), te(r_s), te(r_w), ALU.mult)
                    dve.drain()
                    dve.reduce_sum(r_sl[:, :, k], te(r_c), AX)
                dve.drain()
                dve.tensor_copy(slot_i[:, :, 0:K], r_sl[:, :, 0:K])
                dve.wait_ge(map_ready, nth)
                dve.tensor_scalar(tile_e[:, 0:L.tiles], ps[0:1, 4, 0:L.tiles], float(E - 1), None, ALU.min)

            def rows(L, nth):
                q = lay[L.name]

                def body(b, first):
                    for s in range(2):
                        if not first:
                            dve.wait_ge(q["row_st"][s], 16 * L.K * b)
                            dve.sem_inc(spacer, 1)
                        normed(g_rows[s][:], 2 * b + s)
                        dve.tensor_copy(idx_s[:, s, 0:L.K], slot_i[:, bass.ds(2 * b + s, 1), 0:L.K]
                                        .rearrange("p a k -> p (a k)")).then_inc(row_ready, 1)

                body(0, True)
                with dve.Fori(1, NT // 2) as b:
                    body(b, False)

            def experts(L):
                q = lay[L.name]
                h1 = L.H // L.NC

                def hidden(i, s):
                    dve.wait_ge(q["s_done"], i + 1)
                    dve.wait_ge(q["d_done"], i + 3)
                    for j in range(L.NC):
                        up = ps[0:h1, 2 + s % 2, (L.NC + j) * P:(L.NC + j + 1) * P]
                        sg = h_sg[0:h1, s % 2, j, :]
                        if L.bias:
                            m = dve.scalar_tensor_tensor(h_h[0:h1, s % 2, j, :], up,
                                                         h_w[s][0:h1, L.b0 + L.NC + j:L.b0 + L.NC + j + 1], sg,
                                                         ALU.add, ALU.mult)
                        else:
                            m = dve.tensor_tensor(h_h[0:h1, s % 2, j, :], up, sg, ALU.mult)
                    m.then_inc(q["h_done"], 1)

                def result(i, s, bb):
                    dve.wait_ge(q["d_done"], i + TD + 1)
                    dve.wait_ge(q["y_st"][s], 16 * bb + 16)
                    dve.tensor_copy(h_y[s][:], ps[:, 4 + s % 2, 0:D]).then_inc(q["y_done"], 1)

                def body(b, first):
                    for s in range(TD):
                        i = TD * b + s
                        hidden(i, s)
                        if not (first and s == 0):
                            result(i - 1, (s - 1) % TD, b if s else b - 1)

                body(0, True)
                with dve.Fori(1, L.tiles // TD) as b:
                    body(b, False)
                result(L.tiles - 1, TD - 1, L.tiles // TD - 1)

            def combine(L, gate):
                q = lay[L.name]
                with dve.Fori(0, NT // 2) as b:
                    for s in range(2):
                        t = 2 * b + s
                        dve.wait_ge(q["g_in"][s], 16 * L.K * b + 16 * L.K)
                        dve.sem_inc(spacer, 1)
                        for k in range(L.K):
                            w = weight[:, bass.ds(t, 1), k]
                            if k == 0 and L is L1:
                                dve.tensor_scalar(c_acc[:, s, :], c_g[s][:, k, :], w, None, ALU.mult)
                            else:
                                old = c_acc[:, s, :] if k else z[:, bass.ds(t, 1), :].rearrange("p a d -> p (a d)")
                                dve.scalar_tensor_tensor(c_acc[:, s, :], c_g[s][:, k, :], w, old,
                                                         ALU.mult, ALU.add)
                            dve.drain()
                        xt = x_res[:, bass.ds(t, 1), :].rearrange("p a d -> p (a d)")
                        dve.scalar_tensor_tensor(xt, c_acc[:, s, :], gate, xt, ALU.mult, ALU.add)\
                           .then_inc(q["g_used"], 1)

            route(L0, 1)
            end_stage(dve, "F0")
            rows(L0, 1)
            end_stage(dve, "G0")
            dve.memset(h_h[:], 1.0)
            dve.drain()
            experts(L0)
            end_stage(dve, "H0")
            combine(L0, tgate[:, 2:3])
            end_stage(dve, "I0")

            moments(3)
            dve.wait_ge(in_sem, 16 * n_load["W"])
            dve.wait_ge(wk_pad, 1)
            for c in range(KC):
                dve.memset(w_d[:], 1.0)
                dve.drain()
                dve.tensor_scalar(w_dec[:, c, :, 1:SEQ + 1], w_d[:], w_wu[:, c:c + 1], None, ALU.mult)
                dve.drain()

            def flat(ap):
                return ap.rearrange("p b t -> p (b t)")

            def exponents(g, s, c):
                key = w_k[:, s, c, :, 1:SEQ + 1]
                o_prev, o_now = w_o[:, :, 0:SEQ], w_o[:, :, 1:SEQ + 1]
                u = w_wu[:, KC + c:KC + c + 1]
                dve.drain()
                if c == 0:
                    dve.wait_ge(xT_ready, 2 * NG + g + 2)
                dve.tensor_tensor_scan(flat(w_o[:]), flat(w_dec[:, c]), flat(w_k[:, s, c]), 0.0, ALU.add, ALU.max)
                dve.drain()
                dve.scalar_tensor_tensor(w_n[:], key, u, o_prev, ALU.add, ALU.max)
                dve.wait_ge(wk_e, 2 * g + c + 1)
                dve.tensor_tensor(w_t[:, c, 0], o_prev, o_now, ALU.subtract)
                dve.tensor_tensor(w_t[:, c, 1], key, o_now, ALU.subtract)
                dve.drain()
                dve.tensor_tensor(w_t[:, c, 2], o_prev, w_n[:], ALU.subtract)
                dve.scalar_tensor_tensor(w_t[:, c, 3], key, u, w_n[:], ALU.add, ALU.subtract).then_inc(wk_t, 1)

            def sums(g, s, c, bb):
                val = w_v[:, s, c, :].rearrange("p (b t) -> p b t", t=SEQ)
                dve.drain()
                dve.wait_ge(wk_e, 2 * g + c + 3)
                if c == 0:
                    dve.wait_ge(wk_v[s], 16 * bb + 16)
                dve.tensor_tensor(w_ev[:, :, 1:SEQ + 1], w_e2[:, c, :, 1:SEQ + 1], val, ALU.mult)
                dve.tensor_tensor(w_m[:], w_ex[:, c, 1], val, ALU.mult)
                dve.tensor_tensor_scan(flat(w_q[:]), flat(w_a2[:, c]), flat(w_e2[:, c]), 0.0, ALU.mult, ALU.add)
                dve.drain()
                dve.tensor_tensor_scan(flat(w_p[:]), flat(w_a2[:, c]), flat(w_ev[:]), 0.0, ALU.mult, ALU.add)
                dve.tensor_tensor(w_d[:], w_ex[:, c, 0], w_q[:, :, 0:SEQ], ALU.mult)
                dve.drain()
                dve.tensor_tensor(w_n[:], w_ex[:, c, 0], w_p[:, :, 0:SEQ], ALU.mult)
                dve.tensor_tensor(w_d[:], w_d[:], w_ex[:, c, 1], ALU.add)
                dve.drain()
                dve.tensor_tensor(w_n[:], w_n[:], w_m[:], ALU.add)
                dve.reciprocal(w_d[:], w_d[:])
                dve.drain()
                if c == 0:
                    dve.wait_ge(wk_yt, g + 1)
                m = dve.tensor_tensor(w_y[:, s, c], w_n[:], w_d[:], ALU.mult)
                if c == KC - 1:
                    m.then_inc(wk_y, 1)

            def residual(g, s):
                dve.wait_ge(wk_yt, g + 3)
                dve.sem_inc(spacer, 1)
                dve.scalar_tensor_tensor(group_of(g, x_res), ps[:, 2 + 2 * s:4 + 2 * s, :]
                                         .rearrange("p a n -> p (a n)"), tgate[:, 1:2],
                                         group_of(g, x_res), ALU.mult, ALU.add).then_inc(wk_yu, 1)

            def wkv(b, first, last):
                for s in range(2):
                    g = 2 * b + s
                    if not (last and s == 1):
                        norm_group(2 * NG + g + 1, g + 1, 1 - s)
                    exponents(g, s, 0)
                    prev = not (first and s == 0)
                    if prev:
                        sums(g - 1, 1 - s, 1, None)
                    exponents(g, s, 1)
                    sums(g, s, 0, b)
                    if prev:
                        residual(g - 1, 1 - s)

            norm_group(2 * NG, 0, 0)
            wkv(0, True, False)
            with dve.Fori(1, NG // 2 - 1) as b:
                wkv(b, False, False)
            wkv(NG // 2 - 1, False, True)
            sums(NG - 1, 1, 1, None)
            residual(NG - 1, 1)
            end_stage(dve, "W")

            moments(4)
            with dve.Fori(0, NG // 2) as b:
                for s in range(2):
                    norm_group(3 * NG + 2 * b + s, 2 * b + s, s)
            end_stage(dve, "E1")
            route(L1, 2)
            end_stage(dve, "F1")
            rows(L1, 2)
            end_stage(dve, "G1")
            experts(L1)
            end_stage(dve, "H1")
            combine(L1, tgate[:, 3:4])
            end_stage(dve, "I1")


def kernel(**inputs):
    import numpy as np
    import concourse.bacc as bacc
    from concourse.bass_utils import run_bass_kernel_spmd

    a = {k: np.asarray(v) for k, v in inputs.items()}

    def cols(v, n=1):
        v = np.pad(v, (0, -len(v) % P))
        return np.ascontiguousarray(v.reshape(-1, P).T)

    f = np.float32
    wqkvT = np.concatenate([a["L0_xattn_W" + n].T for n in "kvq"])
    bqkv = np.concatenate([cols(a["L0_xattn_b" + n]) for n in "kvq"], axis=1)
    exp0 = np.zeros((L0.E, P, L0.W), f)
    for k, n in enumerate(("w1", "w3")):
        w = a["L0_ffn_" + n].transpose(0, 2, 1).reshape(L0.E, KC, P, L0.H).transpose(0, 2, 1, 3)
        exp0[:, :, k * KC * L0.H:(k + 1) * KC * L0.H] = w.reshape(L0.E, P, KC * L0.H)
    h1 = L0.H // L0.NC
    w2 = a["L0_ffn_w2"].transpose(0, 2, 1)
    for j in range(L0.NC):
        exp0[:, 0:h1, L0.up0 + j * D:L0.up0 + (j + 1) * D] = w2[:, j * h1:(j + 1) * h1]
        exp0[:, 0:h1, L0.b0 + j] = a["L0_ffn_b1"][:, j * h1:(j + 1) * h1]
        exp0[:, 0:h1, L0.b0 + L0.NC + j] = a["L0_ffn_b3"][:, j * h1:(j + 1) * h1]
    exp0[:, h1, L0.up0:L0.up0 + D] = a["L0_ffn_b2"]
    exp1 = np.zeros((L1.E, P, L1.W), f)
    gu = a["L1_ffn_gate_up_weights"].reshape(L1.E, KC, P, 2 * L1.H).transpose(0, 2, 1, 3)
    exp1[:, :, 0:L1.up0] = gu.reshape(L1.E, P, L1.up0)
    exp1[:, 0:L1.H, L1.up0:L1.up0 + D] = a["L1_ffn_down_weights"]
    feeds = dict(
        x=a["x"].reshape(NTOK, D),
        ctxT=np.ascontiguousarray(a["ctx_2048"].reshape(NTOK, D).T),
        gates=np.concatenate([a["g_xattn"], a["g_ffn"]]),
        wqkvT=wqkvT, bqkv=bqkv, woT=a["L0_xattn_Wo"].T, bo=a["L0_xattn_bo"],
        gate0T=a["L0_ffn_gate_w"].T, gate0b=a["L0_ffn_gate_b"], exp0=exp0,
        sh1T=a["L0_ffn_ws1"].T, sh3T=a["L0_ffn_ws3"].T,
        sh2T=np.pad(a["L0_ffn_ws2"].T, ((0, 3 * P - HS), (0, 0))),
        shb=np.concatenate([cols(a["L0_ffn_bs1"]), cols(a["L0_ffn_bs3"])], axis=1), bs2=a["L0_ffn_bs2"],
        wkv_w=cols(a["L1_xattn_w"]), wkv_u=cols(a["L1_xattn_u"]),
        gate1T=a["L1_ffn_gate_weight"].T, exp1=exp1,
    )
    nc = bacc.Bacc("TRN2", target_bir_lowering=False, num_devices=1)
    arrays, args = {}, []
    for name, v in feeds.items():
        v = np.ascontiguousarray(v)
        arrays[f"in_{name}"] = v
        args.append(nc.dram_tensor(f"in_{name}", v.shape, mybir.dt.from_np(v.dtype), kind="ExternalInput").ap())
    args.append(nc.dram_tensor("out_x", (NTOK, D), F32, kind="ExternalOutput").ap())
    flamingo(nc, *args)
    r = run_bass_kernel_spmd(nc, [arrays], core_ids=[0])
    return r.results[0]["out_x"].reshape(64, 64, D)
```

```python
from contextlib import ExitStack

import concourse.bass as bass
from concourse import mybir

F32 = mybir.dt.float32
BF16 = mybir.dt.bfloat16
I32 = mybir.dt.int32
U32 = mybir.dt.uint32
ALU = mybir.AluOpType
ACT = mybir.ActivationFunctionType
AX = mybir.AxisListType.X

P = 128
D = 256
KC = D // P
NTOK = 64 * 64
NT = NTOK // P
GT = 4
GS = GT * P
NG = NTOK // GS
HEADS = 16
HD = D // HEADS
TB = P // HD
NN = GS // TB
SEQ = 64
GB = GS // SEQ
EPS = 1e-5
LOW = -1e38
HS = 352
HSP = [128, 128, 96]
CHOICES = 8


TD = 8
XB = 2
NA = 4
META = 1 + 2 * CHOICES
RW = 280
RS = 4


class Layer:

    def __init__(self, name, experts, top, hidden, chunks, bias):
        self.name, self.E, self.K, self.H, self.NC, self.bias = name, experts, top, hidden, chunks, bias
        self.MH = hidden // chunks
        self.tiles = -(-(NTOK * top // P + experts - 1) // TD) * TD
        self.up0 = 2 * KC * hidden
        self.W = self.up0 + chunks * D


L0 = Layer("a", 16, 6, 176, 2, True)
L1 = Layer("b", 64, 8, 96, 1, False)
MT = max(L0.tiles, L1.tiles)
def flamingo(nc, x, ctxT, gates, wqkvT, bqkv, woT, bo, gate0T, gate0b, exp0, exp0b, sh1T, sh3T, sh2T, shb, bs2,
             wkv_w, wkv_u, gate1T, exp1, out):
    qkv_d = nc.dram_tensor("qkv_d", (NG, 3, D, GS), F32).ap()
    p_d = nc.dram_tensor("p_d", (NG, P, HEADS * NN), F32).ap()
    o_d = nc.dram_tensor("o_d", (NG, D, GS), F32).ap()
    x_d = nc.dram_tensor("x_d", (P, NT * D), F32).ap()
    xs_d = {L.name: nc.dram_tensor(f"xs_{L.name}", (L.tiles * P, RW), F32).ap() for L in (L0, L1)}
    acc_d = {L.name: [nc.dram_tensor(f"acc_{L.name}{a}", (NTOK + P, D), F32).ap() for a in range(NA)]
             for L in (L0, L1)}

    ctx = ExitStack()
    with ctx:
        names = {}

        def sb_in(stack):
            def sb(name, shape, dt=F32):
                names[name] = names.get(name, 0) + 1
                return stack.enter_context(nc.sbuf_tensor(f"{name}_{names[name]}", shape, dt))
            return sb

        def sem(name):
            return ctx.enter_context(nc.semaphore(name))

        sb = sb_in(ctx)
        big = NT * D * 4
        x_res = nc.alloc_sbuf_tensor_at("x_res", [P, NT, D], F32, offset=nc.sbuf_top - big)
        z_at = nc.sbuf_top - 2 * big
        z = nc.alloc_sbuf_tensor_at("z", [P, NT, D], F32, offset=z_at)
        void_rows = nc.alloc_sbuf_tensor_at("void_rows", [P, TD, RW], F32, offset=z_at)
        zeros = nc.alloc_sbuf_tensor_at("zeros", [P, TD * D], F32, offset=z_at + TD * RW * 4)
        ident = sb("ident", [P, P])
        ones = sb("ones", [P, P])
        ones_h = sb("ones_h", [P, P], BF16)
        before = sb("before", [P, P], BF16)
        tgate = sb("tgate", [P, 4])
        stats = sb("stats", [P, NT, 6])
        mean = sb("mean", [P, NT])
        rstd = sb("rstd", [P, NT])
        mean_v = sb("mean_v", [P, NT])
        tmp_t = sb("tmp_t", [P, NT])
        slot_i = sb("slot_i", [P, NT, CHOICES], I32)
        meta = sb("meta", [P, NT, META])
        tile_e = sb("tile_e", [1, MT], I32)
        tile_ef = sb("tile_ef", [P, MT])
        void_p = sb("void_p", [P, TD], I32)
        idx_s = [sb(f"idx_s{s}", [P, CHOICES], I32) for s in range(RS)]
        rows_s = [sb(f"rows_s{s}", [P, RW]) for s in range(RS)]
        ps = ctx.enter_context(nc.psum_tensor("ps", [P, 8, 512], F32))

        with ExitStack() as st:
            s_ = sb_in(st)
            n_x = s_("n_x", [P, 2, GT, D])
            a_w = s_("a_w", [P, 3 * KC, D])
            a_b = s_("a_b", [P, 3 * KC])
            a_ctx = s_("a_ctx", [P, 2, KC, GS])
            a_xT = s_("a_xT", [P, 2, KC, GS])
            a_out = s_("a_out", [P, 2, 3 * KC, GS])
        with ExitStack() as st:
            s_ = sb_in(st)
            diag = [s_(f"diag{s}", [P, TB, HEADS, NN]) for s in range(2)]
            kv = s_("kv", [P, 2, HEADS, NN])
            s_sub = s_("s_sub", [P, 2, NN, HEADS])
            p_un = s_("p_un", [P, 2, HEADS, NN])
            o_nm = s_("o_nm", [P, 2, HEADS, NN])
            smax = s_("smax", [P, NN])
            rsum = s_("rsum", [P, NG, NN])
        with ExitStack() as st:
            s_ = sb_in(st)
            d_w = s_("d_w", [P, KC, D])
            d_bo = s_("d_bo", [P, D])
            d_o = s_("d_o", [P, 2, KC, GS])
        with ExitStack() as st:
            s_ = sb_in(st)
            s_("n_x", [P, 2, GT, D])
            e_xT = s_("e_xT", [P, 2, KC, GS])
            e_g0 = s_("e_g0", [P, KC, L0.E])
            e_g1 = s_("e_g1", [P, KC, L1.E])
            e_w1 = s_("e_w1", [P, KC, HS])
            e_w3 = s_("e_w3", [P, KC, HS])
            e_w2 = s_("e_w2", [P, 3, D])
            e_b = s_("e_b", [P, 6])
            e_bs2 = s_("e_bs2", [P, D])
            e_sg = s_("e_sg", [P, 2, GS])
            e_h = s_("e_h", [P, 2, 3, GS])
            s0_end = nc.sbuf_base
        with ExitStack() as st:
            s_ = sb_in(st)
            F = L1.E * NT
            r_p = s_("r_p", [P, F])
            r_b = s_("r_b", [P, F])
            r_w = s_("r_w", [P, F])
            r_c = s_("r_c", [P, F])
            r_i = s_("r_i", [P, F])
            r_s = s_("r_s", [P, F])
            r_keep = s_("r_keep", [P, F])
            r_m = s_("r_m", [P, F], BF16)
            r_val = s_("r_val", [P, NT, CHOICES])
            r_idx = s_("r_idx", [P, NT, CHOICES], U32)
            r_idf = s_("r_idf", [P, NT, CHOICES])
            r_sl = s_("r_sl", [P, NT, CHOICES])
            r_gb = s_("r_gb", [P, L0.E])
            r_ie = s_("r_ie", [P, L1.E])
            r_ij = s_("r_ij", [P, NT])
            r_it = s_("r_it", [P, MT])
            r_te = s_("r_te", [P, L1.E])
            r_cum = s_("r_cum", [P, L1.E])
            r_st = s_("r_st", [P, L1.E])
            r_dg = s_("r_dg", [P, L1.E])
            r_end = s_("r_end", [P, 1])
            r_cmp = s_("r_cmp", [P, MT], BF16)
            r_t1 = s_("r_t1", [P, NT])
        with ExitStack() as st:
            s_ = sb_in(st)
            h_x = [s_(f"h_x{s}", [P, XB, RW]) for s in range(TD // XB)]
            h_y = [s_(f"h_y{s}", [P, D]) for s in range(TD)]
            h_ix = [s_(f"h_ix{s}", [P, 1], I32) for s in range(TD)]
            h_w = s_("h_w", [P, TD, CHOICES])
            h_wc = s_("h_wc", [P, TD])
            h_xT = s_("h_xT", [P, 2, KC, P])
            h_sg = s_("h_sg", [P, 2, L0.H])
            h_h = s_("h_h", [P, 2, L0.H])
            h_hT = s_("h_hT", [P, 2, L0.NC, P])
            with ExitStack() as st1:
                s1 = sb_in(st1)
                w_all1 = s1("w_all1", [P, L1.E * L1.W])
                in_front = (nc.sbuf_top - big - (nc.sbuf_base - L1.E * L1.W * 4)) // (L1.W * 4 * 8) * 8
            h_gu = s_("h_gu", [P, 2, 2 * L0.H])
            w_bias = s_("w_bias", [P, L0.E * 2 * L0.H])
            assert nc.sbuf_base >= s0_end
            w_all0 = s_("w_all0", [P, L0.E * L0.W])
            assert nc.sbuf_base <= z_at
        with ExitStack() as st:
            s_ = sb_in(st)
            c_a = s_("c_a", [P, 2, NA, GT * D])
        with ExitStack() as st:
            s_ = sb_in(st)
            s_("n_x", [P, 2, GT, D])
            w_wu = s_("w_wu", [P, 2 * KC])
            w_dec = s_("w_dec", [P, KC, GB, SEQ + 1])
            w_k = s_("w_k", [P, 2, KC, GB, SEQ + 1])
            w_v = s_("w_v", [P, 2, KC, GS])
            w_o = s_("w_o", [P, GB, SEQ + 1])
            w_t = s_("w_t", [P, 2, 4, GB, SEQ])
            w_a2 = s_("w_a2", [P, 2, GB, SEQ + 1])
            w_e2 = s_("w_e2", [P, 2, GB, SEQ + 1])
            w_ex = s_("w_ex", [P, 2, 2, GB, SEQ])
            w_ev = s_("w_ev", [P, GB, SEQ + 1])
            w_p = s_("w_p", [P, GB, SEQ + 1])
            w_q = s_("w_q", [P, GB, SEQ + 1])
            w_n = s_("w_n", [P, GB, SEQ])
            w_m = s_("w_m", [P, GB, SEQ])
            w_d = s_("w_d", [P, GB, SEQ])
            w_y = s_("w_y", [P, 2, KC, GB, SEQ])

        stage_done = sem("stage_done")
        spacer = sem("spacer")
        in_sem = sem("in_sem")
        in_count = [0]
        zeroed = sem("zeroed")
        const_ready = sem("const_ready")
        tanh_done = sem("tanh_done")
        var_ready = sem("var_ready")
        std_ready = sem("std_ready")
        xn_ready = sem("xn_ready")
        tr_done = sem("tr_done")
        xT_ready = sem("xT_ready")
        ctx_in = [sem(f"ctx_in{s}") for s in range(2)]
        proj_done = sem("proj_done")
        proj_out = sem("proj_out")
        qkv_st = [sem(f"qkv_st{s}") for s in range(2)]
        diag_in = [sem(f"diag_in{s}") for s in range(2)]
        diag_zero = sem("diag_zero")
        sc_done = sem("sc_done")
        sub_done = sem("sub_done")
        exp_done = sem("exp_done")
        sum_done = sem("sum_done")
        p_st = [sem(f"p_st{s}") for s in range(2)]
        pv_done = sem("pv_done")
        o_done = sem("o_done")
        o_st = [sem(f"o_st{s}") for s in range(2)]
        o_in = [sem(f"o_in{s}") for s in range(2)]
        op_done = sem("op_done")
        op_used = sem("op_used")
        sh_done = sem("sh_done")
        sh_silu = sem("sh_silu")
        sh_h = sem("sh_h")
        sh_z = sem("sh_z")
        sh_zu = sem("sh_zu")
        rt_done = sem("rt_done")
        sc_ready = sem("sc_ready")
        pr_ready = sem("pr_ready")
        hot_ready = sem("hot_ready")
        rank_ready = sem("rank_ready")
        cmp_ready = sem("cmp_ready")
        map_ready = sem("map_ready")
        row_ready = sem("row_ready")
        lay = {}
        for L in (L0, L1):
            n = L.name
            lay[n] = dict(
                row_st=[sem(f"row_st{n}{s}") for s in range(RS)],
                x_in=[sem(f"x_in{n}{s}") for s in range(TD // XB)],
                t_done=sem(f"t_done{n}"),
                t_ready=sem(f"t_ready{n}"),
                u_done=sem(f"u_done{n}"),
                b_done=sem(f"b_done{n}"),
                s_done=sem(f"s_done{n}"),
                h_done=sem(f"h_done{n}"),
                ht_done=sem(f"ht_done{n}"),
                ht_ready=sem(f"ht_ready{n}"),
                d_done=sem(f"d_done{n}"),
                y_done=sem(f"y_done{n}"),
                ix_done=sem(f"ix_done{n}"),
                chain=[sem(f"chain{n}{a}") for a in range(NA)],
                a_in=[sem(f"a_in{n}{s}") for s in range(2)],
                a_used=sem(f"a_used{n}"),
            )
        wk_y = sem("wk_y")
        wk_t = sem("wk_t")
        wk_e = sem("wk_e")
        wk_yt = sem("wk_yt")
        wk_yu = sem("wk_yu")
        wk_k = sem("wk_k")
        wk_v = [sem(f"wk_v{s}") for s in range(2)]
        wk_pad = sem("wk_pad")
        w_in = sem("w_in")
        x_st = sem("x_st")
        out_st = sem("out_st")
        void_ready = sem("void_ready")
        void_st = sem("void_st")

        block = ctx.enter_context(nc.Block())

        stages = ["A", "B", "C", "D", "E0", "F0", "S0", "H0", "I0", "W", "E1", "F1", "S1", "H1", "I1"]

        def end_stage(eng, name):
            n = stages.index(name) + 1
            eng.drain().then_inc(stage_done, 1)
            eng.wait_ge(stage_done, 5 * n)

        @block.sync
        def _(sp):
            def load(dst, src):
                sp.dma_start(dst, src).then_inc(in_sem, 16)
                in_count[0] += 1

            def loaded():
                sp.wait_ge(in_sem, 16 * in_count[0])

            x_v = x.rearrange("(t p) d -> p t d", p=P)
            for q in range(4):
                load(x_res[:, q * NT // 4:(q + 1) * NT // 4, :], x_v[:, q * NT // 4:(q + 1) * NT // 4, :])
            load(a_w[:], wqkvT.rearrange("(a p) n -> p a n", p=P))
            load(a_b[:], bqkv)
            load(tgate[:], gates.partition_broadcast(P))
            ctx_v = ctxT.rearrange("(c p) (g n) -> g p c n", p=P, n=GS)

            def a_group(b, s):
                sp.wait_ge(proj_done, 12 * b + 6 * s + 6)
                sp.dma_start(a_ctx[:, s], ctx_v[bass.ds(2 * b + s, 1)].rearrange("a p c n -> (a p) c n"))\
                  .then_inc(ctx_in[s], 16)

            with sp.Fori(0, NG // 2) as b:
                for s in range(2):
                    a_group(b, s)
            end_stage(sp, "A")

            q_v = qkv_d.rearrange("u j (h d) (t n) -> u j t d h n", h=HEADS, t=TB)
            v_v = qkv_d.rearrange("u j (g d) (t n) -> u j t g d n", g=HEADS, t=TB)
            p_v = p_d.rearrange("u (t h) (g n) -> u t g h n", h=HEADS, g=HEADS)
            sp.wait_ge(diag_zero, 1)

            def diag_load(u, s, src_d, src_r):
                for t in range(TB):
                    rows = slice(HD * t, HD * t + HD)
                    sp.dma_start(diag[s][rows, t], src_d(u, t)).then_inc(diag_in[s], 16)
                    sp.dma_start(kv[rows, s], src_r(u, t)).then_inc(diag_in[s], 16)

            with sp.Fori(0, NG // 2) as b:
                for s in range(2):
                    sp.wait_ge(sc_done, 2 * b + s + 1)
                    diag_load(2 * b + s, s,
                              lambda u, t: q_v[bass.ds(u, 1), 2, t].rearrange("a d h n -> (a d) h n"),
                              lambda u, t: q_v[bass.ds(u, 1), 0, t].rearrange("a d h n -> (a d) h n"))
            end_stage(sp, "B")
            with sp.Fori(0, NG // 2) as b:
                for s in range(2):
                    sp.wait_ge(pv_done, 2 * b + s + 1)
                    diag_load(2 * b + s, s,
                              lambda u, t: p_v[bass.ds(u, 1), t].rearrange("a g h n -> (a g) h n"),
                              lambda u, t: v_v[bass.ds(u, 1), 1, t].rearrange("a g d n -> (a g) d n"))
            end_stage(sp, "C")

            load(d_w[:], woT.rearrange("(c p) n -> p c n", p=P))
            load(d_bo[:], bo.partition_broadcast(P))
            od_v = o_d.rearrange("u (c p) n -> u p c n", p=P)
            with sp.Fori(0, NG // 2) as b:
                for s in range(2):
                    sp.wait_ge(op_done, 2 * b + s + 1)
                    sp.dma_start(d_o[:, s], od_v[bass.ds(2 * b + s, 1)].rearrange("a p c n -> (a p) c n"))\
                      .then_inc(o_in[s], 16)
            end_stage(sp, "D")

            def experts(L):
                q = lay[L.name]
                x_t = xs_d[L.name].rearrange("(m a p) c -> m p a c", a=XB, p=P)
                with sp.Fori(0, L.tiles // TD) as b:
                    for s in range(TD // XB):
                        m = b * (TD // XB) + s
                        sp.wait_ge(q["y_done"], XB * m + XB)
                        sp.wait_ge(q["ix_done"], XB * m + XB)
                        sp.dma_start(h_x[s][:], x_t[bass.ds(m, 1)].rearrange("o p a c -> (o p) a c"))\
                          .then_inc(q["x_in"][s], 16)

            def sums(L):
                q = lay[L.name]
                with sp.Fori(0, NG // 2) as b:
                    for s in range(2):
                        g = 2 * b + s
                        sp.wait_ge(q["a_used"], g + 1)
                        for a in range(NA):
                            src = acc_d[L.name][a][0:NTOK, :].rearrange("(g t p) d -> g p t d", g=NG, p=P)
                            sp.dma_start(c_a[:, s, a, :].rearrange("p (t d) -> p t d", t=GT),
                                         src[bass.ds(g, 1)].rearrange("o p t d -> (o p) t d"))\
                              .then_inc(q["a_in"][s], 16)

            load(e_g0[:], gate0T.rearrange("(c p) n -> p c n", p=P))
            end_stage(sp, "E0")
            load(r_gb[:], gate0b.partition_broadcast(P))
            end_stage(sp, "F0")
            load(e_w1[:], sh1T.rearrange("(c p) n -> p c n", p=P))
            load(e_w3[:], sh3T.rearrange("(c p) n -> p c n", p=P))
            load(e_w2[:], sh2T.rearrange("(c p) n -> p c n", p=P))
            load(e_b[:], shb)
            load(e_bs2[:], bs2.partition_broadcast(P))
            for e in range(0, L0.E, 4):
                sp.dma_start(w_all0[:, e * L0.W:(e + 4) * L0.W].rearrange("p (e n) -> p e n", e=4),
                             exp0[e:e + 4].rearrange("e p n -> p e n")).then_inc(w_in, 16)
            end_stage(sp, "S0")
            load(w_bias[:], exp0b.partition_broadcast(P))
            experts(L0)
            end_stage(sp, "H0")
            sums(L0)
            end_stage(sp, "I0")
            load(w_wu[:, 0:KC], wkv_w)
            load(w_wu[:, KC:2 * KC], wkv_u)
            with sp.Fori(0, NG // 2) as b:
                for s in range(2):
                    sp.wait_ge(wk_y, 2 * b + s + 1)
                    sp.dma_start(w_v[:, s], ctx_v[bass.ds(2 * b + s, 1)].rearrange("a p c n -> (a p) c n"))\
                      .then_inc(wk_v[s], 16)
            end_stage(sp, "W")
            load(e_g1[:], gate1T.rearrange("(c p) n -> p c n", p=P))
            end_stage(sp, "E1")
            end_stage(sp, "F1")
            sp.dma_start(x_d, x_res[:].rearrange("p t d -> p (t d)")).then_inc(x_st, 16)

            def weights1(e, n):
                sp.dma_start(w_all1[:, e * L1.W:(e + n) * L1.W].rearrange("p (e n) -> p e n", e=n),
                             exp1[e:e + n].rearrange("e p n -> p e n")).then_inc(w_in, 16)

            for e in range(0, in_front, 8):
                weights1(e, 8)
            sp.wait_ge(x_st, 16)
            end_stage(sp, "S1")
            for e in range(in_front, L1.E, 8):
                weights1(e, 8)
            experts(L1)
            end_stage(sp, "H1")
            sp.dma_start(x_res[:].rearrange("p t d -> p (t d)"), x_d).then_inc(x_st, 16)
            sums(L1)
            o_v = out.rearrange("(g t p) d -> g p t d", g=NG, p=P)
            with sp.Fori(0, NG) as g:
                sp.wait_ge(lay["b"]["a_used"], g + 3)
                sp.dma_start(o_v[bass.ds(g, 1)].rearrange("a p t d -> (a p) t d"),
                             x_res[:, bass.ds(g * GT, GT), :]).then_inc(out_st, 16)
            sp.wait_ge(out_st, 16 * NG)
            end_stage(sp, "I1")

        n_load = {"A": 7, "D": 9, "E0": 10, "F0": 11, "S0": 16, "H0": 17, "W": 19, "E1": 20}
        w_count = {"a": L0.E // 4, "b": L0.E // 4 + L1.E // 8}

        @block.gpsimd
        def _(pool):
            pool.memset(ones[:], 1.0)
            pool.memset(ones_h[:], 1.0)
            pool.memset(void_rows[:], 0.0)
            pool.memset(zeros[:], 0.0)
            pool.memset(meta[:], 0.0)
            for s in range(RS):
                pool.memset(rows_s[s][:], 0.0)
            pool.drain()
            pool.affine_select(out=ident[:], in_=ones[:], pattern=[[-1, P]], compare_op=ALU.is_equal, fill=0.0,
                               base=0, channel_multiplier=1)
            pool.affine_select(out=before[:], in_=ones_h[:], pattern=[[1, P]], compare_op=ALU.is_gt, fill=0.0,
                               base=0, channel_multiplier=-1)
            pool.iota(meta[:].bitcast(I32)[:, :, 0:1], pattern=[[P, NT], [1, 1]], base=0, channel_multiplier=1)
            pool.iota(void_p[:], pattern=[[1, TD]], base=0, channel_multiplier=TD)
            pool.drain().then_inc(const_ready, 4)
            end_stage(pool, "A")
            for s in range(2):
                pool.memset(diag[s][:], 0.0)
            pool.drain().then_inc(diag_zero, 1)
            pool.wait_ge(void_ready, 1)
            for L in (L0, L1):
                v = xs_d[L.name].rearrange("(n p r) c -> n p r c", p=P, r=TD)
                for i in range(L.tiles // TD):
                    pool.dma_start(v[i], void_rows[:]).then_inc(void_st, 16)
                for a in range(NA):
                    v = acc_d[L.name][a][0:NTOK, :].rearrange("(n p r) d -> n p (r d)", p=P, r=TD)
                    for i in range(NTOK // (TD * P)):
                        pool.dma_start(v[i], zeros[:]).then_inc(void_st, 16)
                    pool.dma_start(acc_d[L.name][a][NTOK:, :], zeros[:, 0:D]).then_inc(void_st, 16)
            end_stage(pool, "B")
            end_stage(pool, "C")
            end_stage(pool, "D")

            def iotas(L):
                pool.iota(r_ie[:, 0:L.E], pattern=[[1, L.E]], base=0, channel_multiplier=0,
                          allow_small_or_imprecise_dtypes=True)
                pool.iota(r_ij[:], pattern=[[P, NT]], base=0, channel_multiplier=0,
                          allow_small_or_imprecise_dtypes=True)
                pool.iota(r_it[:, 0:L.tiles], pattern=[[1, L.tiles]], base=0, channel_multiplier=0,
                          allow_small_or_imprecise_dtypes=True)
                pool.memset(r_keep[:, 0:L.E * NT], 1.0)
                pool.drain()
                pool.memset(r_keep[:, 0:L.E * NT].rearrange("p (e t) -> p e t", t=NT)[:, :, 0:1], 0.0)
                pool.drain().then_inc(const_ready, 1)

            def sort(L):
                q = lay[L.name]
                with pool.Fori(0, NT // RS) as b:
                    for s in range(RS):
                        pool.wait_ge(row_ready, (0 if L is L0 else NT) + RS * b + s + 1)
                        pool.sem_inc(spacer, 1)
                        for k in range(L.K):
                            pool.indirect_dma_start(
                                xs_d[L.name], bass.IndirectOffsetOnAxis(ap=idx_s[s][:, k:k + 1], axis=0),
                                rows_s[s][:], None).then_inc(q["row_st"][s], 16)
                for s in range(RS):
                    pool.wait_ge(q["row_st"][s], 16 * L.K * NT // RS)

            def experts(L):
                q = lay[L.name]
                pool.sem_inc(q["ix_done"], TD)

                def body(b, first):
                    for s in range(TD):
                        i = TD * b + s
                        pool.wait_ge(q["y_done"], i + TD + 1)
                        if not (first and s < NA):
                            pool.wait_ge(q["chain"][s % NA], 16 * ((TD // NA) * b + s // NA))
                        pool.sem_inc(spacer, 1)
                        pool.tensor_copy(h_ix[s][:], h_x[s // XB][:, s % XB, D:D + 1].bitcast(I32))\
                            .then_inc(q["ix_done"], 1)
                        pool.wait_ge(q["ix_done"], i + TD + 1)
                        pool.sem_inc(spacer, 1)
                        pool.indirect_dma_start(
                            acc_d[L.name][s % NA], bass.IndirectOffsetOnAxis(ap=h_ix[s][:], axis=0),
                            h_y[s][:], None, compute_op=ALU.add).then_inc(q["chain"][s % NA], 16)

                body(0, True)
                with pool.Fori(1, L.tiles // TD) as b:
                    body(b, False)
                for a in range(NA):
                    pool.wait_ge(q["chain"][a], 16 * L.tiles // NA)

            end_stage(pool, "E0")
            iotas(L0)
            pool.wait_ge(void_st, 16 * (L0.tiles // TD + L1.tiles // TD + 2 * NA * (NTOK // (TD * P) + 1)))
            end_stage(pool, "F0")
            sort(L0)
            end_stage(pool, "S0")
            experts(L0)
            end_stage(pool, "H0")
            end_stage(pool, "I0")
            for c in range(KC):
                pool.memset(w_dec[:, c, :, 0:1], LOW)
            for s in range(2):
                for c in range(KC):
                    pool.memset(w_k[:, s, c, :, 0:1], LOW)
                pool.memset(w_a2[:, s, :, 0:1], 0.0)
                pool.memset(w_e2[:, s, :, 0:1], 0.0)
            pool.memset(w_ev[:, :, 0:1], 0.0)
            pool.drain().then_inc(wk_pad, 1)
            end_stage(pool, "W")
            end_stage(pool, "E1")
            iotas(L1)
            end_stage(pool, "F1")
            sort(L1)
            end_stage(pool, "S1")
            experts(L1)
            end_stage(pool, "H1")
            end_stage(pool, "I1")

        @block.tensor
        def _(pe):
            pe.sem_inc(tr_done, 2)
            pe.sem_inc(proj_done, 12)
            pe.sem_inc(sc_done, 2)
            pe.sem_inc(pv_done, 2)
            pe.sem_inc(op_done, 2)
            pe.sem_inc(rt_done, 2)
            pe.sem_inc(wk_yt, 2)
            for L in (L0, L1):
                for name in ("t_done", "u_done", "ht_done", "d_done"):
                    pe.sem_inc(lay[L.name][name], 2)

            def transposes(n, s):
                pe.wait_ge(xn_ready, n + 1)
                pe.wait_ge(xT_ready, n + 1)
                for j in range(GT):
                    for c in range(KC):
                        m = pe.transpose(ps[:, c, j * P:(j + 1) * P], n_x[:, s, j, c * P:(c + 1) * P], ident[:])
                m.then_inc(tr_done, 1)

            pe.wait_ge(const_ready, 4)
            pe.wait_ge(in_sem, 16 * n_load["A"])
            with pe.Fori(0, NG // 2) as b:
                for s in range(2):
                    g = 2 * b + s
                    transposes(g, s)
                    pe.wait_ge(ctx_in[s], 16 * b + 16)
                    for j in range(3 * KC):
                        if j == 2 * KC:
                            pe.wait_ge(xT_ready, g + 2)
                        pe.wait_ge(proj_out, 6 * g + j + 1)
                        src = a_ctx if j < 2 * KC else a_xT
                        for c in range(KC):
                            m = pe.matmul(ps[:, 2 + j, :],
                                          a_w[:, (j // KC) * KC + c, (j % KC) * P:(j % KC) * P + P],
                                          src[:, s, c, :], start=(c == 0), stop=(c == KC - 1))
                        m.then_inc(proj_done, 1)
            end_stage(pe, "A")

            def blocks(done, freed, before_):
                with pe.Fori(0, NG // 2) as b:
                    for s in range(2):
                        pe.wait_ge(diag_in[s], before_ + 16 * 2 * TB * b + 16 * 2 * TB)
                        pe.wait_ge(freed, 2 * b + s + 1)
                        for n in range(NN):
                            m = pe.matmul(ps[:, 2 * s + n // 32, (n % 32) * HD:(n % 32) * HD + HD],
                                          diag[s][:, :, :, n].rearrange("p t h -> p (t h)"), kv[:, s, :, n],
                                          start=True, stop=True)
                        m.then_inc(done, 1)

            blocks(sc_done, sub_done, 0)
            end_stage(pe, "B")
            blocks(pv_done, o_done, 16 * 2 * TB * NG // 2)
            end_stage(pe, "C")

            pe.wait_ge(in_sem, 16 * n_load["D"])
            with pe.Fori(0, NG // 2) as b:
                for s in range(2):
                    pe.wait_ge(o_in[s], 16 * b + 16)
                    pe.wait_ge(op_used, 2 * b + s + 1)
                    for j in range(GT):
                        for c in range(KC):
                            m = pe.matmul(ps[:, 2 * s + j // 2, (j % 2) * D:(j % 2) * D + D],
                                          d_o[:, s, c, j * P:(j + 1) * P], d_w[:, c, :],
                                          start=(c == 0), stop=(c == KC - 1))
                    m.then_inc(op_done, 1)
            end_stage(pe, "D")

            def scores(L, g, s, gw):
                bank = ps[:, 2:2 + L.E * NT // 512, :].rearrange("p b n -> p (b n)")
                for j in range(GT):
                    for c in range(KC):
                        m = pe.matmul(bank[:, bass.ds((g * GT + j) * L.E, L.E)],
                                      e_xT[:, s, c, j * P:(j + 1) * P], gw[:, c, :],
                                      start=(c == 0), stop=(c == KC - 1))
                m.then_inc(rt_done, 1)

            def router(L, n0, gw):
                with pe.Fori(0, NG // 2) as b:
                    for s in range(2):
                        g = 2 * b + s
                        transposes(n0 + g, s)
                        pe.wait_ge(xT_ready, n0 + g + 2)
                        scores(L, g, s, gw)

            pe.wait_ge(in_sem, 16 * n_load["E0"])
            router(L0, NG, e_g0)
            end_stage(pe, "E0")

            def shared(b, last):
                for s in range(2):
                    g = 2 * b + s
                    pe.wait_ge(xT_ready, 2 * NG + g + 2)
                    for q, w in enumerate(HSP):
                        r = (3 * s + q) % 2
                        pe.wait_ge(sh_h, 3 * g + q + 1)
                        for k, wt in enumerate((e_w1, e_w3)):
                            for c in range(KC):
                                m = pe.matmul(ps[0:w, 3 + 2 * r + k, :], wt[:, c, P * q:P * q + w],
                                              e_xT[:, s, c, :], start=(c == 0), stop=(c == KC - 1))
                        m.then_inc(sh_done, 1)
                    if not (last and s == 1):
                        transposes(2 * NG + g + 1, 1 - s)
                    pe.wait_ge(sh_h, 3 * g + 5)
                    for h in range(2):
                        pe.wait_ge(sh_zu, 2 * g + h + 1)
                        for j in (2 * h, 2 * h + 1):
                            for q, w in enumerate(HSP):
                                m = pe.matmul(ps[:, 7, (j % 2) * D:(j % 2) * D + D],
                                              e_h[0:w, s, q, j * P:(j + 1) * P], e_w2[0:w, q, :],
                                              start=(q == 0), stop=(q == 2))
                        m.then_inc(sh_z, 1)

            def route(L, nth):
                F = L.E * NT
                nb = F // 512
                pe.wait_ge(hot_ready, nth)
                for q in range(nb):
                    pe.matmul(ps[:, q, :], before[:], r_m[:, q * 512:(q + 1) * 512], start=True, stop=True)
                    m = pe.matmul(ps[:, 4 + q, :], ones_h[:], r_m[:, q * 512:(q + 1) * 512], start=True, stop=True)
                m.then_inc(rank_ready, 1)
                pe.wait_ge(cmp_ready, nth)
                pe.matmul(ps[:, 4, 0:L.tiles], ones_h[0:L.E, :], r_cmp[0:L.E, 0:L.tiles],
                          start=True, stop=True).then_inc(map_ready, 1)

            def experts(L, w_all):
                q = lay[L.name]
                h1 = L.H // L.NC

                def expert(i):
                    return pe.value_load(tile_e[0:1, bass.ds(i, 1)], min_val=0, max_val=L.E - 1)

                def tr(i, s, b):
                    if s % XB == 0:
                        pe.wait_ge(q["x_in"][s // XB], 16 * b + 16)
                    pe.wait_ge(q["t_ready"], i + 1)
                    for c in range(KC):
                        m = pe.transpose(ps[:, s % 2, c * P:(c + 1) * P], h_x[s // XB][:, s % XB, c * P:(c + 1) * P],
                                         ident[:])
                    m.then_inc(q["t_done"], 1)

                def up(i, s, e):
                    pe.wait_ge(q["t_ready"], i + 3)
                    pe.wait_ge(q["h_done"], i + 1)
                    for c in range(KC):
                        m = pe.matmul(ps[:, 2 + s % 2, 0:2 * L.H], h_xT[:, s % 2, c, :],
                                      w_all[:, bass.ds(e * L.W + c * 2 * L.H, 2 * L.H)],
                                      start=(c == 0), stop=(c == KC - 1))
                    m.then_inc(q["u_done"], 1)

                def turn(i, s):
                    pe.wait_ge(q["h_done"], i + 3)
                    pe.wait_ge(q["ht_ready"], i + 1)
                    for j in range(L.NC):
                        m = pe.transpose(ps[0:h1, 4 + s % 2, j * P:(j + 1) * P],
                                         h_h[:, s % 2, j * h1:(j + 1) * h1], ident[:])
                    m.then_inc(q["ht_done"], 1)

                def down(i, s, e):
                    pe.wait_ge(q["ht_ready"], i + 3)
                    pe.wait_ge(q["y_done"], i + TD - 1)
                    for j in range(L.NC):
                        w = h1 + (1 if L.bias and j == 0 else 0)
                        m = pe.matmul(ps[:, 6 + s % 2, 0:D], h_hT[0:w, s % 2, j, :],
                                      w_all[0:w, bass.ds(e * L.W + L.up0 + j * D, D)],
                                      start=(j == 0), stop=(j == L.NC - 1))
                    m.then_inc(q["d_done"], 1)

                def body(b, first):
                    known = {}
                    for s in range(TD):
                        j = TD * b + s
                        tr(j, s, b)
                        if not (first and s < 1):
                            known[s - 1] = expert(j - 1)
                            up(j - 1, (s - 1) % TD, known[s - 1])
                        if not (first and s < 2):
                            turn(j - 2, (s - 2) % TD)
                        if not (first and s < 3):
                            e = known[s - 3] if s - 3 in known else expert(j - 3)
                            down(j - 3, (s - 3) % TD, e)

                pe.wait_ge(w_in, 16 * w_count[L.name])
                body(0, True)
                with pe.Fori(1, L.tiles // TD) as b:
                    body(b, False)
                n = L.tiles
                up(n - 1, (n - 1) % TD, expert(n - 1))
                turn(n - 2, (n - 2) % TD)
                down(n - 3, (n - 3) % TD, expert(n - 3))
                turn(n - 1, (n - 1) % TD)
                down(n - 2, (n - 2) % TD, expert(n - 2))
                down(n - 1, (n - 1) % TD, expert(n - 1))

            route(L0, 1)
            end_stage(pe, "F0")
            pe.wait_ge(in_sem, 16 * n_load["S0"])
            transposes(2 * NG, 0)
            with pe.Fori(0, NG // 2 - 1) as b:
                shared(b, False)
            shared(NG // 2 - 1, True)
            end_stage(pe, "S0")
            experts(L0, w_all0)
            end_stage(pe, "H0")
            end_stage(pe, "I0")

            transposes(3 * NG, 0)

            def wkv(b, last):
                for s in range(2):
                    g = 2 * b + s
                    if not (last and s == 1):
                        transposes(3 * NG + g + 1, 1 - s)
                    pe.wait_ge(wk_y, g + 3)
                    pe.wait_ge(wk_yu, g + 1)
                    for j in range(GT):
                        for c in range(KC):
                            m = pe.transpose(ps[:, 2 + 2 * s + j // 2,
                                                (j % 2) * D + c * P:(j % 2) * D + c * P + P],
                                             w_y[:, s, c].rearrange("p b t -> p (b t)")[:, j * P:(j + 1) * P],
                                             ident[:])
                    m.then_inc(wk_yt, 1)

            with pe.Fori(0, NG // 2 - 1) as b:
                wkv(b, False)
            wkv(NG // 2 - 1, True)
            end_stage(pe, "W")

            pe.wait_ge(in_sem, 16 * n_load["E1"])
            router(L1, 4 * NG, e_g1)
            end_stage(pe, "E1")
            route(L1, 2)
            end_stage(pe, "F1")
            end_stage(pe, "S1")
            experts(L1, w_all1)
            end_stage(pe, "H1")
            end_stage(pe, "I1")

        @block.scalar
        def _(act):
            act.sem_inc(xT_ready, 1)
            act.sem_inc(proj_out, 6)
            act.sem_inc(exp_done, 2)
            act.sem_inc(wk_e, 2)
            for s in range(2):
                act.sem_inc(qkv_st[s], 16)
                act.sem_inc(p_st[s], 16)
                act.sem_inc(o_st[s], 16 * TB)
            for L in (L0, L1):
                act.sem_inc(lay[L.name]["t_ready"], 2)
                act.sem_inc(lay[L.name]["ht_ready"], 2)

            def std(nth):
                act.wait_ge(var_ready, nth)
                act.activation(rstd[:], mean_v[:], ACT.Sqrt).then_inc(std_ready, 1)

            act.wait_ge(in_sem, 16 * n_load["A"])
            act.activation(tgate[:], tgate[:], ACT.Tanh).then_inc(tanh_done, 1)
            std(1)
            qkv_v = qkv_d.rearrange("u j (c p) n -> u p (j c) n", p=P)
            with act.Fori(0, NG // 2) as b:
                for s in range(2):
                    g = 2 * b + s
                    act.wait_ge(proj_done, 6 * g + 6)
                    act.wait_ge(tr_done, g + 3)
                    act.copy(a_xT[:, s, 0, :], ps[:, 0, :])
                    act.copy(a_xT[:, s, 1, :], ps[:, 1, :]).then_inc(xT_ready, 1)
                    act.wait_ge(qkv_st[s], 16 * b + 16)
                    for j in range(3 * KC):
                        act.wait_ge(proj_done, 6 * g + j + 13)
                        act.activation(a_out[:, s, j, :], ps[:, 2 + j, :], ACT.Identity,
                                       bias=a_b[:, j:j + 1]).then_inc(proj_out, 1)
                    act.wait_ge(proj_out, 6 * g + 12)
                    act.dma_start(qkv_v[bass.ds(g, 1)].rearrange("a p j n -> (a p) j n"), a_out[:, s])\
                       .then_inc(qkv_st[s], 16)
            for s in range(2):
                act.wait_ge(qkv_st[s], 16 * (NG // 2 + 1))
            end_stage(act, "A")

            with act.Fori(0, NG // 2) as b:
                for s in range(2):
                    g = 2 * b + s
                    act.wait_ge(sub_done, g + 3)
                    act.wait_ge(sum_done, g + 1)
                    act.wait_ge(p_st[s], 16 * b + 16)
                    act.activation(p_un[:, s].rearrange("p g n -> p n g"), s_sub[:, s], ACT.Exp)\
                       .then_inc(exp_done, 1)
                    act.wait_ge(exp_done, g + 3)
                    act.dma_start(p_d[bass.ds(g, 1)].rearrange("a p n -> (a p) n"),
                                  p_un[:, s].rearrange("p g n -> p (g n)")).then_inc(p_st[s], 16)
            for s in range(2):
                act.wait_ge(p_st[s], 16 * (NG // 2 + 1))
            end_stage(act, "B")

            ost_v = o_d.rearrange("u (h d) (t n) -> u t h d n", h=HEADS, t=TB)
            with act.Fori(0, NG // 2) as b:
                for s in range(2):
                    g = 2 * b + s
                    act.wait_ge(o_done, g + 3)
                    for t in range(TB):
                        act.dma_start(ost_v[bass.ds(g, 1), t].rearrange("a h d n -> (a h) d n"),
                                      o_nm[HEADS * t:HEADS * t + HEADS, s]).then_inc(o_st[s], 16)
            for s in range(2):
                act.wait_ge(o_st[s], 16 * TB * (NG // 2 + 1))
            end_stage(act, "C")
            end_stage(act, "D")

            def transposed(n, s, dst):
                act.wait_ge(tr_done, n + 3)
                for c in range(KC):
                    m = act.copy(dst(s, c), ps[:, c, :])
                m.then_inc(xT_ready, 1)

            def e_dst(s, c):
                return e_xT[:, s, c, :]

            def router(n0, r0):
                with act.Fori(0, NG // 2) as b:
                    for s in range(2):
                        act.wait_ge(rt_done, r0 + 2 * b + s + 1)
                        transposed(n0 + 2 * b + s, s, e_dst)

            std(2)
            router(NG, 0)
            end_stage(act, "E0")

            def shared(b, last):
                for s in range(2):
                    g = 2 * b + s
                    for q, w in enumerate(HSP):
                        r = (3 * s + q) % 2
                        act.wait_ge(sh_done, 3 * g + q + 1)
                        act.wait_ge(sh_h, 3 * g + q + 1)
                        act.activation(e_sg[0:w, r, :], ps[0:w, 3 + 2 * r, :], ACT.Silu, bias=e_b[0:w, q:q + 1])\
                           .then_inc(sh_silu, 1)
                    if not (last and s == 1):
                        transposed(2 * NG + g + 1, 1 - s, e_dst)

            def route(L, nth):
                act.wait_ge(sc_ready, nth)
                act.activation(r_p[:, 0:L.E * NT], r_p[:, 0:L.E * NT], ACT.Exp).then_inc(pr_ready, 1)

            def experts(L):
                q = lay[L.name]
                h1 = L.H // L.NC

                def tr(i, s):
                    act.wait_ge(q["t_done"], i + 3)
                    act.wait_ge(q["u_done"], i + 1)
                    act.copy(h_xT[:, s % 2].rearrange("p c n -> p (c n)"), ps[:, s % 2, 0:D])\
                       .then_inc(q["t_ready"], 1)

                def gate(i, s):
                    if L.bias:
                        act.wait_ge(q["b_done"], i + 1)
                    else:
                        act.wait_ge(q["u_done"], i + 3)
                    act.wait_ge(q["h_done"], i + 1)
                    src = h_gu[:, s % 2, 0:L.H] if L.bias else ps[:, 2 + s % 2, 0:L.H]
                    act.activation(h_sg[:, s % 2, 0:L.H], src, ACT.Silu).then_inc(q["s_done"], 1)

                def turn(i, s):
                    act.wait_ge(q["ht_done"], i + 3)
                    act.wait_ge(q["d_done"], i + 1)
                    act.copy(h_hT[0:h1, s % 2, 0:L.NC, :].rearrange("p j n -> p (j n)"),
                             ps[0:h1, 4 + s % 2, 0:L.NC * P]).then_inc(q["ht_ready"], 1)

                def body(b, first):
                    for s in range(TD):
                        j = TD * b + s
                        tr(j, s)
                        if not (first and s < 1):
                            gate(j - 1, (s - 1) % TD)
                        if not (first and s < 2):
                            turn(j - 2, (s - 2) % TD)

                act.preload_act_table(ACT.Silu)
                body(0, True)
                with act.Fori(1, L.tiles // TD) as b:
                    body(b, False)
                n = L.tiles
                gate(n - 1, (n - 1) % TD)
                turn(n - 2, (n - 2) % TD)
                turn(n - 1, (n - 1) % TD)

            route(L0, 1)
            end_stage(act, "F0")
            act.wait_ge(in_sem, 16 * n_load["S0"])
            act.preload_act_table(ACT.Silu)
            transposed(2 * NG, 0, e_dst)
            with act.Fori(0, NG // 2 - 1) as b:
                shared(b, False)
            shared(NG // 2 - 1, True)
            end_stage(act, "S0")
            experts(L0)
            end_stage(act, "H0")
            end_stage(act, "I0")

            std(3)
            act.wait_ge(in_sem, 16 * n_load["W"])
            act.wait_ge(wk_pad, 1)
            with act.Fori(0, NG // 2) as b:
                for s in range(2):
                    g = 2 * b + s
                    act.wait_ge(wk_y, g + 1)
                    act.wait_ge(tr_done, 3 * NG + g + 3)
                    for c in range(KC):
                        m = act.copy(w_k[:, s, c, :, 1:SEQ + 1],
                                     ps[:, c, :].rearrange("p (b t) -> p b t", t=SEQ))
                    m.then_inc(xT_ready, 1)
                    for c in range(KC):
                        act.wait_ge(wk_t, 2 * g + c + 1)
                        act.activation(w_a2[:, c, :, 1:SEQ + 1], w_t[:, c, 0], ACT.Exp, bias=w_wu[:, c:c + 1])
                        act.activation(w_e2[:, c, :, 1:SEQ + 1], w_t[:, c, 1], ACT.Exp)
                        act.activation(w_ex[:, c].rearrange("p j b t -> p (j b t)"),
                                       w_t[:, c, 2:4].rearrange("p j b t -> p (j b t)"), ACT.Exp)\
                           .then_inc(wk_e, 1)
            end_stage(act, "W")

            std(4)
            router(4 * NG, NG)
            end_stage(act, "E1")
            route(L1, 2)
            end_stage(act, "F1")
            end_stage(act, "S1")
            experts(L1)
            end_stage(act, "H1")
            end_stage(act, "I1")

        @block.vector
        def _(dve):
            dve.sem_inc(sub_done, 2)
            dve.sem_inc(sum_done, 2)
            dve.sem_inc(o_done, 2)
            dve.sem_inc(op_used, 2)
            dve.sem_inc(sh_h, 2)
            dve.sem_inc(sh_zu, 1)
            dve.sem_inc(wk_y, 2)
            dve.sem_inc(wk_yu, 2)
            for L in (L0, L1):
                dve.sem_inc(lay[L.name]["h_done"], 2)
                dve.sem_inc(lay[L.name]["y_done"], TD)
                dve.sem_inc(lay[L.name]["a_used"], 2)

            def moments(nth):
                with dve.Fori(0, NT) as t:
                    dve.bn_stats(stats[:, bass.ds(t, 1), :].rearrange("p a k -> p (a k)"),
                                 x_res[:, bass.ds(t, 1), :].rearrange("p a d -> p (a d)"))
                dve.drain()
                dve.tensor_tensor(mean[:], stats[:, :, 1], stats[:, :, 4], ALU.add)
                dve.tensor_tensor(tmp_t[:], stats[:, :, 1], stats[:, :, 4], ALU.subtract)
                dve.tensor_tensor(mean_v[:], stats[:, :, 2], stats[:, :, 5], ALU.add)
                dve.drain()
                dve.tensor_scalar(mean[:], mean[:], 0.5, None, ALU.mult)
                dve.tensor_scalar(mean_v[:], mean_v[:], 1.0 / D, EPS, ALU.mult, ALU.add)
                dve.tensor_tensor(tmp_t[:], tmp_t[:], tmp_t[:], ALU.mult)
                dve.drain()
                dve.scalar_tensor_tensor(mean_v[:], tmp_t[:], 0.25, mean_v[:], ALU.mult, ALU.add)\
                   .then_inc(var_ready, 1)
                dve.wait_ge(std_ready, nth)
                dve.reciprocal(rstd[:], rstd[:])
                dve.drain()

            def normed(dst, t):
                return dve.tensor_scalar(dst, x_res[:, bass.ds(t, 1), :].rearrange("p a d -> p (a d)"),
                                         mean[:, bass.ds(t, 1)], rstd[:, bass.ds(t, 1)],
                                         ALU.subtract, ALU.mult)

            def norm_group(n, g, s):
                dve.wait_ge(tr_done, n + 1)
                dve.sem_inc(spacer, 1)
                for j in range(GT):
                    m = normed(n_x[:, s, j, :], g * GT + j)
                m.then_inc(xn_ready, 1)

            dve.wait_ge(in_sem, 16 * n_load["A"])
            moments(1)
            with dve.Fori(0, NG // 2) as b:
                for s in range(2):
                    norm_group(2 * b + s, 2 * b + s, s)
            end_stage(dve, "A")

            dve.tensor_single_scalar(void_p[:], void_p[:], P - 1, ALU.bitwise_and)
            dve.drain()
            dve.tensor_scalar(void_rows[:].bitcast(I32)[:, :, D], void_p[:], float(NTOK), None, ALU.add)
            dve.drain().then_inc(void_ready, 1)
            with dve.Fori(0, NG // 2) as b:
                for s in range(2):
                    g = 2 * b + s
                    sc = ps[:, 2 * s:2 * s + 2, :].rearrange("p a (n g) -> p (a n) g", g=HEADS)
                    dve.wait_ge(sc_done, g + 3)
                    dve.reduce_max(smax[:], sc, AX)
                    dve.drain()
                    dve.wait_ge(exp_done, g + 1)
                    dve.tensor_tensor(s_sub[:, s], sc, smax[:].unsqueeze(2).to_broadcast([P, NN, HEADS]),
                                      ALU.subtract).then_inc(sub_done, 1)
                    dve.wait_ge(exp_done, g + 3)
                    dve.sem_inc(spacer, 1)
                    dve.reduce_sum(rsum[:, bass.ds(g, 1), :].rearrange("p a n -> p (a n)"),
                                   p_un[:, s].rearrange("p g n -> p n g"), AX).then_inc(sum_done, 1)
            dve.drain()
            dve.reciprocal(rsum[:], rsum[:])
            end_stage(dve, "B")

            with dve.Fori(0, NG // 2) as b:
                for s in range(2):
                    g = 2 * b + s
                    dve.wait_ge(o_st[s], 16 * TB * b + 16 * TB)
                    dve.wait_ge(pv_done, g + 3)
                    dve.sem_inc(spacer, 1)
                    dve.tensor_tensor(o_nm[:, s].rearrange("p d n -> p n d"),
                                      ps[:, 2 * s:2 * s + 2, :].rearrange("p a (n d) -> p (a n) d", d=HD),
                                      rsum[:, bass.ds(g, 1), :].rearrange("p a n -> p (a n)").unsqueeze(2)
                                      .to_broadcast([P, NN, HD]), ALU.mult).then_inc(o_done, 1)
            end_stage(dve, "C")

            def group_of(g, ap):
                return ap[:, bass.ds(g * GT, GT), :].rearrange("p t d -> p (t d)")

            dve.wait_ge(in_sem, 16 * n_load["D"])
            dve.wait_ge(tanh_done, 1)
            dve.tensor_scalar(d_bo[:], d_bo[:], tgate[:, 0:1], None, ALU.mult)
            dve.drain()
            with dve.Fori(0, NG // 2) as b:
                for s in range(2):
                    g = 2 * b + s
                    dve.wait_ge(op_done, g + 3)
                    dve.sem_inc(spacer, 1)
                    dve.scalar_tensor_tensor(group_of(g, x_res), ps[:, 2 * s:2 * s + 2, :]
                                             .rearrange("p a n -> p (a n)"), tgate[:, 0:1],
                                             group_of(g, x_res), ALU.mult, ALU.add).then_inc(op_used, 1)
                    dve.drain()
                    dve.tensor_tensor(x_res[:, bass.ds(g * GT, GT), :], x_res[:, bass.ds(g * GT, GT), :],
                                      d_bo[:].unsqueeze(1).to_broadcast([P, GT, D]), ALU.add)
            end_stage(dve, "D")

            def router(n0):
                with dve.Fori(0, NG // 2) as b:
                    for s in range(2):
                        norm_group(n0 + 2 * b + s, 2 * b + s, s)

            moments(2)
            router(NG)
            end_stage(dve, "E0")

            def stage_row(L, t, s):
                normed(rows_s[s][:, 0:D], t)
                dve.tensor_copy(rows_s[s][:, D:D + META], meta[:, bass.ds(t, 1), :].rearrange("p a k -> p (a k)"))
                dve.tensor_copy(idx_s[s][:, 0:L.K], slot_i[:, bass.ds(t, 1), 0:L.K].rearrange("p a k -> p (a k)"))\
                   .then_inc(row_ready, 1)

            def shared(b, first, last):
                for s in range(2):
                    g = 2 * b + s
                    if not (last and s == 1):
                        norm_group(2 * NG + g + 1, g + 1, 1 - s)
                    for q, w in enumerate(HSP):
                        r = (3 * s + q) % 2
                        dve.wait_ge(sh_silu, 3 * g + q + 1)
                        dve.scalar_tensor_tensor(e_h[0:w, s, q, :], ps[0:w, 4 + 2 * r, :], e_b[0:w, 3 + q:4 + q],
                                                 e_sg[0:w, r, :], ALU.add, ALU.mult).then_inc(sh_h, 1)
                    for j in range(GT):
                        if not (first and s == 0):
                            dve.wait_ge(lay["a"]["row_st"][j], 16 * L0.K * g)
                            dve.sem_inc(spacer, 1)
                        stage_row(L0, g * GT + j, j)
                    for h in range(2):
                        dve.wait_ge(sh_z, 2 * g + h + 1)
                        dve.sem_inc(spacer, 1)
                        dve.tensor_tensor(z[:, bass.ds(g * GT + 2 * h, 2), :],
                                          ps[:, 7, :].rearrange("p (t d) -> p t d", t=2),
                                          e_bs2[:].unsqueeze(1).to_broadcast([P, 2, D]), ALU.add)\
                           .then_inc(sh_zu, 1)

            def route(L, nth):
                E, K, F = L.E, L.K, L.E * NT

                ids, weights = meta[:, :, 1:1 + CHOICES], meta[:, :, 1 + CHOICES:1 + 2 * CHOICES]

                def te(ap):
                    return ap[:, 0:F].rearrange("p (t e) -> p t e", e=E)

                def et(ap):
                    return ap[:, 0:F].rearrange("p (e t) -> p e t", t=NT)

                def over(ap, shape):
                    return ap.unsqueeze(2).to_broadcast(shape)

                TE, ET = [P, NT, E], [P, E, NT]
                raw = ps[:, 2:2 + F // 512, :].rearrange("p b (t e) -> p (b t) e", e=E)
                dve.reduce_max(r_t1[:], raw, AX)
                dve.drain()
                dve.tensor_tensor(te(r_p), raw, over(r_t1[:], TE), ALU.subtract).then_inc(sc_ready, 1)
                dve.wait_ge(pr_ready, nth)
                dve.reduce_sum(r_t1[:], te(r_p), AX)
                dve.drain()
                dve.reciprocal(r_t1[:], r_t1[:])
                dve.drain()
                dve.tensor_tensor(te(r_p), te(r_p), over(r_t1[:], TE), ALU.mult)
                dve.drain()
                chosen_by = te(r_p)
                if L is L0:
                    dve.wait_ge(in_sem, 16 * n_load["F0"])
                    dve.tensor_tensor(te(r_b), te(r_p), r_gb[:].unsqueeze(1).to_broadcast(TE), ALU.add)
                    dve.drain()
                    chosen_by = te(r_b)
                for t in range(NT):
                    dve.max(r_val[:, t, :], chosen_by[:, t, :])
                dve.drain()
                for t in range(NT):
                    dve.max_index(r_idx[:, t, :], r_val[:, t, :], chosen_by[:, t, :])
                dve.drain()
                dve.tensor_copy(ids, r_idx[:])
                dve.wait_ge(const_ready, 4 + nth)
                dve.drain()

                def hot(k):
                    dve.tensor_tensor(te(r_w), r_ie[:, 0:E].unsqueeze(1).to_broadcast(TE),
                                      over(ids[:, :, k], TE), ALU.is_equal)
                    dve.drain()

                if L is L0:
                    dve.memset(r_s[:, 0:F], 0.0)
                    for k in range(K):
                        hot(k)
                        dve.tensor_tensor(te(r_s), te(r_s), te(r_w), ALU.add)
                        dve.tensor_tensor(te(r_c), te(r_p), te(r_w), ALU.mult)
                        dve.drain()
                        dve.reduce_sum(weights[:, :, k], te(r_c), AX)
                    dve.tensor_copy(r_m[:, 0:F], r_s[:, 0:F]).then_inc(hot_ready, 1)
                else:
                    for t in range(NT):
                        dve.match_replace(te(r_w)[:, t, :], r_val[:, t, :], te(r_p)[:, t, :], -1.0)
                    dve.drain()
                    dve.tensor_scalar(r_m[:, 0:F], r_w[:, 0:F], 0.0, None, ALU.is_lt).then_inc(hot_ready, 1)
                    dve.reduce_sum(r_t1[:], r_val[:], AX)
                    dve.drain()
                    dve.tensor_scalar(tmp_t[:], r_t1[:], 0.0, None, ALU.is_equal)
                    dve.drain()
                    dve.tensor_tensor(r_t1[:], r_t1[:], tmp_t[:], ALU.add)
                    dve.drain()
                    dve.reciprocal(r_t1[:], r_t1[:])
                    dve.drain()
                    dve.tensor_tensor(weights, r_val[:], over(r_t1[:], [P, NT, CHOICES]), ALU.mult)
                dve.wait_ge(rank_ready, nth)
                nb = F // 512
                dve.tensor_copy(et(r_c).rearrange("p e t -> p t e"),
                                ps[:, 4:4 + nb, :].rearrange("p b (t e) -> p (b t) e", e=E))
                dve.drain()
                dve.tensor_tensor_scan(r_i[:, 0:F], r_keep[:, 0:F], r_c[:, 0:F], 0.0, ALU.mult, ALU.add)
                dve.drain()
                dve.tensor_tensor(et(r_w), over(et(r_i)[:, :, NT - 1], ET), r_ij[:].unsqueeze(1).to_broadcast(ET),
                                  ALU.is_gt)
                dve.drain()
                dve.reduce_sum(r_te[:, 0:E], et(r_w), AX)
                dve.memset(r_dg[:, 0:E], 1.0)
                dve.drain()
                dve.tensor_tensor_scan(r_cum[:, 0:E], r_dg[:, 0:E], r_te[:, 0:E], 0.0, ALU.mult, ALU.add)
                dve.drain()
                dve.tensor_tensor(r_dg[:, 0:E], r_cum[:, 0:E], ident[:, 0:E], ALU.mult)
                dve.tensor_tensor(r_st[:, 0:E], r_cum[:, 0:E], r_te[:, 0:E], ALU.subtract)
                dve.drain()
                dve.reduce_sum(r_end[:], r_dg[:, 0:E], AX)
                dve.tensor_scalar(r_st[:, 0:E], r_st[:, 0:E], float(P), None, ALU.mult)
                dve.tensor_tensor(r_i[:, 0:F], r_i[:, 0:F], r_c[:, 0:F], ALU.subtract)
                dve.drain()
                dve.tensor_scalar(r_cmp[:, 0:L.tiles], r_it[:, 0:L.tiles], r_end[:, 0:1], None, ALU.is_ge)\
                   .then_inc(cmp_ready, 1)
                dve.tensor_tensor(et(r_i), et(r_i), over(r_st[:, 0:E], ET), ALU.add)
                dve.drain()
                dve.tensor_tensor(te(r_s), ps[:, 0:nb, :].rearrange("p b (t e) -> p (b t) e", e=E),
                                  et(r_i).rearrange("p e t -> p t e"), ALU.add)
                dve.drain()
                for k in range(K):
                    hot(k)
                    dve.tensor_tensor(te(r_c), te(r_s), te(r_w), ALU.mult)
                    dve.drain()
                    dve.reduce_sum(r_sl[:, :, k], te(r_c), AX)
                dve.drain()
                dve.tensor_copy(slot_i[:, :, 0:K], r_sl[:, :, 0:K])
                dve.wait_ge(map_ready, nth)
                dve.tensor_scalar(tile_e[:, 0:L.tiles], ps[0:1, 4, 0:L.tiles], float(E - 1), None, ALU.min)
                dve.tensor_scalar(tile_ef[:, 0:L.tiles], ps[:, 4, 0:L.tiles], float(E - 1), None, ALU.min)

            def experts(L):
                q = lay[L.name]

                def hidden(i, s):
                    if L.bias:
                        e = dve.value_load(tile_e[0:1, bass.ds(i, 1)], min_val=0, max_val=L.E - 1)
                        dve.wait_ge(q["u_done"], i + 3)
                        dve.tensor_tensor(h_gu[:, s % 2, :], ps[:, 2 + s % 2, 0:2 * L.H],
                                          w_bias[:, bass.ds(e * 2 * L.H, 2 * L.H)], ALU.add).then_inc(q["b_done"], 1)
                        dve.drain()
                    src = h_gu[:, s % 2, L.H:2 * L.H] if L.bias else ps[:, 2 + s % 2, L.H:2 * L.H]
                    dve.wait_ge(q["ht_done"], i + 1)
                    dve.wait_ge(q["s_done"], i + 1)
                    dve.tensor_tensor(h_h[:, s % 2, 0:L.H], src, h_sg[:, s % 2, 0:L.H], ALU.mult)\
                       .then_inc(q["h_done"], 1)

                def result(i, s, b):
                    row = h_x[s // XB][:, s % XB, :]
                    if b is not None:
                        dve.wait_ge(q["chain"][s % NA], 16 * ((TD // NA) * (b - 1) + s // NA + 1))
                        dve.sem_inc(spacer, 1)
                    dve.scalar_tensor_tensor(h_w[:, s, :], row[:, D + 1:D + 1 + CHOICES], tile_ef[:, bass.ds(i, 1)],
                                             row[:, D + 1 + CHOICES:D + META], ALU.is_equal, ALU.mult,
                                             accum_out=h_wc[:, s:s + 1])
                    dve.drain()
                    dve.wait_ge(q["d_done"], i + 3)
                    dve.tensor_scalar(h_y[s][:], ps[:, 6 + s % 2, 0:D], h_wc[:, s:s + 1], None, ALU.mult)\
                       .then_inc(q["y_done"], 1)

                def body(b, first):
                    for s in range(TD):
                        j = TD * b + s
                        if not (first and s < 1):
                            hidden(j - 1, (s - 1) % TD)
                        if not (first and s < 3):
                            result(j - 3, (s - 3) % TD, None if first or (second and s < 3) else
                                   b if s >= 3 else b - 1)

                second = False
                body(0, True)
                second = True
                body(1, False)
                second = False
                with dve.Fori(2, L.tiles // TD) as b:
                    body(b, False)
                n = L.tiles
                result(n - 3, (n - 3) % TD, n // TD - 1)
                hidden(n - 1, (n - 1) % TD)
                result(n - 2, (n - 2) % TD, n // TD - 1)
                result(n - 1, (n - 1) % TD, n // TD - 1)

            def sums(L, gate):
                q = lay[L.name]
                with dve.Fori(0, NG // 2) as b:
                    for s in range(2):
                        g = 2 * b + s
                        dve.wait_ge(q["a_in"][s], 16 * NA * b + 16 * NA)
                        acc = c_a[:, s, 0, :]
                        dve.sem_inc(spacer, 1)
                        for a in range(1, NA):
                            dve.tensor_tensor(acc, acc, c_a[:, s, a, :], ALU.add)
                            dve.drain()
                        if L is L0:
                            dve.tensor_tensor(acc, acc, group_of(g, z), ALU.add)
                            dve.drain()
                        dve.scalar_tensor_tensor(group_of(g, x_res), acc, gate, group_of(g, x_res),
                                                 ALU.mult, ALU.add).then_inc(q["a_used"], 1)

            route(L0, 1)
            end_stage(dve, "F0")
            dve.wait_ge(in_sem, 16 * n_load["S0"])
            norm_group(2 * NG, 0, 0)
            shared(0, True, False)
            with dve.Fori(1, NG // 2 - 1) as b:
                shared(b, False, False)
            shared(NG // 2 - 1, False, True)
            end_stage(dve, "S0")
            dve.memset(h_hT[:], 1.0)
            dve.wait_ge(in_sem, 16 * n_load["H0"])
            dve.drain()
            experts(L0)
            end_stage(dve, "H0")
            sums(L0, tgate[:, 2:3])
            end_stage(dve, "I0")

            moments(3)
            dve.wait_ge(in_sem, 16 * n_load["W"])
            dve.wait_ge(wk_pad, 1)
            for c in range(KC):
                dve.memset(w_d[:], 1.0)
                dve.drain()
                dve.tensor_scalar(w_dec[:, c, :, 1:SEQ + 1], w_d[:], w_wu[:, c:c + 1], None, ALU.mult)
                dve.drain()

            def flat(ap):
                return ap.rearrange("p b t -> p (b t)")

            def exponents(g, s, c):
                key = w_k[:, s, c, :, 1:SEQ + 1]
                o_prev, o_now = w_o[:, :, 0:SEQ], w_o[:, :, 1:SEQ + 1]
                u = w_wu[:, KC + c:KC + c + 1]
                dve.drain()
                if c == 0:
                    dve.wait_ge(xT_ready, 3 * NG + g + 2)
                dve.tensor_tensor_scan(flat(w_o[:]), flat(w_dec[:, c]), flat(w_k[:, s, c]), 0.0, ALU.add, ALU.max)
                dve.drain()
                dve.scalar_tensor_tensor(w_n[:], key, u, o_prev, ALU.add, ALU.max)
                dve.wait_ge(wk_e, 2 * g + c + 1)
                dve.tensor_tensor(w_t[:, c, 0], o_prev, o_now, ALU.subtract)
                dve.tensor_tensor(w_t[:, c, 1], key, o_now, ALU.subtract)
                dve.drain()
                dve.tensor_tensor(w_t[:, c, 2], o_prev, w_n[:], ALU.subtract)
                dve.scalar_tensor_tensor(w_t[:, c, 3], key, u, w_n[:], ALU.add, ALU.subtract).then_inc(wk_t, 1)

            def over_time(g, s, c, bb):
                val = w_v[:, s, c, :].rearrange("p (b t) -> p b t", t=SEQ)
                dve.drain()
                dve.wait_ge(wk_e, 2 * g + c + 3)
                if c == 0:
                    dve.wait_ge(wk_v[s], 16 * bb + 16)
                dve.tensor_tensor(w_ev[:, :, 1:SEQ + 1], w_e2[:, c, :, 1:SEQ + 1], val, ALU.mult)
                dve.tensor_tensor(w_m[:], w_ex[:, c, 1], val, ALU.mult)
                dve.tensor_tensor_scan(flat(w_q[:]), flat(w_a2[:, c]), flat(w_e2[:, c]), 0.0, ALU.mult, ALU.add)
                dve.drain()
                dve.tensor_tensor_scan(flat(w_p[:]), flat(w_a2[:, c]), flat(w_ev[:]), 0.0, ALU.mult, ALU.add)
                dve.tensor_tensor(w_d[:], w_ex[:, c, 0], w_q[:, :, 0:SEQ], ALU.mult)
                dve.drain()
                dve.tensor_tensor(w_n[:], w_ex[:, c, 0], w_p[:, :, 0:SEQ], ALU.mult)
                dve.tensor_tensor(w_d[:], w_d[:], w_ex[:, c, 1], ALU.add)
                dve.drain()
                dve.tensor_tensor(w_n[:], w_n[:], w_m[:], ALU.add)
                dve.reciprocal(w_d[:], w_d[:])
                dve.drain()
                if c == 0:
                    dve.wait_ge(wk_yt, g + 1)
                m = dve.tensor_tensor(w_y[:, s, c], w_n[:], w_d[:], ALU.mult)
                if c == KC - 1:
                    m.then_inc(wk_y, 1)

            def residual(g, s):
                dve.wait_ge(wk_yt, g + 3)
                dve.sem_inc(spacer, 1)
                dve.scalar_tensor_tensor(group_of(g, x_res), ps[:, 2 + 2 * s:4 + 2 * s, :]
                                         .rearrange("p a n -> p (a n)"), tgate[:, 1:2],
                                         group_of(g, x_res), ALU.mult, ALU.add).then_inc(wk_yu, 1)

            def wkv(b, first, last):
                for s in range(2):
                    g = 2 * b + s
                    if not (last and s == 1):
                        norm_group(3 * NG + g + 1, g + 1, 1 - s)
                    exponents(g, s, 0)
                    prev = not (first and s == 0)
                    if prev:
                        over_time(g - 1, 1 - s, 1, None)
                    exponents(g, s, 1)
                    over_time(g, s, 0, b)
                    if prev:
                        residual(g - 1, 1 - s)

            norm_group(3 * NG, 0, 0)
            wkv(0, True, False)
            with dve.Fori(1, NG // 2 - 1) as b:
                wkv(b, False, False)
            wkv(NG // 2 - 1, False, True)
            over_time(NG - 1, 1, 1, None)
            residual(NG - 1, 1)
            end_stage(dve, "W")

            moments(4)
            router(4 * NG)
            end_stage(dve, "E1")
            route(L1, 2)
            end_stage(dve, "F1")
            for s in range(RS):
                stage_row(L1, s, s)
            with dve.Fori(1, NT // RS) as b:
                for s in range(RS):
                    dve.wait_ge(lay["b"]["row_st"][s], 16 * L1.K * b)
                    dve.sem_inc(spacer, 1)
                    stage_row(L1, RS * b + s, s)
            end_stage(dve, "S1")
            experts(L1)
            end_stage(dve, "H1")
            dve.wait_ge(x_st, 32)
            sums(L1, tgate[:, 3:4])
            end_stage(dve, "I1")


def kernel(**inputs):
    import numpy as np
    import concourse.bacc as bacc
    from concourse.bass_utils import run_bass_kernel_spmd

    a = {k: np.asarray(v) for k, v in inputs.items()}

    def cols(v, n=1):
        v = np.pad(v, (0, -len(v) % P))
        return np.ascontiguousarray(v.reshape(-1, P).T)

    f = np.float32
    wqkvT = np.concatenate([a["L0_xattn_W" + n].T for n in "kvq"])
    bqkv = np.concatenate([cols(a["L0_xattn_b" + n]) for n in "kvq"], axis=1)
    exp0 = np.zeros((L0.E, P, L0.W), f)
    w13 = np.concatenate([a["L0_ffn_w1"].transpose(0, 2, 1), a["L0_ffn_w3"].transpose(0, 2, 1)], axis=2)
    exp0[:, :, 0:L0.up0] = w13.reshape(L0.E, KC, P, 2 * L0.H).transpose(0, 2, 1, 3).reshape(L0.E, P, L0.up0)
    h1 = L0.H // L0.NC
    w2 = a["L0_ffn_w2"].transpose(0, 2, 1)
    for j in range(L0.NC):
        exp0[:, 0:h1, L0.up0 + j * D:L0.up0 + (j + 1) * D] = w2[:, j * h1:(j + 1) * h1]
    exp0[:, h1, L0.up0:L0.up0 + D] = a["L0_ffn_b2"]
    exp0b = np.concatenate([a["L0_ffn_b1"], a["L0_ffn_b3"]], axis=1).reshape(-1)
    exp1 = np.zeros((L1.E, P, L1.W), f)
    gu = a["L1_ffn_gate_up_weights"].reshape(L1.E, KC, P, 2 * L1.H).transpose(0, 2, 1, 3)
    exp1[:, :, 0:L1.up0] = gu.reshape(L1.E, P, L1.up0)
    exp1[:, 0:L1.H, L1.up0:L1.up0 + D] = a["L1_ffn_down_weights"]
    feeds = dict(
        x=a["x"].reshape(NTOK, D),
        ctxT=np.ascontiguousarray(a["ctx_2048"].reshape(NTOK, D).T),
        gates=np.concatenate([a["g_xattn"], a["g_ffn"]]),
        wqkvT=wqkvT, bqkv=bqkv, woT=a["L0_xattn_Wo"].T, bo=a["L0_xattn_bo"],
        gate0T=a["L0_ffn_gate_w"].T, gate0b=a["L0_ffn_gate_b"], exp0=exp0, exp0b=exp0b,
        sh1T=a["L0_ffn_ws1"].T, sh3T=a["L0_ffn_ws3"].T,
        sh2T=np.pad(a["L0_ffn_ws2"].T, ((0, 3 * P - HS), (0, 0))),
        shb=np.concatenate([cols(a["L0_ffn_bs1"]), cols(a["L0_ffn_bs3"])], axis=1), bs2=a["L0_ffn_bs2"],
        wkv_w=cols(a["L1_xattn_w"]), wkv_u=cols(a["L1_xattn_u"]),
        gate1T=a["L1_ffn_gate_weight"].T, exp1=exp1,
    )
    nc = bacc.Bacc("TRN2", target_bir_lowering=False, num_devices=1)
    arrays, args = {}, []
    for name, v in feeds.items():
        v = np.ascontiguousarray(v)
        arrays[f"in_{name}"] = v
        args.append(nc.dram_tensor(f"in_{name}", v.shape, mybir.dt.from_np(v.dtype), kind="ExternalInput").ap())
    args.append(nc.dram_tensor("out_x", (NTOK, D), F32, kind="ExternalOutput").ap())
    flamingo(nc, *args)
    r = run_bass_kernel_spmd(nc, [arrays], core_ids=[0])
    return r.results[0]["out_x"].reshape(64, 64, D)
```

```python
from contextlib import ExitStack

import concourse.bass as bass
from concourse import mybir

F32 = mybir.dt.float32
BF16 = mybir.dt.bfloat16
I32 = mybir.dt.int32
U32 = mybir.dt.uint32
ALU = mybir.AluOpType
ACT = mybir.ActivationFunctionType
AX = mybir.AxisListType.X

P = 128
D = 256
KC = D // P
NTOK = 64 * 64
NT = NTOK // P
GT = 4
GS = GT * P
NG = NTOK // GS
HEADS = 16
HD = D // HEADS
TB = P // HD
NN = GS // TB
BR = P // HEADS
BC = NN // BR
SEQ = 64
GB = GS // SEQ
EPS = 1e-5
LOW = -1e38
HS = 352
HSP = [128, 128, 96]
CHOICES = 8
TD = 8
LEAD = TD
WB = 8
TQ = 4
NA = 2
META = 2 * CHOICES
RW = D + META
RS = 4
OR = 4
ZT = 4


class Layer:

    def __init__(self, name, experts, top, hidden, chunks, bias):
        self.name, self.E, self.K, self.H, self.NC, self.bias = name, experts, top, hidden, chunks, bias
        self.tiles = -(-(NTOK * top // P + experts - 1) // TD) * TD
        self.up0 = 2 * KC * hidden
        self.W = self.up0 + chunks * D


L0 = Layer("a", 16, 6, 176, 2, True)
L1 = Layer("b", 64, 8, 96, 1, False)
MT = max(L0.tiles, L1.tiles)


def flamingo(nc, x, ctxT, gates, wqkvT, bqkv, woT, bo, gate0T, gate0b, exp0, exp0b, sh1T, sh3T, sh2T, shb, bs2,
             wkv_w, wkv_u, gate1T, exp1, out):
    qkv_d = nc.dram_tensor("qkv_d", (NG, 3, D, GS), F32).ap()
    o_d = nc.dram_tensor("o_d", (NG, D, GS), F32).ap()
    x_d = nc.dram_tensor("x_d", (P, NT * D), F32).ap()
    xr_d = nc.dram_tensor("xr_d", (NTOK + P, RW), F32).ap()
    acc_d = {L.name: [nc.dram_tensor(f"acc_{L.name}{a}", (NTOK + P, D), F32).ap() for a in range(NA)]
             for L in (L0, L1)}

    ctx = ExitStack()
    with ctx:
        names = {}

        def sb_in(stack):
            def sb(name, shape, dt=F32):
                names[name] = names.get(name, 0) + 1
                return stack.enter_context(nc.sbuf_tensor(f"{name}_{names[name]}", shape, dt))
            return sb

        def sem(name):
            return ctx.enter_context(nc.semaphore(name))

        sb = sb_in(ctx)
        big = NT * D * 4
        x_res = nc.alloc_sbuf_tensor_at("x_res", [P, NT, D], F32, offset=nc.sbuf_top - big)
        z_at = nc.sbuf_top - 2 * big
        z = nc.alloc_sbuf_tensor_at("z", [P, NT, D], F32, offset=z_at)
        zeros = nc.alloc_sbuf_tensor_at("zeros", [P, ZT * D], F32, offset=nc.sbuf_top - big - ZT * D * 4)
        ident = sb("ident", [P, P])
        ones = sb("ones", [P, P])
        ones_h = sb("ones_h", [P, P], BF16)
        before = sb("before", [P, P], BF16)
        tgate = sb("tgate", [P, 4])
        stats = sb("stats", [P, NT, 6])
        mean = sb("mean", [P, NT])
        rstd = sb("rstd", [P, NT])
        mean_v = sb("mean_v", [P, NT])
        tmp_t = sb("tmp_t", [P, NT])
        row_in = sb("row_in", [P, NT, CHOICES])
        row_of = sb("row_of", [P, NT, CHOICES])
        tile_row = sb("tile_row", [P, MT])
        lanes = sb("lanes", [P, P])
        token1 = sb("token1", [P, NT])
        void1 = sb("void1", [P, 1])
        order = sb("order", [P, MT], I32)
        meta = sb("meta", [P, NT, META])
        tile_e = sb("tile_e", [1, MT], I32)
        tile_ef = sb("tile_ef", [P, MT])
        rows_s = [sb(f"rows_s{s}", [P, RW]) for s in range(RS)]
        ps = ctx.enter_context(nc.psum_tensor("ps", [P, 8, 512], F32))

        with ExitStack() as st:
            s_ = sb_in(st)
            n_x = s_("n_x", [P, 2, GT, D])
            a_w = s_("a_w", [P, 3 * KC, D])
            a_b = s_("a_b", [P, 3 * KC])
            a_ctx = s_("a_ctx", [P, 2, KC, GS])
            a_xT = s_("a_xT", [P, 2, KC, GS])
            a_out = s_("a_out", [P, 2, 3 * KC, GS])
            a_end = nc.sbuf_base
        with ExitStack() as st:
            s_ = sb_in(st)
            q_pad = s_("q_pad", [P, 2, 3 * HEADS, NN])
            probs = s_("probs", [P, 2, BC * P])
            pT_pad = s_("pT_pad", [P, NN, 3 * HEADS])
            o_nm = s_("o_nm", [P, BC * P])
            oT = s_("oT", [P, 2, HEADS, NN])
            smax = s_("smax", [P, BC * TB])
            rsum = s_("rsum", [P, 2, BC * TB])
            assert nc.sbuf_base >= a_end
            k_diag = [s_(f"k_diag{s}", [P, TB, HEADS, NN]) for s in range(2)]
            v_diag = s_("v_diag", [P, TB, HD, NN])
            assert nc.sbuf_base <= nc.sbuf_top - big - ZT * D * 4
        with ExitStack() as st:
            s_ = sb_in(st)
            d_w = s_("d_w", [P, KC, D])
            d_bo = s_("d_bo", [P, D])
            d_o = s_("d_o", [P, 2, KC, GS])
        with ExitStack() as st:
            s_ = sb_in(st)
            s_("n_x", [P, 2, GT, D])
            e_xT = s_("e_xT", [P, 2, KC, GS])
            o_in_row = s_("o_in_row", [P, OR, P])
            o_of_tile = s_("o_of_tile", [P, OR, MT])
            order_end = nc.sbuf_base
            e_g0 = s_("e_g0", [P, KC, L0.E])
            e_g1 = s_("e_g1", [P, KC, L1.E])
            e_w1 = s_("e_w1", [P, KC, HS])
            e_w3 = s_("e_w3", [P, KC, HS])
            e_w2 = s_("e_w2", [P, 3, D])
            e_b = s_("e_b", [P, 6])
            e_bs2 = s_("e_bs2", [P, D])
            e_sg = s_("e_sg", [P, 2, GS])
            e_h = s_("e_h", [P, 2, 3, GS])
            s0_end = nc.sbuf_base
        with ExitStack() as st:
            s_ = sb_in(st)
            F = L1.E * NT
            r_p = s_("r_p", [P, F])
            r_b = s_("r_b", [P, F])
            r_w = s_("r_w", [P, F])
            r_c = s_("r_c", [P, F])
            r_i = s_("r_i", [P, F])
            r_s = s_("r_s", [P, F])
            r_keep = s_("r_keep", [P, F])
            r_m = s_("r_m", [P, F], BF16)
            r_val = s_("r_val", [P, NT, CHOICES])
            r_idx = s_("r_idx", [P, NT, CHOICES], U32)
            r_si = s_("r_si", [P, NT, CHOICES], I32)
            r_sl = s_("r_sl", [P, NT, CHOICES])
            r_gb = s_("r_gb", [P, L0.E])
            r_ie = s_("r_ie", [P, L1.E])
            r_ij = s_("r_ij", [P, NT])
            r_te = s_("r_te", [P, L1.E])
            r_cum = s_("r_cum", [P, L1.E])
            r_st = s_("r_st", [P, L1.E])
            r_dg = s_("r_dg", [P, L1.E])
            r_end = s_("r_end", [P, 1])
            r_cmp = s_("r_cmp", [P, MT], BF16)
            r_t1 = s_("r_t1", [P, NT])
        with ExitStack() as st:
            s_ = sb_in(st)
            h_x = [s_(f"h_x{s}", [P, RW]) for s in range(TD)]
            h_y = [s_(f"h_y{s}", [P, D]) for s in range(TD)]
            h_ix = s_("h_ix", [P, 2 * TD], I32)
            h_w = s_("h_w", [P, TD, CHOICES])
            h_wc = s_("h_wc", [P, TD])
            h_xT = s_("h_xT", [P, 2, KC, P])
            h_sg = s_("h_sg", [P, 2, L0.H])
            h_h = s_("h_h", [P, 2, L0.H])
            h_hT = s_("h_hT", [P, 2, L0.NC, P])
            with ExitStack() as st1:
                s1 = sb_in(st1)
                assert nc.sbuf_base >= order_end
                w_all1 = s1("w_all1", [P, L1.E * L1.W])
                in_front = (nc.sbuf_top - big - (nc.sbuf_base - L1.E * L1.W * 4)) // (L1.W * 4 * WB) * WB
            h_gu = s_("h_gu", [P, 2, 2 * L0.H])
            w_bias = s_("w_bias", [P, L0.E * 2 * L0.H])
            if nc.sbuf_base < s0_end:
                s_("gap", [P, (s0_end - nc.sbuf_base) // 4])
            w_all0 = s_("w_all0", [P, L0.E * L0.W])
            assert nc.sbuf_base <= z_at
        with ExitStack() as st:
            s_ = sb_in(st)
            c_a = s_("c_a", [P, 2, NA, GT * D])
        with ExitStack() as st:
            s_ = sb_in(st)
            s_("n_x", [P, 2, GT, D])
            w_wu = s_("w_wu", [P, 2 * KC])
            w_dec = s_("w_dec", [P, KC, GB, SEQ + 1])
            w_k = s_("w_k", [P, 2, KC, GB, SEQ + 1])
            w_v = s_("w_v", [P, 2, KC, GS])
            w_o = s_("w_o", [P, GB, SEQ + 1])
            w_t = s_("w_t", [P, 2, 4, GB, SEQ])
            w_a2 = s_("w_a2", [P, 2, GB, SEQ + 1])
            w_e2 = s_("w_e2", [P, 2, GB, SEQ + 1])
            w_ex = s_("w_ex", [P, 2, 2, GB, SEQ])
            w_ev = s_("w_ev", [P, GB, SEQ + 1])
            w_max = s_("w_max", [P, GB, SEQ])
            w_p = s_("w_p", [P, KC, GB, SEQ + 1])
            w_q = s_("w_q", [P, KC, GB, SEQ + 1])
            w_n = s_("w_n", [P, KC, GB, SEQ])
            w_d = s_("w_d", [P, KC, GB, SEQ])
            w_m = s_("w_m", [P, GB, SEQ])
            w_y = s_("w_y", [P, 2, KC, GB, SEQ])

        stage_done = sem("stage_done")
        spacer = sem("spacer")
        in_sem = sem("in_sem")
        in_count = [0]
        x_in = [sem(f"x_in{q}") for q in range(4)]
        const_ready = sem("const_ready")
        tanh_done = sem("tanh_done")
        var_ready = sem("var_ready")
        std_ready = sem("std_ready")
        xn_ready = sem("xn_ready")
        tr_done = sem("tr_done")
        xT_ready = sem("xT_ready")
        ctx_in = [sem(f"ctx_in{s}") for s in range(2)]
        proj_done = sem("proj_done")
        proj_out = sem("proj_out")
        qkv_st = [sem(f"qkv_st{s}") for s in range(2)]
        pad_zero = sem("pad_zero")
        kq_in = [sem(f"kq_in{s}") for s in range(2)]
        v_in = sem("v_in")
        sc_done = sem("sc_done")
        sub_done = sem("sub_done")
        exp_done = sem("exp_done")
        pt_done = sem("pt_done")
        pt_ready = sem("pt_ready")
        pv_done = sem("pv_done")
        o_done = sem("o_done")
        ot_done = sem("ot_done")
        ot_ready = sem("ot_ready")
        o_st = [sem(f"o_st{s}") for s in range(2)]
        o_in = [sem(f"o_in{s}") for s in range(2)]
        op_done = sem("op_done")
        op_used = sem("op_used")
        sh_done = sem("sh_done")
        sh_silu = sem("sh_silu")
        sh_h = sem("sh_h")
        sh_z = sem("sh_z")
        sh_zu = sem("sh_zu")
        rt_done = sem("rt_done")
        sc_ready = sem("sc_ready")
        pr_ready = sem("pr_ready")
        hot_ready = sem("hot_ready")
        rank_ready = sem("rank_ready")
        cmp_ready = sem("cmp_ready")
        map_ready = sem("map_ready")
        row_ready = sem("row_ready")
        pair_ready = sem("pair_ready")
        pair_done = sem("pair_done")
        order_ready = sem("order_ready")
        lay = {}
        for L in (L0, L1):
            n = L.name
            lay[n] = dict(
                row_st=[sem(f"row_st{n}{s}") for s in range(RS)],
                x_in=[sem(f"x_in{n}{s}") for s in range(TD)],
                t_done=sem(f"t_done{n}"),
                t_ready=sem(f"t_ready{n}"),
                u_done=sem(f"u_done{n}"),
                b_done=sem(f"b_done{n}"),
                s_done=sem(f"s_done{n}"),
                h_done=sem(f"h_done{n}"),
                ht_done=sem(f"ht_done{n}"),
                ht_ready=sem(f"ht_ready{n}"),
                d_done=sem(f"d_done{n}"),
                y_done=sem(f"y_done{n}"),
                ix_done=sem(f"ix_done{n}"),
                chain=[sem(f"chain{n}{a}") for a in range(NA)],
                a_in=[sem(f"a_in{n}{s}") for s in range(2)],
                a_used=sem(f"a_used{n}"),
            )
        wk_y = sem("wk_y")
        wk_t = sem("wk_t")
        wk_e = sem("wk_e")
        wk_yt = sem("wk_yt")
        wk_yu = sem("wk_yu")
        wk_s = sem("wk_s")
        wk_nd = sem("wk_nd")
        wk_v = [sem(f"wk_v{s}") for s in range(2)]
        wk_pad = sem("wk_pad")
        w_in = sem("w_in")
        x_st = sem("x_st")
        out_st = sem("out_st")
        zero_st = sem("zero_st")

        block = ctx.enter_context(nc.Block())

        stages = ["A", "B", "D", "E0", "F0", "S0", "H0", "I0", "W", "E1", "F1", "S1", "H1", "I1"]

        def end_stage(eng, name):
            n = stages.index(name) + 1
            eng.drain().then_inc(stage_done, 1)
            eng.wait_ge(stage_done, 5 * n)

        @block.sync
        def _(sp):
            def load(dst, src):
                sp.dma_start(dst, src).then_inc(in_sem, 16)
                in_count[0] += 1

            def loaded():
                sp.wait_ge(in_sem, 16 * in_count[0])

            x_v = x.rearrange("(t p) d -> p t d", p=P)
            for q in range(4):
                part = slice(q * NT // 4, (q + 1) * NT // 4)
                sp.dma_start(x_res[:, part, :], x_v[:, part, :]).then_inc(x_in[q], 16)
            load(a_w[:], wqkvT.rearrange("(a p) n -> p a n", p=P))
            load(a_b[:], bqkv)
            load(tgate[:], gates.partition_broadcast(P))
            ctx_v = ctxT.rearrange("(c p) (g n) -> g p c n", p=P, n=GS)

            def a_group(b, s):
                sp.wait_ge(proj_done, 12 * b + 6 * s + 6)
                sp.dma_start(a_ctx[:, s], ctx_v[bass.ds(2 * b + s, 1)].rearrange("a p c n -> (a p) c n"))\
                  .then_inc(ctx_in[s], 16)

            with sp.Fori(0, NG // 2) as b:
                for s in range(2):
                    a_group(b, s)
            end_stage(sp, "A")

            qk_v = qkv_d.rearrange("u j (h d) (t n) -> u j t d h n", h=HEADS, t=TB)
            v_v = qkv_d.rearrange("u j (g d) (t n) -> u j t g d n", g=HEADS, t=TB)

            def kq_load(g, s):
                for t in range(TB):
                    rows = slice(HD * t, HD * t + HD)
                    sp.dma_start(k_diag[s][rows, t], qk_v[bass.ds(g, 1), 0, t].rearrange("a d h n -> (a d) h n"))\
                      .then_inc(kq_in[s], 16)
                    sp.dma_start(q_pad[rows, s, HEADS:2 * HEADS],
                                 qk_v[bass.ds(g, 1), 2, t].rearrange("a d h n -> (a d) h n")).then_inc(kq_in[s], 16)

            def v_load(g):
                for t in range(TB):
                    sp.dma_start(v_diag[HEADS * t:HEADS * t + HEADS, t],
                                 v_v[bass.ds(g, 1), 1, t].rearrange("a g d n -> (a g) d n")).then_inc(v_in, 16)

            kq_load(0, 0)
            kq_load(1, 1)
            for g in range(2):
                if g == 1:
                    sp.wait_ge(pv_done, 1)
                v_load(g)
                sp.wait_ge(sc_done, g + 1)
                kq_load(g + 2, g)
            with sp.Fori(1, NG // 2 - 1) as b:
                for s in range(2):
                    sp.wait_ge(pv_done, 2 * b + s)
                    v_load(2 * b + s)
                    sp.wait_ge(sc_done, 2 * b + s + 1)
                    kq_load(2 * b + s + 2, s)
            for g in range(NG - 2, NG):
                sp.wait_ge(pv_done, g)
                v_load(g)
            end_stage(sp, "B")

            load(d_w[:], woT.rearrange("(c p) n -> p c n", p=P))
            load(d_bo[:], bo.partition_broadcast(P))
            od_v = o_d.rearrange("u (c p) n -> u p c n", p=P)
            with sp.Fori(0, NG // 2) as b:
                for s in range(2):
                    sp.wait_ge(op_done, 2 * b + s + 1)
                    sp.dma_start(d_o[:, s], od_v[bass.ds(2 * b + s, 1)].rearrange("a p c n -> (a p) c n"))\
                      .then_inc(o_in[s], 16)
            end_stage(sp, "D")

            def rows(L, before_, weights=0):
                q = lay[L.name]

                def steps(b):
                    for s in range(RS):
                        sp.wait_ge(row_ready, before_ + RS * b + s + 1)
                        sp.dma_start(xr_d[0:NTOK].rearrange("(t p) c -> t p c", p=P)[bass.ds(RS * b + s, 1)]
                                     .rearrange("o p c -> (o p) c"), rows_s[s][:]).then_inc(q["row_st"][s], 16)

                n = NT // RS
                if weights:
                    with sp.Fori(0, weights // WB) as b:
                        steps(b)
                        weights1(b)
                with sp.Fori(weights // WB, n) as b:
                    steps(b)
                for s in range(RS):
                    sp.wait_ge(q["row_st"][s], 16 * n)

            def weights1(b):
                sp.dma_start(w_all1[:, bass.ds(b * WB * L1.W, WB * L1.W)].rearrange("p (e n) -> p e n", e=WB),
                             exp1[bass.ds(b * WB, WB)].rearrange("e p n -> p e n")).then_inc(w_in, 16)

            def sums(L):
                q = lay[L.name]
                with sp.Fori(0, NG // 2) as b:
                    for s in range(2):
                        g = 2 * b + s
                        sp.wait_ge(q["a_used"], g + 1)
                        if L is L1:
                            sp.dma_start(x_res[:, bass.ds(g * GT, GT), :].rearrange("p t d -> p (t d)"),
                                         x_d[:, bass.ds(g * GT * D, GT * D)]).then_inc(q["a_in"][s], 16)
                        for a in range(NA):
                            src = acc_d[L.name][a][0:NTOK, :].rearrange("(g t p) d -> g p t d", g=NG, p=P)
                            sp.dma_start(c_a[:, s, a, :].rearrange("p (t d) -> p t d", t=GT),
                                         src[bass.ds(g, 1)].rearrange("o p t d -> (o p) t d"))\
                              .then_inc(q["a_in"][s], 16)

            load(e_g0[:], gate0T.rearrange("(c p) n -> p c n", p=P))
            end_stage(sp, "E0")
            load(r_gb[:], gate0b.partition_broadcast(P))
            end_stage(sp, "F0")
            load(e_w1[:], sh1T.rearrange("(c p) n -> p c n", p=P))
            load(e_w3[:], sh3T.rearrange("(c p) n -> p c n", p=P))
            load(e_w2[:], sh2T.rearrange("(c p) n -> p c n", p=P))
            load(e_b[:], shb)
            load(e_bs2[:], bs2.partition_broadcast(P))
            for e in range(0, L0.E, 4):
                sp.dma_start(w_all0[:, e * L0.W:(e + 4) * L0.W].rearrange("p (e n) -> p e n", e=4),
                             exp0[e:e + 4].rearrange("e p n -> p e n")).then_inc(w_in, 16)
            rows(L0, 0)
            end_stage(sp, "S0")
            load(w_bias[:], exp0b.partition_broadcast(P))
            end_stage(sp, "H0")
            sums(L0)
            end_stage(sp, "I0")
            load(w_wu[:, 0:KC], wkv_w)
            load(w_wu[:, KC:2 * KC], wkv_u)
            with sp.Fori(0, NG // 2) as b:
                for s in range(2):
                    sp.wait_ge(wk_y, 2 * b + s + 1)
                    sp.dma_start(w_v[:, s], ctx_v[bass.ds(2 * b + s, 1)].rearrange("a p c n -> (a p) c n"))\
                      .then_inc(wk_v[s], 16)
            end_stage(sp, "W")
            load(e_g1[:], gate1T.rearrange("(c p) n -> p c n", p=P))
            end_stage(sp, "E1")
            end_stage(sp, "F1")
            sp.dma_start(x_d, x_res[:].rearrange("p t d -> p (t d)")).then_inc(x_st, 16)

            rows(L1, NT, in_front)
            sp.wait_ge(x_st, 16)
            end_stage(sp, "S1")
            for b in range(in_front // WB, L1.E // WB):
                weights1(b)
            end_stage(sp, "H1")
            sums(L1)
            o_v = out.rearrange("(g t p) d -> g p t d", g=NG, p=P)
            with sp.Fori(0, NG) as g:
                sp.wait_ge(lay["b"]["a_used"], g + 3)
                sp.dma_start(o_v[bass.ds(g, 1)].rearrange("a p t d -> (a p) t d"),
                             x_res[:, bass.ds(g * GT, GT), :]).then_inc(out_st, 16)
            sp.wait_ge(out_st, 16 * NG)
            end_stage(sp, "I1")

        n_load = {"A": 3, "D": 5, "E0": 6, "F0": 7, "S0": 12, "H0": 13, "W": 15, "E1": 16}
        w_count = {"a": L0.E // 4, "b": L0.E // 4 + L1.E // WB}

        @block.gpsimd
        def _(pool):
            pool.memset(ones[:], 1.0)
            pool.memset(ones_h[:], 1.0)
            pool.memset(zeros[:], 0.0)
            pool.memset(meta[:], 0.0)
            for s in range(RS):
                pool.memset(rows_s[s][:], 0.0)
            pool.drain()
            pool.affine_select(out=ident[:], in_=ones[:], pattern=[[-1, P]], compare_op=ALU.is_equal, fill=0.0,
                               base=0, channel_multiplier=1)
            pool.affine_select(out=before[:], in_=ones_h[:], pattern=[[1, P]], compare_op=ALU.is_gt, fill=0.0,
                               base=0, channel_multiplier=-1)
            def count(ap, pattern, base=0, step=0):
                pool.iota(ap, pattern=pattern, base=base, channel_multiplier=step,
                          allow_small_or_imprecise_dtypes=True)

            count(tile_row[:], [[P, MT]])
            count(lanes[:], [[1, P]])
            count(token1[:], [[P, NT]], base=1, step=1)
            count(void1[:], [[1, 1]], base=NTOK + 1, step=1)
            pool.drain().then_inc(const_ready, 4)

            def zero_accumulators(L):
                for a in range(NA):
                    v = acc_d[L.name][a][0:NTOK, :].rearrange("(n p r) d -> n p (r d)", p=P, r=ZT)
                    for i in range(NT // ZT):
                        pool.dma_start(v[i], zeros[:]).then_inc(zero_st, 16)
                    pool.dma_start(acc_d[L.name][a][NTOK:, :], zeros[:, 0:D]).then_inc(zero_st, 16)

            pool.wait_ge(x_in[3], 16)
            pool.wait_ge(in_sem, 16 * n_load["A"])
            zero_accumulators(L0)
            pool.dma_start(xr_d[NTOK:, :], zeros[:, 0:RW]).then_inc(zero_st, 16)
            for s in range(2):
                pool.memset(k_diag[s][:], 0.0)
            pool.memset(v_diag[:], 0.0)
            end_stage(pool, "A")
            end_stage(pool, "B")
            end_stage(pool, "D")

            def iotas(L):
                count(r_ie[:, 0:L.E], [[1, L.E]])
                count(r_ij[:], [[P, NT]])
                pool.memset(r_keep[:, 0:L.E * NT], 1.0)
                pool.drain()
                pool.memset(r_keep[:, 0:L.E * NT].rearrange("p (e t) -> p e t", t=NT)[:, :, 0:1], 0.0)
                pool.drain().then_inc(const_ready, 1)

            def experts(L):
                q = lay[L.name]

                def tokens(m, h):
                    pool.tensor_copy(h_ix[:, h * TQ:(h + 1) * TQ], order[:, bass.ds(TQ * m, TQ)])\
                        .then_inc(q["ix_done"], 1)

                def gather(s):
                    pool.indirect_dma_start(
                        h_x[s % TD][:], None, xr_d, bass.IndirectOffsetOnAxis(ap=h_ix[:, s:s + 1], axis=0))\
                        .then_inc(q["x_in"][s % TD], 16)

                def body(b, first, last):
                    for s in range(2 * TD):
                        i = 2 * TD * b + s
                        pool.wait_ge(q["y_done"], i + TD + 1)
                        if not (first and s < NA):
                            pool.wait_ge(q["chain"][s % NA], 16 * ((2 * TD // NA) * b + s // NA))
                        pool.sem_inc(spacer, 1)
                        pool.indirect_dma_start(
                            acc_d[L.name][s % NA], bass.IndirectOffsetOnAxis(ap=h_ix[:, s:s + 1], axis=0),
                            h_y[s % TD][:], None, compute_op=ALU.add).then_inc(q["chain"][s % NA], 16)
                        n = (s + LEAD) % (2 * TD)
                        if last and s + LEAD >= 2 * TD:
                            continue
                        m = 2 * TD // TQ * b + (s + LEAD) // TQ
                        if n % TQ == 0:
                            if not (first and s + LEAD < 2 * TD):
                                for a in range(NA):
                                    pool.wait_ge(q["chain"][a], 16 * (m + 1 - 2 * TD // TQ))
                                pool.sem_inc(spacer, 1)
                            tokens(m, n // TQ)
                            pool.wait_ge(q["ix_done"], m + 1)
                            pool.sem_inc(spacer, 1)
                        gather(n)

                for h in range(LEAD // TQ):
                    tokens(h, h)
                pool.wait_ge(q["ix_done"], LEAD // TQ)
                for s in range(LEAD):
                    gather(s)
                n = L.tiles // (2 * TD)
                body(0, True, False)
                with pool.Fori(1, n - 1) as b:
                    body(b, False, False)
                body(n - 1, False, True)
                for a in range(NA):
                    pool.wait_ge(q["chain"][a], 16 * L.tiles // NA)

            end_stage(pool, "E0")
            iotas(L0)
            pool.wait_ge(zero_st, 16 * (NA * (NT // ZT + 1) + 1))
            end_stage(pool, "F0")
            end_stage(pool, "S0")
            pool.wait_ge(order_ready, 1)
            experts(L0)
            end_stage(pool, "H0")
            end_stage(pool, "I0")
            for c in range(KC):
                pool.memset(w_dec[:, c, :, 0:1], LOW)
            for s in range(2):
                for c in range(KC):
                    pool.memset(w_k[:, s, c, :, 0:1], LOW)
                pool.memset(w_a2[:, s, :, 0:1], 0.0)
                pool.memset(w_e2[:, s, :, 0:1], 0.0)
            pool.memset(w_ev[:, :, 0:1], 0.0)
            pool.memset(zeros[:], 0.0)
            pool.drain().then_inc(wk_pad, 1)
            pool.sem_inc(wk_nd, 2)
            with pool.Fori(0, NG // 2) as b:
                for s in range(2):
                    for c in range(KC):
                        i = 2 * KC * b + KC * s + c
                        val = w_v[:, s, c, :].rearrange("p (b t) -> p b t", t=SEQ)
                        pool.drain()
                        pool.wait_ge(wk_s, i + 1)
                        pool.sem_inc(spacer, 1)
                        pool.tensor_tensor(w_m[:], w_ex[:, c, 1], val, ALU.mult)
                        pool.tensor_tensor(w_d[:, c], w_ex[:, c, 0], w_q[:, c, :, 0:SEQ], ALU.mult)
                        pool.tensor_tensor(w_n[:, c], w_ex[:, c, 0], w_p[:, c, :, 0:SEQ], ALU.mult)
                        pool.drain()
                        pool.tensor_tensor(w_d[:, c], w_d[:, c], w_ex[:, c, 1], ALU.add)
                        pool.tensor_tensor(w_n[:, c], w_n[:, c], w_m[:], ALU.add).then_inc(wk_nd, 1)
            end_stage(pool, "W")
            zero_accumulators(L1)
            end_stage(pool, "E1")
            iotas(L1)
            pool.wait_ge(zero_st, 16 * (2 * NA * (NT // ZT + 1) + 1))
            end_stage(pool, "F1")
            end_stage(pool, "S1")
            pool.wait_ge(order_ready, 2)
            experts(L1)
            end_stage(pool, "H1")
            end_stage(pool, "I1")

        @block.tensor
        def _(pe):
            pe.sem_inc(tr_done, 2)
            pe.sem_inc(proj_done, 12)
            pe.sem_inc(op_done, 2)
            pe.sem_inc(rt_done, 2)
            pe.sem_inc(wk_yt, 2)
            for L in (L0, L1):
                for name in ("t_done", "u_done", "ht_done", "d_done"):
                    pe.sem_inc(lay[L.name][name], 2)
            pe.sem_inc(pair_done, OR)

            def transposes(n, s, bank=0):
                pe.wait_ge(xn_ready, n + 1)
                pe.wait_ge(xT_ready, n if bank else n + 1)
                for j in range(GT):
                    for c in range(KC):
                        m = pe.transpose(ps[:, bank + c, j * P:(j + 1) * P], n_x[:, s, j, c * P:(c + 1) * P], ident[:])
                m.then_inc(tr_done, 1)

            pe.wait_ge(const_ready, 4)
            pe.wait_ge(in_sem, 16 * n_load["A"])
            with pe.Fori(0, NG // 2) as b:
                for s in range(2):
                    g = 2 * b + s
                    transposes(g, s)
                    pe.wait_ge(ctx_in[s], 16 * b + 16)
                    for j in range(3 * KC):
                        if j == 2 * KC:
                            pe.wait_ge(xT_ready, g + 2)
                        pe.wait_ge(proj_out, 6 * g + j + 1)
                        src = a_ctx if j < 2 * KC else a_xT
                        for c in range(KC):
                            m = pe.matmul(ps[:, 2 + j, :],
                                          a_w[:, (j // KC) * KC + c, (j % KC) * P:(j % KC) * P + P],
                                          src[:, s, c, :], start=(c == 0), stop=(c == KC - 1))
                        m.then_inc(proj_done, 1)
            end_stage(pe, "A")

            def block_products(bank, stationary, moving):
                for c in range(BC):
                    for e in range(BR):
                        m = pe.matmul(ps[32 * (e // 2):32 * (e // 2) + 32, bank + c // 4, (c % 4) * P:(c % 4 + 1) * P],
                                      stationary(BR * c + e, HEADS * (1 - e % 2)), moving(BR * c + e),
                                      start=(e % 2 == 0), stop=(e % 2 == 1))
                return m

            def scores_of(g, s, b, used=True):
                pe.wait_ge(kq_in[s], 16 * 2 * TB * b + 16 * 2 * TB)
                if used:
                    pe.wait_ge(sub_done, g)
                block_products(0, lambda n, z0: q_pad[:, s, z0:z0 + 2 * HEADS, n],
                               lambda n: k_diag[s][:, :, :, n].rearrange("p t h -> p (t h)"))\
                    .then_inc(sc_done, 1)

            def results_back(g):
                pe.wait_ge(o_done, g + 1)
                pe.wait_ge(ot_ready, g + 1)
                for c in range(BC):
                    m = pe.transpose(ps[:, 6 + c // 4, (c % 4) * P:(c % 4 + 1) * P],
                                     o_nm[:, c * P:(c + 1) * P], ident[:])
                m.then_inc(ot_done, 1)

            def results_of(g, back):
                pe.wait_ge(pt_ready, g + 1)
                pe.wait_ge(v_in, 16 * TB * g + 16 * TB)
                if back:
                    pe.wait_ge(o_done, g)
                block_products(4, lambda n, z0: pT_pad[:, n, z0:z0 + 2 * HEADS],
                               lambda n: v_diag[:, :, :, n].rearrange("p t d -> p (t d)"))\
                    .then_inc(pv_done, 1)

            def exponentials_back(g, s):
                pe.wait_ge(exp_done, g + 1)
                for c in range(BC):
                    m = pe.transpose(ps[:, 2 + c // 4, (c % 4) * P:(c % 4 + 1) * P],
                                     probs[:, s, c * P:(c + 1) * P], ident[:])
                m.then_inc(pt_done, 1)

            pe.wait_ge(pad_zero, 1)
            scores_of(0, 0, 0, False)
            exponentials_back(0, 0)
            scores_of(1, 1, 0)
            results_of(0, False)
            exponentials_back(1, 1)
            with pe.Fori(1, NG // 2) as b:
                for s in range(2):
                    g = 2 * b + s
                    scores_of(g, s, b)
                    results_back(g - 2)
                    results_of(g - 1, True)
                    exponentials_back(g, s)
            results_back(NG - 2)
            results_of(NG - 1, True)
            results_back(NG - 1)
            end_stage(pe, "B")

            pe.wait_ge(in_sem, 16 * n_load["D"])
            with pe.Fori(0, NG // 2) as b:
                for s in range(2):
                    pe.wait_ge(o_in[s], 16 * b + 16)
                    pe.wait_ge(op_used, 2 * b + s + 1)
                    for j in range(GT):
                        for c in range(KC):
                            m = pe.matmul(ps[:, 2 * s + j // 2, (j % 2) * D:(j % 2) * D + D],
                                          d_o[:, s, c, j * P:(j + 1) * P], d_w[:, c, :],
                                          start=(c == 0), stop=(c == KC - 1))
                    m.then_inc(op_done, 1)
            end_stage(pe, "D")

            def scores(L, g, s, gw):
                bank = ps[:, 2:2 + L.E * NT // 512, :].rearrange("p b n -> p (b n)")
                for j in range(GT):
                    for c in range(KC):
                        m = pe.matmul(bank[:, bass.ds((g * GT + j) * L.E, L.E)],
                                      e_xT[:, s, c, j * P:(j + 1) * P], gw[:, c, :],
                                      start=(c == 0), stop=(c == KC - 1))
                m.then_inc(rt_done, 1)

            def router(L, n0, gw):
                def groups(b, last):
                    for s in range(2):
                        g = 2 * b + s
                        if not (last and s == 1):
                            transposes(n0 + g + 1, 1 - s, 6 * (1 - s))
                        pe.wait_ge(xT_ready, n0 + g + 2)
                        scores(L, g, s, gw)

                transposes(n0, 0)
                with pe.Fori(0, NG // 2 - 1) as b:
                    groups(b, False)
                groups(NG // 2 - 1, True)

            pe.wait_ge(in_sem, 16 * n_load["E0"])
            router(L0, NG, e_g0)
            end_stage(pe, "E0")

            def pair(L, n, r, first=False, last=False):
                pe.wait_ge(pair_ready, n + 1)
                pe.matmul(ps[:, 2, 0:L.tiles], o_in_row[:, r, :], o_of_tile[:, r, 0:L.tiles],
                          start=first, stop=last).then_inc(pair_done, 1)

            def shared(b, first, last):
                k0 = GT * L0.K // 4

                def pairs(s, q):
                    for k in range(q * k0, (q + 1) * k0):
                        pair(L0, (2 * b + s) * GT * L0.K + k, k % OR, first and s == 0 and k == 0,
                             last and s == 1 and k == GT * L0.K - 1)

                for s in range(2):
                    g = 2 * b + s
                    pe.wait_ge(xT_ready, 2 * NG + g + 2)
                    for q, w in enumerate(HSP):
                        r = (3 * s + q) % 2
                        pe.wait_ge(sh_h, 3 * g + q + 1)
                        for k, wt in enumerate((e_w1, e_w3)):
                            for c in range(KC):
                                m = pe.matmul(ps[0:w, 3 + 2 * r + k, :], wt[:, c, P * q:P * q + w],
                                              e_xT[:, s, c, :], start=(c == 0), stop=(c == KC - 1))
                        m.then_inc(sh_done, 1)
                        pairs(s, q)
                    if not (last and s == 1):
                        transposes(2 * NG + g + 1, 1 - s)
                    pairs(s, 3)
                    pe.wait_ge(sh_h, 3 * g + 5)
                    for h in range(2):
                        pe.wait_ge(sh_zu, 2 * g + h + 1)
                        for j in (2 * h, 2 * h + 1):
                            for q, w in enumerate(HSP):
                                m = pe.matmul(ps[:, 7, (j % 2) * D:(j % 2) * D + D],
                                              e_h[0:w, s, q, j * P:(j + 1) * P], e_w2[0:w, q, :],
                                              start=(q == 0), stop=(q == 2))
                        m.then_inc(sh_z, 1)

            def route(L, nth):
                F = L.E * NT
                nb = F // 512
                pe.wait_ge(hot_ready, nth)
                for q in range(nb):
                    pe.matmul(ps[:, q, :], before[:], r_m[:, q * 512:(q + 1) * 512], start=True, stop=True)
                    m = pe.matmul(ps[:, 4 + q, :], ones_h[:], r_m[:, q * 512:(q + 1) * 512], start=True, stop=True)
                m.then_inc(rank_ready, 1)
                pe.wait_ge(cmp_ready, nth)
                pe.matmul(ps[:, 4, 0:L.tiles], ones_h[0:L.E, :], r_cmp[0:L.E, 0:L.tiles],
                          start=True, stop=True).then_inc(map_ready, 1)

            def experts(L, w_all):
                q = lay[L.name]
                h1 = L.H // L.NC

                def expert(i):
                    return pe.value_load(tile_e[0:1, bass.ds(i, 1)], min_val=0, max_val=L.E - 1)

                def tr(i, s, b):
                    pe.wait_ge(q["x_in"][s], 16 * b + 16)
                    pe.wait_ge(q["t_ready"], i + 1)
                    for c in range(KC):
                        m = pe.transpose(ps[:, s % 2, c * P:(c + 1) * P], h_x[s][:, c * P:(c + 1) * P],
                                         ident[:])
                    m.then_inc(q["t_done"], 1)

                def up(i, s, e):
                    pe.wait_ge(q["t_ready"], i + 3)
                    pe.wait_ge(q["h_done"], i + 1)
                    for c in range(KC):
                        m = pe.matmul(ps[:, 2 + s % 2, 0:2 * L.H], h_xT[:, s % 2, c, :],
                                      w_all[:, bass.ds(e * L.W + c * 2 * L.H, 2 * L.H)],
                                      start=(c == 0), stop=(c == KC - 1))
                    m.then_inc(q["u_done"], 1)

                def turn(i, s):
                    pe.wait_ge(q["h_done"], i + 3)
                    pe.wait_ge(q["ht_ready"], i + 1)
                    for j in range(L.NC):
                        m = pe.transpose(ps[0:h1, 4 + s % 2, j * P:(j + 1) * P],
                                         h_h[:, s % 2, j * h1:(j + 1) * h1], ident[:])
                    m.then_inc(q["ht_done"], 1)

                def down(i, s, e):
                    pe.wait_ge(q["ht_ready"], i + 3)
                    pe.wait_ge(q["y_done"], i + TD - 1)
                    for j in range(L.NC):
                        w = h1 + (1 if L.bias and j == 0 else 0)
                        m = pe.matmul(ps[:, 6 + s % 2, 0:D], h_hT[0:w, s % 2, j, :],
                                      w_all[0:w, bass.ds(e * L.W + L.up0 + j * D, D)],
                                      start=(j == 0), stop=(j == L.NC - 1))
                    m.then_inc(q["d_done"], 1)

                def body(b, first):
                    known = {}
                    if not first:
                        known[-1] = expert(TD * b - 1)
                    for s in range(TD):
                        j = TD * b + s
                        tr(j, s, b)
                        if not (first and s < 1):
                            up(j - 1, (s - 1) % TD, known[s - 1])
                        if s < TD - 1:
                            known[s] = expert(j)
                        if not first and s < 2:
                            known[s - 3] = expert(j - 3)
                        if not (first and s < 2):
                            turn(j - 2, (s - 2) % TD)
                        if not (first and s < 3):
                            down(j - 3, (s - 3) % TD, known[s - 3])

                pe.wait_ge(w_in, 16 * w_count[L.name])
                body(0, True)
                with pe.Fori(1, L.tiles // TD) as b:
                    body(b, False)
                n = L.tiles
                up(n - 1, (n - 1) % TD, expert(n - 1))
                turn(n - 2, (n - 2) % TD)
                down(n - 3, (n - 3) % TD, expert(n - 3))
                turn(n - 1, (n - 1) % TD)
                down(n - 2, (n - 2) % TD, expert(n - 2))
                down(n - 1, (n - 1) % TD, expert(n - 1))

            route(L0, 1)
            end_stage(pe, "F0")
            pe.wait_ge(in_sem, 16 * n_load["S0"])
            transposes(2 * NG, 0)
            shared(0, True, False)
            with pe.Fori(1, NG // 2 - 1) as b:
                shared(b, False, False)
            shared(NG // 2 - 1, False, True)
            end_stage(pe, "S0")
            experts(L0, w_all0)
            end_stage(pe, "H0")
            end_stage(pe, "I0")

            def states_back(g, s):
                pe.wait_ge(wk_y, g + 3)
                pe.wait_ge(wk_yu, g + 1)
                for j in range(GT):
                    for c in range(KC):
                        m = pe.transpose(ps[:, 2 + 2 * s + j // 2, (j % 2) * D + c * P:(j % 2) * D + c * P + P],
                                         w_y[:, s, c].rearrange("p b t -> p (b t)")[:, j * P:(j + 1) * P],
                                         ident[:])
                m.then_inc(wk_yt, 1)

            for g in range(2):
                transposes(3 * NG + g, g)
            with pe.Fori(0, NG // 2 - 1) as b:
                for s in range(2):
                    transposes(3 * NG + 2 * b + s + 2, s)
                    states_back(2 * b + s, s)
            for s in range(2):
                states_back(NG - 2 + s, s)
            end_stage(pe, "W")

            pe.wait_ge(in_sem, 16 * n_load["E1"])
            router(L1, 4 * NG, e_g1)
            end_stage(pe, "E1")
            route(L1, 2)
            end_stage(pe, "F1")

            def pairs1(t, first, last):
                for k in range(L1.K):
                    pair(L1, NT * L0.K + t * L1.K + k, k % OR, first and k == 0, last and k == L1.K - 1)

            pairs1(0, True, False)
            with pe.Fori(1, NT - 1) as t:
                pairs1(t, False, False)
            pairs1(NT - 1, False, True)
            end_stage(pe, "S1")
            experts(L1, w_all1)
            end_stage(pe, "H1")
            end_stage(pe, "I1")

        @block.scalar
        def _(act):
            act.sem_inc(xT_ready, 1)
            act.sem_inc(proj_out, 6)
            act.sem_inc(ot_ready, 1)
            act.sem_inc(wk_e, 2)
            for s in range(2):
                act.sem_inc(qkv_st[s], 16)
                act.sem_inc(o_st[s], 16)
            for L in (L0, L1):
                act.sem_inc(lay[L.name]["t_ready"], 2)
                act.sem_inc(lay[L.name]["ht_ready"], 2)

            def std(nth):
                act.wait_ge(var_ready, nth)
                act.activation(rstd[:], mean_v[:], ACT.Sqrt).then_inc(std_ready, 1)

            act.wait_ge(in_sem, 16 * n_load["A"])
            act.activation(tgate[:], tgate[:], ACT.Tanh).then_inc(tanh_done, 1)
            std(1)
            qkv_v = qkv_d.rearrange("u j (c p) n -> u p (j c) n", p=P)
            with act.Fori(0, NG // 2) as b:
                for s in range(2):
                    g = 2 * b + s
                    act.wait_ge(proj_done, 6 * g + 6)
                    act.wait_ge(tr_done, g + 3)
                    act.copy(a_xT[:, s, 0, :], ps[:, 0, :])
                    act.copy(a_xT[:, s, 1, :], ps[:, 1, :]).then_inc(xT_ready, 1)
                    act.wait_ge(qkv_st[s], 16 * b + 16)
                    for j in range(3 * KC):
                        act.wait_ge(proj_done, 6 * g + j + 13)
                        act.activation(a_out[:, s, j, :], ps[:, 2 + j, :], ACT.Identity,
                                       bias=a_b[:, j:j + 1]).then_inc(proj_out, 1)
                    act.wait_ge(proj_out, 6 * g + 12)
                    act.dma_start(qkv_v[bass.ds(g, 1)].rearrange("a p j n -> (a p) j n"), a_out[:, s])\
                       .then_inc(qkv_st[s], 16)
            for s in range(2):
                act.wait_ge(qkv_st[s], 16 * (NG // 2 + 1))
            end_stage(act, "A")

            ost_v = o_d.rearrange("u (h d) (t n) -> u (d t) h n", h=HEADS, t=TB)

            def exponentials(g, s):
                act.wait_ge(sub_done, g + 1)
                act.activation(probs[:, s], probs[:, s], ACT.Exp).then_inc(exp_done, 1)

            def exponentials_out(g):
                act.wait_ge(pt_done, g + 1)
                act.copy(pT_pad[:, :, HEADS:2 * HEADS],
                         ps[:, 2:4, :].rearrange("p a (n h) -> p (a n) h", h=HEADS)).then_inc(pt_ready, 1)

            def results_out(g, s, b):
                act.wait_ge(ot_done, g + 1)
                act.wait_ge(o_st[s], 16 * b + 16)
                act.copy(oT[:, s].rearrange("p h n -> p n h"),
                         ps[:, 6:8, :].rearrange("p a (n h) -> p (a n) h", h=HEADS)).then_inc(ot_ready, 1)
                act.wait_ge(ot_ready, g + 2)
                act.dma_start(ost_v[bass.ds(g, 1)].rearrange("a p h n -> (a p) h n"), oT[:, s])\
                   .then_inc(o_st[s], 16)

            for s in range(2):
                exponentials(s, s)
                exponentials_out(s)
            with act.Fori(1, NG // 2) as b:
                for s in range(2):
                    exponentials(2 * b + s, s)
                    results_out(2 * b + s - 2, s, b - 1)
                    exponentials_out(2 * b + s)
            for s in range(2):
                results_out(NG - 2 + s, s, NG // 2 - 1)
            for s in range(2):
                act.wait_ge(o_st[s], 16 * (NG // 2 + 1))
            end_stage(act, "B")
            end_stage(act, "D")

            def transposed(n, s, dst, bank=0):
                act.wait_ge(tr_done, n + 3)
                for c in range(KC):
                    m = act.copy(dst(s, c), ps[:, bank + c, :])
                m.then_inc(xT_ready, 1)

            def e_dst(s, c):
                return e_xT[:, s, c, :]

            def router(n0, r0):
                with act.Fori(0, NG // 2) as b:
                    for s in range(2):
                        act.wait_ge(rt_done, r0 + 2 * b + s + 1)
                        transposed(n0 + 2 * b + s, s, e_dst, 6 * s)

            std(2)
            router(NG, 0)
            end_stage(act, "E0")

            def shared(b, last):
                for s in range(2):
                    g = 2 * b + s
                    for q, w in enumerate(HSP):
                        r = (3 * s + q) % 2
                        act.wait_ge(sh_done, 3 * g + q + 1)
                        act.wait_ge(sh_h, 3 * g + q + 1)
                        act.activation(e_sg[0:w, r, :], ps[0:w, 3 + 2 * r, :], ACT.Silu, bias=e_b[0:w, q:q + 1])\
                           .then_inc(sh_silu, 1)
                    if not (last and s == 1):
                        transposed(2 * NG + g + 1, 1 - s, e_dst)

            def route(L, nth):
                act.wait_ge(sc_ready, nth)
                act.activation(r_p[:, 0:L.E * NT], r_p[:, 0:L.E * NT], ACT.Exp).then_inc(pr_ready, 1)

            def experts(L):
                q = lay[L.name]
                h1 = L.H // L.NC

                def tr(i, s):
                    act.wait_ge(q["t_done"], i + 3)
                    act.wait_ge(q["u_done"], i + 1)
                    act.copy(h_xT[:, s % 2].rearrange("p c n -> p (c n)"), ps[:, s % 2, 0:D])\
                       .then_inc(q["t_ready"], 1)

                def gate(i, s):
                    if L.bias:
                        act.wait_ge(q["b_done"], i + 1)
                    else:
                        act.wait_ge(q["u_done"], i + 3)
                    act.wait_ge(q["h_done"], i + 1)
                    src = h_gu[:, s % 2, 0:L.H] if L.bias else ps[:, 2 + s % 2, 0:L.H]
                    act.activation(h_sg[:, s % 2, 0:L.H], src, ACT.Silu).then_inc(q["s_done"], 1)

                def turn(i, s):
                    act.wait_ge(q["ht_done"], i + 3)
                    act.wait_ge(q["d_done"], i + 1)
                    act.copy(h_hT[0:h1, s % 2, 0:L.NC, :].rearrange("p j n -> p (j n)"),
                             ps[0:h1, 4 + s % 2, 0:L.NC * P]).then_inc(q["ht_ready"], 1)

                def body(b, first):
                    for s in range(TD):
                        j = TD * b + s
                        tr(j, s)
                        if not (first and s < 1):
                            gate(j - 1, (s - 1) % TD)
                        if not (first and s < 2):
                            turn(j - 2, (s - 2) % TD)

                act.preload_act_table(ACT.Silu)
                body(0, True)
                with act.Fori(1, L.tiles // TD) as b:
                    body(b, False)
                n = L.tiles
                gate(n - 1, (n - 1) % TD)
                turn(n - 2, (n - 2) % TD)
                turn(n - 1, (n - 1) % TD)

            route(L0, 1)
            end_stage(act, "F0")
            act.wait_ge(in_sem, 16 * n_load["S0"])
            act.preload_act_table(ACT.Silu)
            transposed(2 * NG, 0, e_dst)
            with act.Fori(0, NG // 2 - 1) as b:
                shared(b, False)
            shared(NG // 2 - 1, True)
            end_stage(act, "S0")
            experts(L0)
            end_stage(act, "H0")
            end_stage(act, "I0")

            std(3)
            act.wait_ge(in_sem, 16 * n_load["W"])
            act.wait_ge(wk_pad, 1)
            with act.Fori(0, NG // 2) as b:
                for s in range(2):
                    g = 2 * b + s
                    act.wait_ge(wk_t, 2 * g + 2)
                    act.wait_ge(tr_done, 3 * NG + g + 3)
                    for c in range(KC):
                        m = act.copy(w_k[:, s, c, :, 1:SEQ + 1],
                                     ps[:, c, :].rearrange("p (b t) -> p b t", t=SEQ))
                    m.then_inc(xT_ready, 1)
                    for c in range(KC):
                        act.wait_ge(wk_t, 2 * g + c + 5)
                        act.wait_ge(wk_nd, 2 * g + c + 1)
                        act.activation(w_a2[:, c, :, 1:SEQ + 1], w_t[:, c, 0], ACT.Exp, bias=w_wu[:, c:c + 1])
                        act.activation(w_e2[:, c, :, 1:SEQ + 1], w_t[:, c, 1], ACT.Exp)
                        act.activation(w_ex[:, c].rearrange("p j b t -> p (j b t)"),
                                       w_t[:, c, 2:4].rearrange("p j b t -> p (j b t)"), ACT.Exp)\
                           .then_inc(wk_e, 1)
            end_stage(act, "W")

            std(4)
            router(4 * NG, NG)
            end_stage(act, "E1")
            route(L1, 2)
            end_stage(act, "F1")
            end_stage(act, "S1")
            experts(L1)
            end_stage(act, "H1")
            end_stage(act, "I1")

        @block.vector
        def _(dve):
            dve.sem_inc(op_used, 2)
            dve.sem_inc(sh_h, 2)
            dve.sem_inc(sh_zu, 1)
            dve.sem_inc(wk_y, 2)
            dve.sem_inc(wk_t, 4)
            dve.sem_inc(wk_yu, 2)
            for L in (L0, L1):
                dve.sem_inc(lay[L.name]["h_done"], 2)
                dve.sem_inc(lay[L.name]["y_done"], TD)
                dve.sem_inc(lay[L.name]["a_used"], 2)

            def group_stats(g):
                for j in range(GT):
                    t = g * GT + j
                    dve.bn_stats(stats[:, bass.ds(t, 1), :].rearrange("p a k -> p (a k)"),
                                 x_res[:, bass.ds(t, 1), :].rearrange("p a d -> p (a d)"))

            def moments(nth, have_stats=False):
                if not have_stats:
                    with dve.Fori(0, NG) as g:
                        group_stats(g)
                    dve.drain()
                dve.tensor_tensor(mean[:], stats[:, :, 1], stats[:, :, 4], ALU.add)
                dve.tensor_tensor(tmp_t[:], stats[:, :, 1], stats[:, :, 4], ALU.subtract)
                dve.tensor_tensor(mean_v[:], stats[:, :, 2], stats[:, :, 5], ALU.add)
                dve.drain()
                dve.tensor_scalar(mean[:], mean[:], 0.5, None, ALU.mult)
                dve.tensor_scalar(mean_v[:], mean_v[:], 1.0 / D, EPS, ALU.mult, ALU.add)
                dve.tensor_tensor(tmp_t[:], tmp_t[:], tmp_t[:], ALU.mult)
                dve.drain()
                dve.scalar_tensor_tensor(mean_v[:], tmp_t[:], 0.25, mean_v[:], ALU.mult, ALU.add)\
                   .then_inc(var_ready, 1)
                dve.wait_ge(std_ready, nth)
                dve.reciprocal(rstd[:], rstd[:])
                dve.drain()

            def normed(dst, t):
                return dve.tensor_scalar(dst, x_res[:, bass.ds(t, 1), :].rearrange("p a d -> p (a d)"),
                                         mean[:, bass.ds(t, 1)], rstd[:, bass.ds(t, 1)],
                                         ALU.subtract, ALU.mult)

            def norm_group(n, g, s):
                dve.wait_ge(tr_done, n + 1)
                dve.sem_inc(spacer, 1)
                for j in range(GT):
                    m = normed(n_x[:, s, j, :], g * GT + j)
                m.then_inc(xn_ready, 1)

            for q in range(4):
                dve.wait_ge(x_in[q], 16)
                for g in range(q * NG // 4, (q + 1) * NG // 4):
                    group_stats(g)
            dve.drain()
            moments(1, have_stats=True)
            with dve.Fori(0, NG // 2) as b:
                for s in range(2):
                    norm_group(2 * b + s, 2 * b + s, s)
            end_stage(dve, "A")

            for side in (slice(0, HEADS), slice(2 * HEADS, 3 * HEADS)):
                dve.memset(q_pad[:, :, side], 0.0)
                dve.memset(pT_pad[:, :, side], 0.0)
            dve.drain().then_inc(pad_zero, 1)
            by_key = ps[:, 0:2, :].rearrange("p a (n g) -> p (a n) g", g=HEADS)

            def less_maxima(g, s, used):
                dve.wait_ge(sc_done, g + 1)
                dve.reduce_max(smax[:], by_key, AX)
                dve.drain()
                if used:
                    dve.wait_ge(pt_done, g - 1)
                dve.tensor_tensor(probs[:, s].rearrange("p (n g) -> p n g", g=HEADS), by_key,
                                  smax[:].unsqueeze(2).to_broadcast([P, BC * TB, HEADS]), ALU.subtract)\
                   .then_inc(sub_done, 1)

            def their_sums(g, s):
                dve.wait_ge(exp_done, g + 1)
                dve.reduce_sum(rsum[:, s], probs[:, s].rearrange("p (n g) -> p n g", g=HEADS), AX)
                dve.drain()
                dve.reciprocal(rsum[:, s], rsum[:, s])
                dve.drain()

            def normalised(g, s, used):
                dve.wait_ge(pv_done, g + 1)
                if used:
                    dve.wait_ge(ot_done, g)
                dve.tensor_tensor(o_nm[:].rearrange("p (c d t) -> p c t d", d=HD, t=TB),
                                  ps[:, 4:6, :].rearrange("p a (c t d) -> p (a c) t d", d=HD, t=TB),
                                  rsum[:, s].rearrange("p (c t) -> p c t", t=TB).unsqueeze(3)
                                  .to_broadcast([P, BC, TB, HD]), ALU.mult)\
                   .then_inc(o_done, 1)

            less_maxima(0, 0, False)
            their_sums(0, 0)
            less_maxima(1, 1, False)
            their_sums(1, 1)
            normalised(0, 0, False)
            with dve.Fori(1, NG // 2) as b:
                for s in range(2):
                    less_maxima(2 * b + s, s, True)
                    their_sums(2 * b + s, s)
                    normalised(2 * b + s - 1, 1 - s, True)
            normalised(NG - 1, 1, True)
            end_stage(dve, "B")

            def group_of(g, ap):
                return ap[:, bass.ds(g * GT, GT), :].rearrange("p t d -> p (t d)")

            dve.wait_ge(in_sem, 16 * n_load["D"])
            dve.wait_ge(tanh_done, 1)
            dve.tensor_scalar(d_bo[:], d_bo[:], tgate[:, 0:1], None, ALU.mult)
            dve.drain()
            with dve.Fori(0, NG // 2) as b:
                for s in range(2):
                    g = 2 * b + s
                    dve.wait_ge(op_done, g + 3)
                    dve.sem_inc(spacer, 1)
                    dve.scalar_tensor_tensor(group_of(g, x_res), ps[:, 2 * s:2 * s + 2, :]
                                             .rearrange("p a n -> p (a n)"), tgate[:, 0:1],
                                             group_of(g, x_res), ALU.mult, ALU.add).then_inc(op_used, 1)
                    dve.drain()
                    dve.tensor_tensor(x_res[:, bass.ds(g * GT, GT), :], x_res[:, bass.ds(g * GT, GT), :],
                                      d_bo[:].unsqueeze(1).to_broadcast([P, GT, D]), ALU.add)
                    dve.drain()
                    group_stats(g)
            end_stage(dve, "D")

            def router(n0):
                with dve.Fori(0, NG // 2) as b:
                    for s in range(2):
                        norm_group(n0 + 2 * b + s, 2 * b + s, s)

            moments(2, have_stats=True)
            router(NG)
            end_stage(dve, "E0")

            def stage_row(t, s):
                normed(rows_s[s][:, 0:D], t)
                dve.tensor_copy(rows_s[s][:, D:RW], meta[:, bass.ds(t, 1), :].rearrange("p a k -> p (a k)"))\
                   .then_inc(row_ready, 1)

            def pair(L, n, t, k, r):
                dve.wait_ge(pair_done, n + 1)
                dve.sem_inc(spacer, 1)
                dve.tensor_scalar(o_in_row[:, r, :], lanes[:],
                                  row_in[:, bass.ds(t, 1), k:k + 1].rearrange("p a k -> p (a k)"), None,
                                  ALU.is_equal)
                dve.tensor_scalar(o_of_tile[:, r, 0:L.tiles], tile_row[:, 0:L.tiles],
                                  row_of[:, bass.ds(t, 1), k:k + 1].rearrange("p a k -> p (a k)"),
                                  token1[:, bass.ds(t, 1)], ALU.is_equal, ALU.mult).then_inc(pair_ready, 1)

            def in_order(L, n):
                dve.wait_ge(pair_done, n + OR)
                dve.tensor_scalar(o_of_tile[:, 0, 0:L.tiles], ps[:, 2, 0:L.tiles], 0.0, void1[:, 0:1],
                                  ALU.is_equal, ALU.mult)
                dve.drain()
                dve.scalar_tensor_tensor(order[:, 0:L.tiles], ps[:, 2, 0:L.tiles], -1.0,
                                         o_of_tile[:, 0, 0:L.tiles], ALU.add, ALU.add)
                dve.drain().then_inc(order_ready, 1)

            def shared(b, first, last):
                k0 = GT * L0.K // 4

                def pairs(s, q):
                    for k in range(q * k0, (q + 1) * k0):
                        g = 2 * b + s
                        pair(L0, g * GT * L0.K + k, g * GT + k // L0.K, k % L0.K, k % OR)

                for s in range(2):
                    g = 2 * b + s
                    if not (last and s == 1):
                        norm_group(2 * NG + g + 1, g + 1, 1 - s)
                    pairs(s, 0)
                    for q, w in enumerate(HSP):
                        r = (3 * s + q) % 2
                        dve.wait_ge(sh_silu, 3 * g + q + 1)
                        dve.scalar_tensor_tensor(e_h[0:w, s, q, :], ps[0:w, 4 + 2 * r, :], e_b[0:w, 3 + q:4 + q],
                                                 e_sg[0:w, r, :], ALU.add, ALU.mult).then_inc(sh_h, 1)
                        pairs(s, q + 1)
                    for j in range(GT):
                        if not (first and s == 0):
                            dve.wait_ge(lay["a"]["row_st"][j], 16 * g)
                            dve.sem_inc(spacer, 1)
                        stage_row(g * GT + j, j)
                    for h in range(2):
                        dve.wait_ge(sh_z, 2 * g + h + 1)
                        dve.sem_inc(spacer, 1)
                        dve.tensor_tensor(z[:, bass.ds(g * GT + 2 * h, 2), :],
                                          ps[:, 7, :].rearrange("p (t d) -> p t d", t=2),
                                          e_bs2[:].unsqueeze(1).to_broadcast([P, 2, D]), ALU.add)\
                           .then_inc(sh_zu, 1)

            def route(L, nth):
                E, K, F = L.E, L.K, L.E * NT

                ids, weights = meta[:, :, 0:CHOICES], meta[:, :, CHOICES:META]

                def te(ap):
                    return ap[:, 0:F].rearrange("p (t e) -> p t e", e=E)

                def et(ap):
                    return ap[:, 0:F].rearrange("p (e t) -> p e t", t=NT)

                def over(ap, shape):
                    return ap.unsqueeze(2).to_broadcast(shape)

                TE, ET = [P, NT, E], [P, E, NT]
                raw = ps[:, 2:2 + F // 512, :].rearrange("p b (t e) -> p (b t) e", e=E)
                dve.reduce_max(r_t1[:], raw, AX)
                dve.drain()
                dve.tensor_tensor(te(r_p), raw, over(r_t1[:], TE), ALU.subtract).then_inc(sc_ready, 1)
                dve.wait_ge(pr_ready, nth)
                dve.reduce_sum(r_t1[:], te(r_p), AX)
                dve.drain()
                dve.reciprocal(r_t1[:], r_t1[:])
                dve.drain()
                dve.tensor_tensor(te(r_p), te(r_p), over(r_t1[:], TE), ALU.mult)
                dve.drain()
                chosen_by = te(r_p)
                if L is L0:
                    dve.wait_ge(in_sem, 16 * n_load["F0"])
                    dve.tensor_tensor(te(r_b), te(r_p), r_gb[:].unsqueeze(1).to_broadcast(TE), ALU.add)
                    dve.drain()
                    chosen_by = te(r_b)
                for t in range(NT):
                    dve.max(r_val[:, t, :], chosen_by[:, t, :])
                dve.drain()
                for t in range(NT):
                    dve.max_index(r_idx[:, t, :], r_val[:, t, :], chosen_by[:, t, :])
                dve.drain()
                dve.tensor_copy(ids, r_idx[:])
                dve.wait_ge(const_ready, 4 + nth)
                dve.drain()

                def hot(k):
                    dve.tensor_tensor(te(r_w), r_ie[:, 0:E].unsqueeze(1).to_broadcast(TE),
                                      over(ids[:, :, k], TE), ALU.is_equal)
                    dve.drain()

                if L is L0:
                    dve.memset(r_s[:, 0:F], 0.0)
                    for k in range(K):
                        hot(k)
                        dve.tensor_tensor(te(r_s), te(r_s), te(r_w), ALU.add)
                        dve.tensor_tensor(te(r_c), te(r_p), te(r_w), ALU.mult)
                        dve.drain()
                        dve.reduce_sum(weights[:, :, k], te(r_c), AX)
                    dve.tensor_copy(r_m[:, 0:F], r_s[:, 0:F]).then_inc(hot_ready, 1)
                else:
                    for t in range(NT):
                        dve.match_replace(te(r_w)[:, t, :], r_val[:, t, :], te(r_p)[:, t, :], -1.0)
                    dve.drain()
                    dve.tensor_scalar(r_m[:, 0:F], r_w[:, 0:F], 0.0, None, ALU.is_lt).then_inc(hot_ready, 1)
                    dve.reduce_sum(r_t1[:], r_val[:], AX)
                    dve.drain()
                    dve.tensor_scalar(tmp_t[:], r_t1[:], 0.0, None, ALU.is_equal)
                    dve.drain()
                    dve.tensor_tensor(r_t1[:], r_t1[:], tmp_t[:], ALU.add)
                    dve.drain()
                    dve.reciprocal(r_t1[:], r_t1[:])
                    dve.drain()
                    dve.tensor_tensor(weights, r_val[:], over(r_t1[:], [P, NT, CHOICES]), ALU.mult)
                dve.wait_ge(rank_ready, nth)
                nb = F // 512
                dve.tensor_copy(et(r_c).rearrange("p e t -> p t e"),
                                ps[:, 4:4 + nb, :].rearrange("p b (t e) -> p (b t) e", e=E))
                dve.drain()
                dve.tensor_tensor_scan(r_i[:, 0:F], r_keep[:, 0:F], r_c[:, 0:F], 0.0, ALU.mult, ALU.add)
                dve.drain()
                dve.tensor_tensor(et(r_w), over(et(r_i)[:, :, NT - 1], ET), r_ij[:].unsqueeze(1).to_broadcast(ET),
                                  ALU.is_gt)
                dve.drain()
                dve.reduce_sum(r_te[:, 0:E], et(r_w), AX)
                dve.memset(r_dg[:, 0:E], 1.0)
                dve.drain()
                dve.tensor_tensor_scan(r_cum[:, 0:E], r_dg[:, 0:E], r_te[:, 0:E], 0.0, ALU.mult, ALU.add)
                dve.drain()
                dve.tensor_tensor(r_dg[:, 0:E], r_cum[:, 0:E], ident[:, 0:E], ALU.mult)
                dve.tensor_tensor(r_st[:, 0:E], r_cum[:, 0:E], r_te[:, 0:E], ALU.subtract)
                dve.drain()
                dve.reduce_sum(r_end[:], r_dg[:, 0:E], AX)
                dve.drain()
                dve.tensor_scalar(r_end[:], r_end[:], float(P), None, ALU.mult)
                dve.tensor_scalar(r_st[:, 0:E], r_st[:, 0:E], float(P), None, ALU.mult)
                dve.tensor_tensor(r_i[:, 0:F], r_i[:, 0:F], r_c[:, 0:F], ALU.subtract)
                dve.drain()
                dve.tensor_scalar(r_cmp[:, 0:L.tiles], tile_row[:, 0:L.tiles], r_end[:, 0:1], None, ALU.is_ge)\
                   .then_inc(cmp_ready, 1)
                dve.tensor_tensor(et(r_i), et(r_i), over(r_st[:, 0:E], ET), ALU.add)
                dve.drain()
                dve.tensor_tensor(te(r_s), ps[:, 0:nb, :].rearrange("p b (t e) -> p (b t) e", e=E),
                                  et(r_i).rearrange("p e t -> p t e"), ALU.add)
                dve.drain()
                for k in range(K):
                    if L is L0:
                        hot(k)
                        dve.tensor_tensor(te(r_c), te(r_s), te(r_w), ALU.mult)
                        dve.drain()
                        dve.reduce_sum(r_sl[:, :, k], te(r_c), AX)
                    else:
                        junk = te(r_c if k % 2 else r_b)
                        for t in range(NT):
                            dve.scalar_tensor_tensor(junk[:, t, :], r_ie[:, 0:E], ids[:, t, k:k + 1],
                                                     te(r_s)[:, t, :], ALU.is_equal, ALU.mult,
                                                     accum_out=r_sl[:, t, k:k + 1])
                        dve.drain()
                dve.drain()
                dve.tensor_copy(r_si[:, :, 0:K], r_sl[:, :, 0:K])
                dve.drain()
                dve.tensor_single_scalar(r_si[:, :, 0:K], r_si[:, :, 0:K], P - 1, ALU.bitwise_and)
                dve.drain()
                dve.tensor_copy(row_in[:, :, 0:K], r_si[:, :, 0:K])
                dve.drain()
                dve.tensor_tensor(row_of[:, :, 0:K], r_sl[:, :, 0:K], row_in[:, :, 0:K], ALU.subtract)
                dve.wait_ge(map_ready, nth)
                dve.tensor_scalar(tile_e[:, 0:L.tiles], ps[0:1, 4, 0:L.tiles], float(E - 1), None, ALU.min)
                dve.tensor_scalar(tile_ef[:, 0:L.tiles], ps[:, 4, 0:L.tiles], float(E - 1), None, ALU.min)

            def experts(L):
                q = lay[L.name]

                def hidden(i, s):
                    if L.bias:
                        e = dve.value_load(tile_e[0:1, bass.ds(i, 1)], min_val=0, max_val=L.E - 1)
                        dve.wait_ge(q["u_done"], i + 3)
                        dve.tensor_tensor(h_gu[:, s % 2, :], ps[:, 2 + s % 2, 0:2 * L.H],
                                          w_bias[:, bass.ds(e * 2 * L.H, 2 * L.H)], ALU.add).then_inc(q["b_done"], 1)
                        dve.drain()
                    src = h_gu[:, s % 2, L.H:2 * L.H] if L.bias else ps[:, 2 + s % 2, L.H:2 * L.H]
                    dve.wait_ge(q["ht_done"], i + 1)
                    dve.wait_ge(q["s_done"], i + 1)
                    dve.tensor_tensor(h_h[:, s % 2, 0:L.H], src, h_sg[:, s % 2, 0:L.H], ALU.mult)\
                       .then_inc(q["h_done"], 1)

                def result(i, s, b):
                    row = h_x[s]
                    if b is not None:
                        dve.wait_ge(q["chain"][s % NA], 16 * ((TD // NA) * (b - 1) + s // NA + 1))
                        dve.sem_inc(spacer, 1)
                    dve.scalar_tensor_tensor(h_w[:, s, :], row[:, D:D + CHOICES], tile_ef[:, bass.ds(i, 1)],
                                             row[:, D + CHOICES:RW], ALU.is_equal, ALU.mult,
                                             accum_out=h_wc[:, s:s + 1])
                    dve.drain()
                    dve.wait_ge(q["d_done"], i + 3)
                    dve.tensor_scalar(h_y[s][:], ps[:, 6 + s % 2, 0:D], h_wc[:, s:s + 1], None, ALU.mult)\
                       .then_inc(q["y_done"], 1)

                def body(b, first):
                    for s in range(TD):
                        j = TD * b + s
                        if not (first and s < 1):
                            hidden(j - 1, (s - 1) % TD)
                        if not (first and s < 3):
                            result(j - 3, (s - 3) % TD, None if first or (second and s < 3) else
                                   b if s >= 3 else b - 1)

                second = False
                body(0, True)
                second = True
                body(1, False)
                second = False
                with dve.Fori(2, L.tiles // TD) as b:
                    body(b, False)
                n = L.tiles
                result(n - 3, (n - 3) % TD, n // TD - 1)
                hidden(n - 1, (n - 1) % TD)
                result(n - 2, (n - 2) % TD, n // TD - 1)
                result(n - 1, (n - 1) % TD, n // TD - 1)

            def sums(L, gate):
                q = lay[L.name]
                with dve.Fori(0, NG // 2) as b:
                    for s in range(2):
                        g = 2 * b + s
                        n = 16 * (NA + (1 if L is L1 else 0))
                        dve.wait_ge(q["a_in"][s], n * b + n)
                        acc = c_a[:, s, 0, :]
                        dve.sem_inc(spacer, 1)
                        for a in range(1, NA):
                            dve.tensor_tensor(acc, acc, c_a[:, s, a, :], ALU.add)
                            dve.drain()
                        if L is L0:
                            dve.tensor_tensor(acc, acc, group_of(g, z), ALU.add)
                            dve.drain()
                        dve.scalar_tensor_tensor(group_of(g, x_res), acc, gate, group_of(g, x_res),
                                                 ALU.mult, ALU.add).then_inc(q["a_used"], 1)
                        if L is L0:
                            dve.drain()
                            group_stats(g)

            route(L0, 1)
            end_stage(dve, "F0")
            dve.wait_ge(in_sem, 16 * n_load["S0"])
            norm_group(2 * NG, 0, 0)
            shared(0, True, False)
            with dve.Fori(1, NG // 2 - 1) as b:
                shared(b, False, False)
            shared(NG // 2 - 1, False, True)
            in_order(L0, NT * L0.K)
            end_stage(dve, "S0")
            dve.memset(h_hT[:], 1.0)
            dve.wait_ge(in_sem, 16 * n_load["H0"])
            dve.drain()
            experts(L0)
            end_stage(dve, "H0")
            sums(L0, tgate[:, 2:3])
            end_stage(dve, "I0")

            moments(3, have_stats=True)
            dve.wait_ge(in_sem, 16 * n_load["W"])
            dve.wait_ge(wk_pad, 1)
            for c in range(KC):
                dve.memset(w_max[:], 1.0)
                dve.drain()
                dve.tensor_scalar(w_dec[:, c, :, 1:SEQ + 1], w_max[:], w_wu[:, c:c + 1], None, ALU.mult)
                dve.drain()

            def flat(ap):
                return ap.rearrange("p b t -> p (b t)")

            def exponents(g, s, c):
                key = w_k[:, s, c, :, 1:SEQ + 1]
                o_prev, o_now = w_o[:, :, 0:SEQ], w_o[:, :, 1:SEQ + 1]
                u = w_wu[:, KC + c:KC + c + 1]
                dve.drain()
                if c == 0:
                    dve.wait_ge(xT_ready, 3 * NG + g + 2)
                dve.tensor_tensor_scan(flat(w_o[:]), flat(w_dec[:, c]), flat(w_k[:, s, c]), 0.0, ALU.add, ALU.max)
                dve.drain()
                dve.scalar_tensor_tensor(w_max[:], key, u, o_prev, ALU.add, ALU.max)
                dve.wait_ge(wk_e, 2 * g + c + 1)
                dve.tensor_tensor(w_t[:, c, 0], o_prev, o_now, ALU.subtract)
                dve.tensor_tensor(w_t[:, c, 1], key, o_now, ALU.subtract)
                dve.drain()
                dve.tensor_tensor(w_t[:, c, 2], o_prev, w_max[:], ALU.subtract)
                dve.scalar_tensor_tensor(w_t[:, c, 3], key, u, w_max[:], ALU.add, ALU.subtract).then_inc(wk_t, 1)

            def over_time(g, s, c, bb):
                val = w_v[:, s, c, :].rearrange("p (b t) -> p b t", t=SEQ)
                dve.drain()
                dve.wait_ge(wk_e, 2 * g + c + 3)
                if c == 0:
                    dve.wait_ge(wk_v[s], 16 * bb + 16)
                dve.tensor_tensor(w_ev[:, :, 1:SEQ + 1], w_e2[:, c, :, 1:SEQ + 1], val, ALU.mult)
                dve.tensor_tensor_scan(flat(w_q[:, c]), flat(w_a2[:, c]), flat(w_e2[:, c]), 0.0, ALU.mult, ALU.add)
                dve.drain()
                dve.tensor_tensor_scan(flat(w_p[:, c]), flat(w_a2[:, c]), flat(w_ev[:]), 0.0, ALU.mult, ALU.add)\
                   .then_inc(wk_s, 1)

            def divided(g, s, c):
                dve.wait_ge(wk_nd, 2 * g + c + 3)
                dve.reciprocal(w_d[:, c], w_d[:, c])
                dve.drain()
                if c == 0:
                    dve.wait_ge(wk_yt, g + 1)
                m = dve.tensor_tensor(w_y[:, s, c], w_n[:, c], w_d[:, c], ALU.mult)
                if c == KC - 1:
                    m.then_inc(wk_y, 1)

            def residual(g, s):
                dve.wait_ge(wk_yt, g + 3)
                dve.sem_inc(spacer, 1)
                dve.scalar_tensor_tensor(group_of(g, x_res), ps[:, 2 + 2 * s:4 + 2 * s, :]
                                         .rearrange("p a n -> p (a n)"), tgate[:, 1:2],
                                         group_of(g, x_res), ALU.mult, ALU.add).then_inc(wk_yu, 1)

            def wkv(b, first, last):
                for s in range(2):
                    g = 2 * b + s
                    if not (last and s == 1):
                        norm_group(3 * NG + g + 1, g + 1, 1 - s)
                    exponents(g, s, 0)
                    prev = not (first and s == 0)
                    if prev:
                        over_time(g - 1, 1 - s, 1, None)
                        divided(g - 1, 1 - s, 0)
                    if not first:
                        residual(g - 2, s)
                    exponents(g, s, 1)
                    over_time(g, s, 0, b)
                    if prev:
                        divided(g - 1, 1 - s, 1)

            norm_group(3 * NG, 0, 0)
            wkv(0, True, False)
            with dve.Fori(1, NG // 2 - 1) as b:
                wkv(b, False, False)
            wkv(NG // 2 - 1, False, True)
            over_time(NG - 1, 1, 1, None)
            for c in range(KC):
                divided(NG - 1, 1, c)
            residual(NG - 2, 0)
            residual(NG - 1, 1)
            end_stage(dve, "W")

            moments(4)
            router(4 * NG)
            end_stage(dve, "E1")
            route(L1, 2)
            end_stage(dve, "F1")
            def token_tile(t, s):
                stage_row(t, s)
                for k in range(L1.K):
                    pair(L1, NT * L0.K + t * L1.K + k, t, k, k % OR)

            for s in range(RS):
                token_tile(s, s)
            with dve.Fori(1, NT // RS) as b:
                for s in range(RS):
                    dve.wait_ge(lay["b"]["row_st"][s], 16 * b)
                    dve.sem_inc(spacer, 1)
                    token_tile(RS * b + s, s)
            in_order(L1, NT * L0.K + NT * L1.K)
            end_stage(dve, "S1")
            experts(L1)
            end_stage(dve, "H1")
            sums(L1, tgate[:, 3:4])
            end_stage(dve, "I1")


def kernel(**inputs):
    import numpy as np
    import concourse.bacc as bacc
    from concourse.bass_utils import run_bass_kernel_spmd

    a = {k: np.asarray(v) for k, v in inputs.items()}

    def cols(v, n=1):
        v = np.pad(v, (0, -len(v) % P))
        return np.ascontiguousarray(v.reshape(-1, P).T)

    f = np.float32
    wqkvT = np.concatenate([a["L0_xattn_W" + n].T for n in "kvq"])
    bqkv = np.concatenate([cols(a["L0_xattn_b" + n]) for n in "kvq"], axis=1)
    exp0 = np.zeros((L0.E, P, L0.W), f)
    w13 = np.concatenate([a["L0_ffn_w1"].transpose(0, 2, 1), a["L0_ffn_w3"].transpose(0, 2, 1)], axis=2)
    exp0[:, :, 0:L0.up0] = w13.reshape(L0.E, KC, P, 2 * L0.H).transpose(0, 2, 1, 3).reshape(L0.E, P, L0.up0)
    h1 = L0.H // L0.NC
    w2 = a["L0_ffn_w2"].transpose(0, 2, 1)
    for j in range(L0.NC):
        exp0[:, 0:h1, L0.up0 + j * D:L0.up0 + (j + 1) * D] = w2[:, j * h1:(j + 1) * h1]
    exp0[:, h1, L0.up0:L0.up0 + D] = a["L0_ffn_b2"]
    exp0b = np.concatenate([a["L0_ffn_b1"], a["L0_ffn_b3"]], axis=1).reshape(-1)
    exp1 = np.zeros((L1.E, P, L1.W), f)
    gu = a["L1_ffn_gate_up_weights"].reshape(L1.E, KC, P, 2 * L1.H).transpose(0, 2, 1, 3)
    exp1[:, :, 0:L1.up0] = gu.reshape(L1.E, P, L1.up0)
    exp1[:, 0:L1.H, L1.up0:L1.up0 + D] = a["L1_ffn_down_weights"]
    feeds = dict(
        x=a["x"].reshape(NTOK, D),
        ctxT=np.ascontiguousarray(a["ctx_2048"].reshape(NTOK, D).T),
        gates=np.concatenate([a["g_xattn"], a["g_ffn"]]),
        wqkvT=wqkvT, bqkv=bqkv, woT=a["L0_xattn_Wo"].T, bo=a["L0_xattn_bo"],
        gate0T=a["L0_ffn_gate_w"].T, gate0b=a["L0_ffn_gate_b"], exp0=exp0, exp0b=exp0b,
        sh1T=a["L0_ffn_ws1"].T, sh3T=a["L0_ffn_ws3"].T,
        sh2T=np.pad(a["L0_ffn_ws2"].T, ((0, 3 * P - HS), (0, 0))),
        shb=np.concatenate([cols(a["L0_ffn_bs1"]), cols(a["L0_ffn_bs3"])], axis=1), bs2=a["L0_ffn_bs2"],
        wkv_w=cols(a["L1_xattn_w"]), wkv_u=cols(a["L1_xattn_u"]),
        gate1T=a["L1_ffn_gate_weight"].T, exp1=exp1,
    )
    nc = bacc.Bacc("TRN2", target_bir_lowering=False, num_devices=1)
    arrays, args = {}, []
    for name, v in feeds.items():
        v = np.ascontiguousarray(v)
        arrays[f"in_{name}"] = v
        args.append(nc.dram_tensor(f"in_{name}", v.shape, mybir.dt.from_np(v.dtype), kind="ExternalInput").ap())
    args.append(nc.dram_tensor("out_x", (NTOK, D), F32, kind="ExternalOutput").ap())
    flamingo(nc, *args)
    r = run_bass_kernel_spmd(nc, [arrays], core_ids=[0])
    return r.results[0]["out_x"].reshape(64, 64, D)
```
